# Optimizing a Trainium2 kernel written in Bass

```python
import numpy as np
import jax
import jax.numpy as jnp

def _softmax(x, axis=-1):
    return jax.nn.softmax(x, axis=axis)

def _gelu(x):
    return jax.nn.gelu(x, approximate=True)

def _silu(x):
    return jax.nn.silu(x)

def _sigmoid(x):
    return jax.nn.sigmoid(x)

def _layernorm(x, axis=-1, eps=1e-05):
    m = jnp.mean(x, axis=axis, keepdims=True)
    v = jnp.var(x, axis=axis, keepdims=True)
    return (x - m) / jnp.sqrt(v + eps)

def _scatter_add(tgt, idx, src, axis=0):
    return tgt.at[idx].add(src)

def _segment_sum(src, seg, n):
    return jax.ops.segment_sum(src, seg, n)
kernel_name = 'mk_hybrid_d2_jaxref_r8_c460b9'

def setup_inputs(seed: int=0):
    np.random.seed(seed)
    _w = jnp.asarray

    def _L0_attn_a_setup():
        import jax, jax.numpy as jnp
        import numpy as np
        HEADS = 16
        key = jax.random.key(seed)
        ks = jax.random.split(key, 5)
        B, T, D = (2, 256, 256)
        s = 0.02
        return {'x': jax.random.normal(ks[0], (B, T, D), dtype=jnp.float32), 'Wq': jax.random.normal(ks[1], (D, D), dtype=jnp.float32) * s, 'Wk': jax.random.normal(ks[2], (D, D), dtype=jnp.float32) * s, 'Wv': jax.random.normal(ks[3], (D, D), dtype=jnp.float32) * s, 'Wo': jax.random.normal(ks[4], (D, D), dtype=jnp.float32) * s}
    _L0_attn_a_in = _L0_attn_a_setup()

    def _L0_attn_b_setup():
        import jax, jax.numpy as jnp
        import numpy as np
        D = 256
        key = jax.random.key(seed)
        ks = jax.random.split(key, 5)
        scale = 1.0 / np.sqrt(D)
        x = jax.random.normal(ks[0], (4, 512, D), dtype=jnp.float32)
        Wq = jax.random.normal(ks[1], (D, D), dtype=jnp.float32) * scale
        Wk = jax.random.normal(ks[2], (D, D), dtype=jnp.float32) * scale
        Wv = jax.random.normal(ks[3], (D, D), dtype=jnp.float32) * scale
        Wo = jax.random.normal(ks[4], (D, D), dtype=jnp.float32) * scale
        return {'x': x, 'Wq': Wq, 'Wk': Wk, 'Wv': Wv, 'Wo': Wo}
    _L0_attn_b_in = _L0_attn_b_setup()

    def _L0_ffn_setup():
        import jax, jax.numpy as jnp
        import numpy as np
        DIM_IN = 256
        DIM_HIDDEN = 1024
        key = jax.random.key(seed)
        k_x, k_g, k_u, k_d = jax.random.split(key, 4)
        s_in = 1.0 / np.sqrt(DIM_IN)
        s_hid = 1.0 / np.sqrt(DIM_HIDDEN)
        x = jax.random.normal(k_x, (4, 256, DIM_IN), dtype=jnp.float32)
        w_gate = jax.random.uniform(k_g, (DIM_HIDDEN, DIM_IN), jnp.float32, -s_in, s_in)
        w_up = jax.random.uniform(k_u, (DIM_HIDDEN, DIM_IN), jnp.float32, -s_in, s_in)
        w_down = jax.random.uniform(k_d, (DIM_IN, DIM_HIDDEN), jnp.float32, -s_hid, s_hid)
        return {'x': x, 'w_gate': w_gate, 'w_up': w_up, 'w_down': w_down}
    _L0_ffn_in = _L0_ffn_setup()

    def _L1_attn_a_setup():
        import jax, jax.numpy as jnp
        import numpy as np
        import math
        N_HEAD = 16
        LAYER = 1
        LAMBDA_INIT = 0.8 - 0.6 * math.exp(-0.3 * (LAYER - 1))
        key = jax.random.key(seed)
        ks = jax.random.split(key, 7)
        B, T, E = (2, 256, 256)
        s = 0.02
        return {'x': jax.random.normal(ks[0], (B, T, E), dtype=jnp.float32), 'W_attn': jax.random.normal(ks[1], (E, 3 * E), dtype=jnp.float32) * s, 'W_proj': jax.random.normal(ks[2], (E, E), dtype=jnp.float32) * s, 'lambda_q1': jax.random.normal(ks[3], (E,), dtype=jnp.float32) * 0.1, 'lambda_k1': jax.random.normal(ks[4], (E,), dtype=jnp.float32) * 0.1, 'lambda_q2': jax.random.normal(ks[5], (E,), dtype=jnp.float32) * 0.1, 'lambda_k2': jax.random.normal(ks[6], (E,), dtype=jnp.float32) * 0.1}
    _L1_attn_a_in = _L1_attn_a_setup()

    def _L1_attn_b_setup():
        import jax, jax.numpy as jnp
        import numpy as np
        D, DC, DR, NH = (256, 64, 64, 16)
        HD = D // NH
        B, T = (2, 256)

        def _rope_tables(sl, off, dr):
            inv = 1.0 / 10000.0 ** (jnp.arange(0, dr, 2, dtype=jnp.float32) / dr)
            t = jnp.arange(off, off + sl, dtype=jnp.float32)
            f = jnp.outer(t, inv)
            e = jnp.concatenate([f, f], -1)
            return (jnp.cos(e), jnp.sin(e))

        def _rap(x, c, s):
            d = x.shape[-1]
            x1, x2 = (x[..., :d // 2], x[..., d // 2:])
            ch, sh = (c[..., :d // 2], s[..., :d // 2])
            return jnp.concatenate([x1 * ch - x2 * sh, x2 * ch + x1 * sh], -1)

        def _reference_tuple_inner(x, Wkv, Wkup, Wvup, Wq, Wqr, Wkr, Wo):
            Bx, Tx, d = x.shape
            offset = 0
            ckv = x @ Wkv
            kr = ckv @ Wkr
            cos, sin = _rope_tables(Tx, offset, DR)
            kr = _rap(kr, cos[None], sin[None])
            entry = jnp.concatenate([ckv, kr], -1)
            tl = entry.shape[1]
            k = (ckv @ Wkup).reshape(Bx, tl, NH, HD).transpose(0, 2, 1, 3)
            v = (ckv @ Wvup).reshape(Bx, tl, NH, HD).transpose(0, 2, 1, 3)
            q = (x @ Wq).reshape(Bx, Tx, NH, HD).transpose(0, 2, 1, 3)
            qr = _rap(x @ Wqr, cos[None], sin[None])
            ac = jnp.einsum('bhtd,bhsd->bhts', q, k)
            ar = jnp.einsum('btd,bsd->bts', qr, kr)
            scale = np.sqrt(HD + DR).astype(np.float32)
            scores = (ac + ar[:, None]) / scale
            i = jnp.arange(Tx)[:, None]
            j = jnp.arange(tl)[None, :]
            mask = j > i + (tl - Tx)
            scores = jnp.where(mask[None, None], -jnp.inf, scores)
            attn = jax.nn.softmax(scores, -1)
            out = jnp.einsum('bhts,bhsd->bhtd', attn, v).transpose(0, 2, 1, 3).reshape(Bx, Tx, -1)
            return (out @ Wo, entry)
        key = jax.random.key(seed)
        ks = jax.random.split(key, 8)

        def w(k, i, o):
            return jax.random.normal(k, (i, o), jnp.float32) * (1.0 / np.sqrt(i))
        return {'x': jax.random.normal(ks[0], (B, T, D), jnp.float32), 'Wkv': w(ks[1], D, DC), 'Wkup': w(ks[2], DC, D), 'Wvup': w(ks[3], DC, D), 'Wq': w(ks[4], D, D), 'Wqr': w(ks[5], D, DR), 'Wkr': w(ks[6], DC, DR), 'Wo': w(ks[7], D, D)}
    _L1_attn_b_in = _L1_attn_b_setup()

    def _L1_ffn_setup():
        import jax, jax.numpy as jnp
        import numpy as np
        EPS = 1e-07
        CURVATURE = 1.0
        MAX_NORM_RATIO = 0.99
        B, L, N, K = (4, 256, 256, 256)

        def _ternary_init(key, n, k):
            rand = jax.random.normal(key, (n, k), dtype=jnp.float32)
            threshold = 0.5 * jnp.mean(jnp.abs(rand))
            return jnp.where(rand > threshold, 1.0, jnp.where(rand < -threshold, -1.0, 0.0)).astype(jnp.float32)
        key = jax.random.key(seed)
        kx, kw = jax.random.split(key)
        x = jax.random.normal(kx, (B, L, N), dtype=jnp.float32)
        weight = _ternary_init(kw, N, K)
        scale = jnp.full((K,), 1.0 / np.sqrt(N), dtype=jnp.float32)
        return {'x': x, 'weight': weight, 'scale': scale}
    _L1_ffn_in = _L1_ffn_setup()
    _d = {'L0_attn_a_x': _L0_attn_a_in['x'], 'L0_attn_a_Wq': _L0_attn_a_in['Wq'], 'L0_attn_a_Wk': _L0_attn_a_in['Wk'], 'L0_attn_a_Wv': _L0_attn_a_in['Wv'], 'L0_attn_a_Wo': _L0_attn_a_in['Wo'], 'L0_attn_b_Wq': _L0_attn_b_in['Wq'], 'L0_attn_b_Wk': _L0_attn_b_in['Wk'], 'L0_attn_b_Wv': _L0_attn_b_in['Wv'], 'L0_attn_b_Wo': _L0_attn_b_in['Wo'], 'L0_ffn_w_gate': _L0_ffn_in['w_gate'], 'L0_ffn_w_up': _L0_ffn_in['w_up'], 'L0_ffn_w_down': _L0_ffn_in['w_down'], 'L1_attn_a_W_attn': _L1_attn_a_in['W_attn'], 'L1_attn_a_W_proj': _L1_attn_a_in['W_proj'], 'L1_attn_a_lambda_q1': _L1_attn_a_in['lambda_q1'], 'L1_attn_a_lambda_k1': _L1_attn_a_in['lambda_k1'], 'L1_attn_a_lambda_q2': _L1_attn_a_in['lambda_q2'], 'L1_attn_a_lambda_k2': _L1_attn_a_in['lambda_k2'], 'L1_attn_b_Wkv': _L1_attn_b_in['Wkv'], 'L1_attn_b_Wkup': _L1_attn_b_in['Wkup'], 'L1_attn_b_Wvup': _L1_attn_b_in['Wvup'], 'L1_attn_b_Wq': _L1_attn_b_in['Wq'], 'L1_attn_b_Wqr': _L1_attn_b_in['Wqr'], 'L1_attn_b_Wkr': _L1_attn_b_in['Wkr'], 'L1_attn_b_Wo': _L1_attn_b_in['Wo'], 'L1_ffn_weight': _L1_ffn_in['weight'], 'L1_ffn_scale': _L1_ffn_in['scale']}
    _x0 = _d['L0_attn_a_x']
    _d['L0_attn_a_x'] = jax.random.normal(jax.random.fold_in(jax.random.key(seed), 1), (1, 2048, 256), dtype=_x0.dtype)
    del _x0
    return _d

def reference(L0_attn_a_x, L0_attn_a_Wq, L0_attn_a_Wk, L0_attn_a_Wv, L0_attn_a_Wo, L0_attn_b_Wq, L0_attn_b_Wk, L0_attn_b_Wv, L0_attn_b_Wo, L0_ffn_w_gate, L0_ffn_w_up, L0_ffn_w_down, L1_attn_a_W_attn, L1_attn_a_W_proj, L1_attn_a_lambda_q1, L1_attn_a_lambda_k1, L1_attn_a_lambda_q2, L1_attn_a_lambda_k2, L1_attn_b_Wkv, L1_attn_b_Wkup, L1_attn_b_Wvup, L1_attn_b_Wq, L1_attn_b_Wqr, L1_attn_b_Wkr, L1_attn_b_Wo, L1_ffn_weight, L1_ffn_scale):

    def _L0_attn_a_ref(x, Wq, Wk, Wv, Wo):
        import jax, jax.numpy as jnp
        import numpy as np
        HEADS = 16
        B, T, _ = x.shape
        H = HEADS
        Dh = Wq.shape[1] // H
        q = (x @ Wq).reshape(B, T, H, Dh)
        k = (x @ Wk).reshape(B, T, H, Dh)
        v = (x @ Wv).reshape(B, T, H, Dh)
        scores = jnp.einsum('bthd,bshd->bhts', q, k)
        mask = jnp.tril(jnp.ones((T, T), dtype=scores.dtype))
        scores = scores * mask
        attn = jax.nn.softmax(scores / T ** 0.5, axis=-1)
        out = jnp.einsum('bhts,bshd->bthd', attn, v).reshape(B, T, H * Dh)
        return out @ Wo

    def _L0_attn_b_ref(x, Wq, Wk, Wv, Wo):
        import jax, jax.numpy as jnp
        import numpy as np
        D = 256
        q = jnp.einsum('bsd,ed->bse', x, Wq)
        k = jnp.einsum('bsd,ed->bse', x, Wk)
        v = jnp.einsum('bsd,ed->bse', x, Wv)
        seq = x.shape[-2]
        denom = jnp.sqrt(jnp.float32(x.shape[-1])) / seq
        kvt = jnp.cumsum(k * v, axis=-2) * denom
        vhat = q * kvt
        return jnp.einsum('bse,fe->bsf', vhat, Wo)

    def _L0_ffn_ref(x, w_gate, w_up, w_down):
        import jax, jax.numpy as jnp
        import numpy as np
        DIM_IN = 256
        DIM_HIDDEN = 1024
        gate = jnp.einsum('bsd,hd->bsh', x, w_gate)
        up = jnp.einsum('bsd,hd->bsh', x, w_up)
        gated = jax.nn.silu(gate) * up
        return jnp.einsum('bsh,dh->bsd', gated, w_down)

    def _L1_attn_a_ref(x, W_attn, W_proj, lambda_q1, lambda_k1, lambda_q2, lambda_k2):
        import jax, jax.numpy as jnp
        import numpy as np
        import math
        N_HEAD = 16
        LAYER = 1
        LAMBDA_INIT = 0.8 - 0.6 * math.exp(-0.3 * (LAYER - 1))
        B, T, E = x.shape
        C = E // 2
        H = N_HEAD
        hd = E // H // 2
        scale = hd ** (-0.5)
        qkv = x @ W_attn
        q1 = qkv[..., 0 * C:1 * C].reshape(B, T, H, hd)
        k1 = qkv[..., 1 * C:2 * C].reshape(B, T, H, hd)
        q2 = qkv[..., 2 * C:3 * C].reshape(B, T, H, hd)
        k2 = qkv[..., 3 * C:4 * C].reshape(B, T, H, hd)
        v = qkv[..., 4 * C:6 * C].reshape(B, T, H, 2 * hd)
        lam = jnp.exp(jnp.dot(lambda_q1, lambda_k1)) - jnp.exp(jnp.dot(lambda_q2, lambda_k2)) + LAMBDA_INIT
        attn1 = jnp.einsum('bthd,bshd->bhts', q1, k1) * scale
        attn2 = jnp.einsum('bthd,bshd->bhts', q2, k2) * scale
        score = jax.nn.softmax(attn1 - lam * attn2, axis=-1)
        out = jnp.einsum('bhts,bshd->bthd', score, v)
        out = (1.0 - LAMBDA_INIT) * out.reshape(B, T, E)
        return out @ W_proj

    def _L1_attn_b_ref(x, Wkv, Wkup, Wvup, Wq, Wqr, Wkr, Wo):
        import jax, jax.numpy as jnp
        import numpy as np
        D, DC, DR, NH = (256, 64, 64, 16)
        HD = D // NH
        B, T = (2, 256)

        def _rope_tables(sl, off, dr):
            inv = 1.0 / 10000.0 ** (jnp.arange(0, dr, 2, dtype=jnp.float32) / dr)
            t = jnp.arange(off, off + sl, dtype=jnp.float32)
            f = jnp.outer(t, inv)
            e = jnp.concatenate([f, f], -1)
            return (jnp.cos(e), jnp.sin(e))

        def _rap(x, c, s):
            d = x.shape[-1]
            x1, x2 = (x[..., :d // 2], x[..., d // 2:])
            ch, sh = (c[..., :d // 2], s[..., :d // 2])
            return jnp.concatenate([x1 * ch - x2 * sh, x2 * ch + x1 * sh], -1)

        def _reference_tuple_inner(x, Wkv, Wkup, Wvup, Wq, Wqr, Wkr, Wo):
            Bx, Tx, d = x.shape
            offset = 0
            ckv = x @ Wkv
            kr = ckv @ Wkr
            cos, sin = _rope_tables(Tx, offset, DR)
            kr = _rap(kr, cos[None], sin[None])
            entry = jnp.concatenate([ckv, kr], -1)
            tl = entry.shape[1]
            k = (ckv @ Wkup).reshape(Bx, tl, NH, HD).transpose(0, 2, 1, 3)
            v = (ckv @ Wvup).reshape(Bx, tl, NH, HD).transpose(0, 2, 1, 3)
            q = (x @ Wq).reshape(Bx, Tx, NH, HD).transpose(0, 2, 1, 3)
            qr = _rap(x @ Wqr, cos[None], sin[None])
            ac = jnp.einsum('bhtd,bhsd->bhts', q, k)
            ar = jnp.einsum('btd,bsd->bts', qr, kr)
            scale = np.sqrt(HD + DR).astype(np.float32)
            scores = (ac + ar[:, None]) / scale
            i = jnp.arange(Tx)[:, None]
            j = jnp.arange(tl)[None, :]
            mask = j > i + (tl - Tx)
            scores = jnp.where(mask[None, None], -jnp.inf, scores)
            attn = jax.nn.softmax(scores, -1)
            out = jnp.einsum('bhts,bhsd->bhtd', attn, v).transpose(0, 2, 1, 3).reshape(Bx, Tx, -1)
            return (out @ Wo, entry)
        return _reference_tuple_inner(x, Wkv, Wkup, Wvup, Wq, Wqr, Wkr, Wo)[0]

    def _L1_ffn_ref(x, weight, scale):
        import jax, jax.numpy as jnp
        import numpy as np
        EPS = 1e-07
        CURVATURE = 1.0
        MAX_NORM_RATIO = 0.99
        B, L, N, K = (4, 256, 256, 256)

        def _ternary_init(key, n, k):
            rand = jax.random.normal(key, (n, k), dtype=jnp.float32)
            threshold = 0.5 * jnp.mean(jnp.abs(rand))
            return jnp.where(rand > threshold, 1.0, jnp.where(rand < -threshold, -1.0, 0.0)).astype(jnp.float32)
        sqrt_c = jnp.sqrt(jnp.float32(CURVATURE))
        out = jnp.einsum('bln,nk->blk', x, weight) * scale
        v_norm = jnp.maximum(jnp.linalg.norm(out, axis=-1, keepdims=True), EPS)
        scaled_norm = sqrt_c * v_norm
        out = out * (jnp.tanh(scaled_norm) / (scaled_norm + EPS))
        max_norm = MAX_NORM_RATIO / sqrt_c
        o_norm = jnp.maximum(jnp.linalg.norm(out, axis=-1, keepdims=True), EPS)
        out = out * jnp.minimum(max_norm / o_norm, 1.0)
        return out.astype(x.dtype)
    x = L0_attn_a_x
    x = x + _L0_attn_a_ref(_layernorm(x, axis=-1), L0_attn_a_Wq, L0_attn_a_Wk, L0_attn_a_Wv, L0_attn_a_Wo)
    x = x + _L0_ffn_ref(_layernorm(x, axis=-1), L0_ffn_w_gate, L0_ffn_w_up, L0_ffn_w_down)
    x = x + _L0_attn_b_ref(_layernorm(x, axis=-1), L0_attn_b_Wq, L0_attn_b_Wk, L0_attn_b_Wv, L0_attn_b_Wo)
    x = x + _L0_ffn_ref(_layernorm(x, axis=-1), L0_ffn_w_gate, L0_ffn_w_up, L0_ffn_w_down)
    x = x + _L1_attn_a_ref(_layernorm(x, axis=-1), L1_attn_a_W_attn, L1_attn_a_W_proj, L1_attn_a_lambda_q1, L1_attn_a_lambda_k1, L1_attn_a_lambda_q2, L1_attn_a_lambda_k2)
    x = x + _L1_ffn_ref(_layernorm(x, axis=-1), L1_ffn_weight, L1_ffn_scale)
    x = x + _L1_attn_b_ref(_layernorm(x, axis=-1), L1_attn_b_Wkv, L1_attn_b_Wkup, L1_attn_b_Wvup, L1_attn_b_Wq, L1_attn_b_Wqr, L1_attn_b_Wkr, L1_attn_b_Wo)
    x = x + _L1_ffn_ref(_layernorm(x, axis=-1), L1_ffn_weight, L1_ffn_scale)
    return x

_drawn_inputs = setup_inputs


def setup_inputs(seed=0):
    import zlib

    import numpy as np

    out = dict(_drawn_inputs(seed))
    spreads = {'L1_ffn_scale': (0.0625, 0.6)}
    factors = {'L0_attn_a_Wq': 8.0,
     'L0_attn_a_Wk': 8.0,
     'L0_attn_a_Wv': 8.0,
     'L0_attn_a_Wo': 8.0,
     'L1_attn_a_W_attn': 8.0,
     'L1_attn_a_W_proj': 8.0,
     'L1_attn_a_lambda_q1': 8.0,
     'L1_attn_a_lambda_k1': 8.0,
     'L1_attn_a_lambda_q2': 64.0,
     'L1_attn_a_lambda_k2': 64.0,
     'L1_attn_b_Wkup': 3.946,
     'L1_attn_b_Wq': 3.933,
     'L1_attn_b_Wqr': 2.906,
     'L1_attn_b_Wkr': 2.783}
    for name, (base, spread) in spreads.items():
        noise = np.random.default_rng([zlib.crc32(name.encode()), seed]).standard_normal(out[name].shape)
        drawn = base * np.exp(spread * noise) if base else spread * noise
        out[name] = jnp.asarray(drawn.astype(out[name].dtype))
    for name, factor in factors.items():
        out[name] = (out[name] * factor).astype(out[name].dtype)
    return out
```

```python
from contextlib import ExitStack

import numpy as np

import concourse.bass as bass
from concourse import mybir

F32 = mybir.dt.float32
BF16 = mybir.dt.bfloat16
I32 = mybir.dt.int32
ALU = mybir.AluOpType
ACT = mybir.ActivationFunctionType
AX = mybir.AxisListType

P = 128
T, D, HID = 2048, 256, 1024
H, DH = 16, 16
NB = T // P
CH = 512
NC = T // CH
BPC = CH // P
KD = D // P
HG = 4
NG = H // HG
W1 = 1024
PARTS = 3
SROWS = 6 * DH
MROW = SROWS
KROWS = SROWS + PARTS
ROPE = 64
LATENT = 64
LN_EPS = 1e-5
EPS = 1e-7
LOWEST = -3.0e38
LAMBDA_INIT = 0.2
DIFF_SCALE = (D // H // 2) ** -0.5
MAX_NORM = 0.99
LAG = 2
SETS = 3
RING2 = 3


class Count:

    def __init__(self, base=0):
        self.base, self.k = base, 0

    def next(self):
        self.k += 1
        return self.base + self.k


class Layer:

    def __init__(self, name, causal, zeros, rope, sem):
        self.name, self.causal, self.zeros, self.rope = name, causal, zeros, rope
        self.units = []
        self.chunk_last = []
        for c in range(NC):
            for sb in range(BPC * (c + 1) if causal else NB):
                self.units.append(("s", c, sb, max(0, sb - BPC * c) * P if causal else 0))
            if zeros:
                self.units += [("e", c, None, 0), ("m", c, None, 0)]
            self.chunk_last.append(len(self.units) - 1)
        self.jobs = []
        for j in range(HG):
            for tb in range(NB):
                end = (tb + 1) * P if causal else T
                for i, s0 in enumerate(range(0, end, W1)):
                    w = min(W1, end - s0)
                    self.jobs.append((j, tb, i, s0, w, causal and s0 + w == end))
        self.exps = [u for u, x in enumerate(self.units) if x[0] != "m"]
        self.exp_no = {u: HG * n for n, u in enumerate(self.exps)}
        self.n_exp = HG * len(self.exps)
        self.masked = [u for u, x in enumerate(self.units) if x[0] == "m" or (x[0] == "s" and self.diagonal(u))]
        self.mask_no = {u: HG * n for n, u in enumerate(self.masked)}
        self.n_mask = HG * len(self.masked)
        self.n_unit = len(self.units)
        self.first = self.plan_first()
        self.stage = self.plan(True)
        self.last = self.plan(False)
        ring = ("max", "mtr", "otr")
        self.r_first = sum(s[0] in ring for s in self.first)
        self.r_stage = sum(s[0] in ring for s in self.stage)
        assert self.r_first % 2 == 0 and self.r_stage % 2 == 0
        self.chain_first = CHAIN_NEG
        self.chain_stage = CHAIN_NEG + NC * CHAIN_OUT
        s = lambda x: sem(f"{name}_{x}")
        self.stack_in = [s(f"stack_in{j}") for j in range(HG)]
        self.max_rows_in = s("max_rows_in")
        self.rope_in = s("rope_in")
        self.slot_ready = s("slot_ready")
        self.slot_free = s("slot_free")
        self.neg_ready = s("neg_ready")
        self.score_ready = s("score_ready")
        self.exp_done = s("exp_done")
        self.mask_done = s("mask_done")
        self.pv_done = s("pv_done")
        self.out_saved = s("out_saved")
        self.v_ready = s("v_ready")
        self.suffix_ready = s("suffix_ready")
        self.chain = s("chain")

    def diagonal(self, u):
        kind, c, sb, off = self.units[u]
        return self.causal and kind == "s" and sb >= BPC * c

    def plan_first(self):
        return [("max", n) for n in range(len(self.jobs))] + [("neg",), ("mtr", 0), ("mtr", 1)]

    def plan(self, with_next):
        n = self.n_unit
        ahead = [("max", i) for i in range(len(self.jobs))] if with_next else []
        total, steps, given = len(ahead), [], 0
        late = []
        cost = [0.25 * (CH - x[3]) / P if x[0] == "s" else 0.8 for x in self.units]
        whole, run = sum(cost), 0.0
        negged = not with_next
        for u in range(n + LAG):
            if u < n:
                if self.units[u][0] != "m":
                    steps.append(("score", u))
                run += cost[u]
            want = min(total, int(total * (run / whole - 0.04) / 0.86)) if u >= 2 else 0
            while given < want:
                steps.append(ahead[given])
                given += 1
            if given == total and not negged:
                steps.append(("neg",))
                late.append((u + 2, ("mtr", 0)))
                late.append((u + 2, ("mtr", 1)))
                negged = True
            if u >= LAG:
                steps.append(("pv", u - LAG))
                if u - LAG in self.chunk_last:
                    c = self.chunk_last.index(u - LAG)
                    steps.append(("save", c))
                    late.append((u + 1, ("otr", c)))
            for at, step in [x for x in late if x[0] <= u]:
                steps.append(step)
            late = [x for x in late if x[0] > u]
        return steps + [x[1] for x in late]


CHAIN_NEG = 4
CHAIN_OUT = 1


def build(nc, a, out):
    nc.disable_value_cache = True
    ctx = ExitStack()
    with ctx:
        def sb(name, shape, dt=F32):
            return ctx.enter_context(nc.sbuf_tensor(name, shape, dt))

        def sem(name):
            return ctx.enter_context(nc.semaphore(name))

        X = sb("X", [P, NB, D])
        HT = sb("HT", [P, NC, KD, CH])
        ON = HT[:].rearrange("p c k t -> p (c k t)").rearrange("p (b d) -> p b d", d=D)
        VALL = sb("VALL", [P, NB, D])
        VG = sb("VG", [P, NB, HG, 2 * DH])
        QF = sb("QF", [P, 2 * HG * T // 2])
        KF = sb("KF", [P, 2 * HG * T // 2])
        QS = QF[:].bitcast(BF16)
        KS = KF[:].bitcast(BF16)
        PF = sb("PF", [P, SETS * HG * CH])
        PT = PF[:].rearrange("p (u j t) -> p u j t", u=SETS, j=HG)
        WA = sb("WA", [P, 6144])
        WB = sb("WB", [P, 4096])
        WC = sb("WC", [P, 3072])
        MASKS = sb("MASKS", [P, 2, W1], BF16)
        JUNK = sb("JUNK", [P, W1], BF16)
        OS = sb("OS", [P, CH])
        IDF = sb("IDF", [P, P])
        IDB = sb("IDB", [P, P], BF16)
        ONE = sb("ONE", [P, 1])
        ONESEL = sb("ONESEL", [P, P], BF16)
        MP = sb("MP", [P, 2, HG * NB])
        MX = sb("MX", [P, 2, HG * NB])
        NM = sb("NM", [P, 4, HG * NB], BF16)
        MR = sb("MR", [P, 2, P], BF16)
        RZ = sb("RZ", [P, BPC, HG])
        ST = sb("ST", [P, BPC, 6])
        MV = sb("MV", [P, BPC, 2])
        NW = sb("NW", [P, 8, BPC])
        LAM = sb("LAM", [P, 8])
        QSC = sb("QSC", [P, 1])
        SEL = sb("SEL", [P, 2])
        PS = ctx.enter_context(nc.psum_tensor("PS", [P, 8 * CH], F32))
        bank = lambda b, n=CH, o=0: PS[:, b * CH + o:b * CH + o + n]

        GT = QF[:, 0:4096].rearrange("p (m t) -> p m t", t=CH)
        LNH = QF[:, 4096:6144].rearrange("p (x b d) -> p x b d", x=2, d=D)
        OT = QF[:, 6144:8192].rearrange("p (x k t) -> p x k t", x=2, k=KD)
        TH = PF[:, 0:1024].rearrange("p (x t) -> p x t", x=2)
        TA = PF[:, 1024:2048].rearrange("p (x t) -> p x t", x=2)
        Y2 = PF[:, 2048:3072].rearrange("p (b d) -> p b d", d=D)
        CUM = PF[:, 2048:4096].rearrange("p (x k t) -> p x k t", x=2, k=KD)
        CKV = PF[0:LATENT, 3072:4096].rearrange("p (x t) -> p x t", x=2)
        VH = PF[:, 4096:5120].rearrange("p (k t) -> p k t", k=KD)
        VS = PF[:, 5120:6144].rearrange("p (x t) -> p x t", x=2)
        STG = PF[:, 4096:5632].bitcast(BF16).rearrange("p (x i t) -> p x i t", x=2, i=PARTS)
        RA = QF[0:ROPE, 0:1024].rearrange("p (x t) -> p x t", x=2)
        COS = KF[0:ROPE, 0:T]
        SIN = KF[0:ROPE, T:2 * T]

        WGT = WA[:, 0:2048].rearrange("p (k m) -> p k m", k=KD)
        WUT = WA[:, 2048:4096].rearrange("p (k m) -> p k m", k=KD)
        WDT = WA[:, 4096:6144].rearrange("p (m d) -> p m d", d=D)
        sq = lambda w, o: w[:, o:o + KD * D].rearrange("p (k n) -> p k n", k=KD)
        W0 = {x: sq(WB, 512 * i) for i, x in enumerate(("q", "k", "v", "o"))}
        WL = {x: sq(WB, 2048 + 512 * i) for i, x in enumerate(("q", "k", "v", "o"))}
        WAT = WB[:, 0:1536].rearrange("p (k n) -> p k n", k=KD)
        W1A = {"q": sq(WB, 1536), "k": sq(WB, 2048), "v": WAT[:, :, 2 * D:3 * D], "o": sq(WB, 2560)}
        FG = WC[:, 0:2048].rearrange("p (b j d) -> p b j d", b=NB, j=HG)
        W2 = {"q": sq(WC, 0), "o": sq(WC, 512)}
        WN = sq(WC, 1024)
        SCALE = WC[:, 1536:1792]
        WKV = WC[:, 1792:1920].rearrange("p (k n) -> p k n", k=KD)
        WQR = [WC[:, 1920 + 128 * i:2048 + 128 * i].rearrange("p (k n) -> p k n", k=KD) for i in range(2)]
        WKR = [WC[0:LATENT, 2176 + 64 * i:2240 + 64 * i] for i in range(2)]
        WKUP = WC[0:LATENT, 2304:2560]
        WVUP = WC[0:LATENT, 2560:2816]
        RS = WA[:, 0:5120].bitcast(BF16).rearrange("p (i t) -> p i t", t=T)
        ROPE_Q, ROPE_K = (0, 1, 2), (3, 3, 4)

        NAT = {"gate": QF[:, 0:2048].rearrange("p (m d) -> p m d", d=D),
               "up": QF[:, 2048:4096].rearrange("p (m d) -> p m d", d=D),
               "down": QF[:, 6144:8192].rearrange("p (r m) -> p r m", r=KD)}
        NATL = {x: PF[:, 512 * i:512 * (i + 1)].rearrange("p (e d) -> p e d", e=KD) for i, x in enumerate(("q", "k", "v", "o"))}

        LV = PF[:, 3072:4096].rearrange("p (i d) -> p i d", d=D)

        L0 = Layer("a", True, True, False, sem)
        L1 = Layer("b", False, False, False, sem)
        L2 = Layer("c", True, False, True, sem)
        scr = {(L.name, w): nc.dram_tensor(f"parts_{L.name}_{w}", (PARTS, D, T), BF16, kind="Internal").ap()
               for L in (L0, L1, L2) for w in "qk"}
        scr_r = {w: nc.dram_tensor(f"rope_parts_{w}", (PARTS, ROPE, T), BF16, kind="Internal").ap() for w in "qk"}

        x_in = sem("x_in")
        x_ins = [x_in] + [sem(f"x_in{c}") for c in range(1, NC)]
        w_nat_in = sem("w_nat_in")
        w0_in = sem("w0_in")
        w1_in = sem("w1_in")
        w2_in = sem("w2_in")
        lam_in = sem("lam_in")
        rope_tab_in = sem("rope_tab_in")
        const_ready = sem("const_ready")
        gp = sem("gp")
        d_ready, d_free = sem("d_ready"), sem("d_free")
        a_ready, a_free = sem("a_ready"), sem("a_free")
        tanh_ready = sem("tanh_ready")
        v_used = sem("v_used")
        norm_ready = sem("norm_ready")
        split_ready = sem("split_ready")
        parts_ready = sem("parts_ready")
        parts_out = [sem("parts_out0"), sem("parts_out1")]
        n2_ready, n2_tanh = sem("n2_ready"), sem("n2_tanh")
        lam_dots, lam_exp, lam_done = sem("lam_dots"), sem("lam_exp"), sem("lam_done")
        perm_done = sem("perm_done")
        l1w_free = sem("l1w_free")
        out_dma = sem("out_dma")
        vc = sem("vc")
        x_done = sem("x_done")

        att = {"A": L0, "B": L1, "C": L2}
        def each(*kinds):
            return [(k, c) for k in kinds for c in range(NC)]
        PROGRAM = [("in", each("in", "p0")), ("A", None), ("", each("o0", "ffn", "lin", "ffn", "p1")), ("B", None),
                   ("", each("o1", "hyp", "p2")), ("C", None), ("", each("o2", "hypout"))]
        HAS_NORM = {"in", "o0", "ffn", "lin", "o1", "hyp", "o2"}
        OUTW = {"o0": W0["o"], "o1": W1A["o"], "o2": W2["o"], "lin": WL["o"]}
        PROJ = {"p0": (L0, W0, T ** -0.5), "p1": (L1, W1A, None), "p2": (L2, W2, (DH + ROPE) ** -0.5)}
        N_TRANSPOSED = 16

        BANKS = {"in": (0, 0), "p0": (4, 2), "p1": (4, 2), "p2": (8, 3), "o0": (2, 2), "o1": (2, 2), "o2": (2, 2),
                 "ffn": (18, 0), "lin": (6, 2), "hyp": (2, 0), "hypout": (2, 0)}
        D_COUNT, A_COUNT, HT_AT = {}, {}, []
        d_total, a_total = 0, N_TRANSPOSED
        for kind, steps in PROGRAM:
            if steps is None:
                D_COUNT[kind], A_COUNT[kind] = d_total, a_total
                continue
            pending = False
            for i, (k, c) in enumerate(steps):
                steps[i] = (k, c, d_total, a_total)
                d_total += BANKS[k][0]
                a_total += BANKS[k][1]
                if pending:
                    a_total += KD
                    HT_AT.append(a_total)
                pending = k in HAS_NORM
        L_KEY = {"a": "A", "b": "B", "c": "C"}

        block = ctx.enter_context(nc.Block())

        STACK_DMAS = 16 * 9
        PARTS_ORDER = [("q", 0), ("q", 1), ("k", 0), ("k", 1)]
        N_CONST = 9

        passed = {n: sem(f"passed_{n}") for n in ("sp", "pool", "dve")}

        def settled(name, engine):
            engine.sem_inc(passed[name], 1)

        @block.sync
        def _(sp):
            xv = a["x"].rearrange("o (b p) d -> p (o b) d", p=P)
            for c in range(NC):
                sp.dma_start(X[:, BPC * c:BPC * (c + 1), :], xv[:, BPC * c:BPC * (c + 1), :]).then_inc(x_ins[c], 16)
            km = lambda w: w.rearrange("(k p) n -> p k n", p=P)
            for x in ("q", "k", "v", "o"):
                sp.dma_start(W0[x], km(a["L0a_" + x])).then_inc(w0_in, 16)
            sp.dma_start(NAT["gate"], km(a["gate"])).then_inc(w_nat_in, 16)
            sp.dma_start(NAT["up"], km(a["up"])).then_inc(w_nat_in, 16)
            sp.dma_start(NAT["down"], km(a["down"])).then_inc(w_nat_in, 16)
            for x in ("q", "k", "v", "o"):
                sp.dma_start(NATL[x], km(a["L0b_" + x])).then_inc(w_nat_in, 16)
            for i, x in enumerate(("lq1", "lk1", "lq2", "lk2")):
                sp.dma_start(LV[:, i, :], a[x].partition_broadcast(P)).then_inc(lam_in, 16)
            sp.dma_start(SEL[:], a["rows"]).then_inc(lam_in, 16)
            parts = Count()

            def parts_to_dram(dst, rows):
                n = parts.next() - 1
                sp.wait_ge(parts_ready, n + 1)
                sp.dma_start(dst, STG[0:rows, n % 2, :, :]).then_inc(parts_out[n % 2], 16)

            def project(kind, c):
                L = PROJ[kind][0]
                t = slice(c * CH, (c + 1) * CH)
                for w, e in PARTS_ORDER:
                    parts_to_dram(scr[L.name, w][:, e * P:(e + 1) * P, t].rearrange("i f t -> f i t"), P)
                if L.rope:
                    for w in "qk":
                        parts_to_dram(scr_r[w][:, :, t].rearrange("i f t -> f i t"), ROPE)

            def load_head(L, j, row, slot):
                q, k = scr[L.name, "q"], scr[L.name, "k"]
                rows = lambda w, i, n=1: w[i:i + n, bass.ds(row, DH), :]
                s = bass.ds(slot, T)
                for n, i in enumerate((0, 0, 0, 1, 1, 2)):
                    sp.dma_start(QS[n * DH:(n + 1) * DH, s], rows(q, i)).then_inc(L.stack_in[j], 16)
                sp.dma_start(KS[0:3 * DH, s], rows(k, 0, 3)).then_inc(L.stack_in[j], 16)
                sp.dma_start(KS[3 * DH:5 * DH, s], rows(k, 0, 2)).then_inc(L.stack_in[j], 16)
                sp.dma_start(KS[5 * DH:6 * DH, s], rows(k, 0)).then_inc(L.stack_in[j], 16)

            def max_rows(L, parity, ring_base):
                sp.wait_ge(L.slot_free, ring_base)
                settled("sp", sp)
                for i in range(PARTS):
                    dst = QS[MROW + i:MROW + i + 1, bass.ds(parity * HG * T, HG * T)]
                    src = MR[64 * (i % 2):64 * (i % 2) + 64, i // 2, :]
                    sp.dma_start(dst.rearrange("o (n t) -> o n t", t=P), src).then_inc(L.max_rows_in, 16)

            def attention(L):
                for i in range(2):
                    sp.wait_ge(parts_out[i], 16 * ((parts.k + 1 - i) // 2))
                for j in range(HG):
                    load_head(L, j, j * DH, j * T)
                if L.rope:
                    rq, rk = scr_r["q"], scr_r["k"]
                    for i, (top, bottom) in enumerate(((rq[0], rq[0]), (rq[1], rq[1]), (rq[0], rq[2]), (rk[0], rk[1]), (rk[2], rk[0]))):
                        sp.dma_start(RS[0:ROPE, i, :], top).then_inc(L.rope_in, 16)
                        sp.dma_start(RS[ROPE:P, i, :], bottom).then_inc(L.rope_in, 16)
                for j in range(HG):
                    sp.wait_ge(L.stack_in[j], STACK_DMAS)
                    load_head(L, j, (HG + j) * DH, (HG + j) * T)
                at = max(i for i, s in enumerate([s for s in L.stage if s[0] in ("max", "mtr", "otr")]) if s[0] == "mtr") + 1
                max_rows(L, 0, L.r_first)
                with sp.Fori(0, NG - 2) as g:
                    sp.wait_ge(L.max_rows_in, (g + 1) * 16 * PARTS)
                    max_rows(L, 1 - (g & 1), g * L.r_stage + (L.r_first + at))
                    sp.wait_ge(L.pv_done, (g + 1) * L.n_unit)
                    settled("sp", sp)
                    for j in range(HG):
                        sp.wait_ge(L.stack_in[j], (g + 2) * STACK_DMAS)
                        settled("sp", sp)
                        load_head(L, j, (g + 2) * (HG * DH) + j * DH, (g & 1) * (HG * T) + j * T)
                max_rows(L, (NG - 1) & 1, (NG - 2) * L.r_stage + L.r_first + at)

            for kind, steps in PROGRAM:
                if steps is None:
                    attention(att[kind])
                    if kind == "A":
                        sp.wait_ge(L0.pv_done, NG * L0.n_unit)
                        for dst, src in ((W2["q"], km(a["L1b_q"])), (W2["o"], km(a["L1b_o"])), (WN, km(a["hyp_w"])),
                                         (SCALE, a["hyp_scale"].partition_broadcast(P)),
                                         (WKV, km(a["kv"])), (WKUP, a["kup"]), (WVUP, a["vup"])):
                            sp.dma_start(dst, src).then_inc(w2_in, 16)
                        half = ROPE // 2
                        for i in range(2):
                            for h in range(2):
                                o = half * (h if i == 0 else 1 - h)
                                dst = slice(o, o + half)
                                src = slice(half * h, half * (h + 1))
                                sp.dma_start(WQR[i][:, :, dst], km(a["qr"])[:, :, src]).then_inc(w2_in, 16)
                                sp.dma_start(WKR[i][:, dst], a["kr"][:, src]).then_inc(w2_in, 16)
                    continue
                for k, c, d0, a0 in steps:
                    if (k, c) == ("p1", 0):
                        sp.wait_ge(l1w_free, 1)
                        sp.dma_start(WAT, km(a["attn"])).then_inc(w1_in, 16)
                        sp.dma_start(W1A["o"], km(a["proj"])).then_inc(w1_in, 16)
                    if (k, c) == ("p2", 0):
                        sp.wait_ge(L1.pv_done, NG * L1.n_unit)
                        sp.dma_start(COS, a["cos"]).then_inc(rope_tab_in, 16)
                        sp.dma_start(SIN, a["sin"]).then_inc(rope_tab_in, 16)
                    if k in PROJ:
                        project(k, c)
                    if k == "hypout":
                        sp.wait_ge(x_done, c + 1)
                        ov = out.rearrange("o (b p) d -> p (o b) d", p=P)
                        sp.dma_start(ov[:, BPC * c:BPC * (c + 1), :], X[:, BPC * c:BPC * (c + 1), :]).then_inc(out_dma, 16)
            sp.wait_ge(out_dma, 16 * NC)

        @block.gpsimd
        def _(pool):
            g_ = nc.gpsimd
            order = Count()

            def link(ins):
                ins.then_inc(gp, 1)
                pool.wait_ge(gp, order.next())

            consts = Count()

            def constant(ins):
                ins.then_inc(const_ready, 1)
                pool.wait_ge(const_ready, consts.next())

            link(g_.memset(IDF[:], 0.0))
            link(g_.affine_select(out=IDF[:], in_=IDF[:], compare_op=ALU.not_equal, fill=1.0, base=0,
                                  pattern=[[-1, P]], channel_multiplier=1))
            constant(g_.tensor_copy(IDB[:], IDF[:]))
            link(g_.memset(MASKS[:, 0, :], 1.0))
            constant(g_.affine_select(out=MASKS[:, 0, W1 - P:W1], in_=MASKS[:, 0, W1 - P:W1], compare_op=ALU.is_ge, fill=0.0,
                                      base=0, pattern=[[-1, P]], channel_multiplier=1))
            constant(g_.tensor_scalar(MASKS[:, 1, :], MASKS[:, 0, :], -1.0, -LOWEST, ALU.add, ALU.mult))
            link(g_.memset(ONESEL[:], 0.0))
            constant(g_.memset(ONESEL[MROW:KROWS, :], 1.0))
            constant(g_.memset(ONE[:], 1.0))
            constant(g_.memset(VG[:, :, :, DH:2 * DH], 1.0))
            constant(g_.memset(FG[:, NB - 1, :, :], 0.0))
            constant(g_.memset(NM[:, 3, :], 0.0))
            constant(g_.memset(KS[MROW:KROWS, :], 1.0))
            parts = Count()

            def split(rows):
                n = parts.next() - 1
                pool.wait_ge(split_ready, n + 1)
                link(g_.tensor_copy(STG[0:rows, n % 2, 1, :], TA[0:rows, n % 2, :]))
                g_.tensor_tensor(STG[0:rows, n % 2, 2, :], TA[0:rows, n % 2, :], STG[0:rows, n % 2, 1, :], ALU.subtract)\
                    .then_inc(parts_ready, 1)

            def stage(L, g):
                chain = Count(g * (NB - 1))
                quarter = NB // 4
                for i in range(4):
                    b = slice(quarter * i, quarter * (i + 1))
                    src = VALL[:, b, bass.ds(g * (HG * DH), HG * DH)].rearrange("p b (j d) -> p b j d", d=DH)
                    g_.tensor_copy(VG[:, b, :, 0:DH], src).then_inc(L.v_ready, 1)
                for step in L.stage:
                    if step[0] != "score" and step[0] != "pv":
                        continue
                    u = step[1]
                    kind, c, sb_, off = L.units[u]
                    if step[0] == "score" and L.diagonal(u):
                        for j in range(HG):
                            tile = PT[:, u % SETS, j, off:off + P]
                            pool.wait_ge(L.exp_done, g * L.n_exp + (L.exp_no[u] + j + 1))
                            settled("pool", pool)
                            g_.affine_select(out=tile, in_=tile, compare_op=ALU.is_ge, fill=0.0, base=0,
                                             pattern=[[1, P]], channel_multiplier=-1).then_inc(L.mask_done, 1)
                    if step[0] == "score" and kind == "e":
                        if c == 0:
                            pool.wait_ge(L.v_ready, g * 4 + 4)
                            for b in range(NB - 2, -1, -1):
                                g_.tensor_tensor(FG[:, b], FG[:, b + 1], VG[:, b + 1], ALU.add).then_inc(L.suffix_ready, 1)
                                pool.wait_ge(L.suffix_ready, chain.next())
                        m = u + 1
                        if m >= SETS:
                            pool.wait_ge(L.pv_done, g * L.n_unit + (m - SETS + 1))
                        for j in range(HG):
                            pool.wait_ge(L.exp_done, g * L.n_exp + (L.exp_no[u] + j + 1))
                            settled("pool", pool)
                            v = lambda s: PT[:, s, j, :].rearrange("p (b t) -> p b t", t=P)
                            g_.affine_select(out=v(m % SETS), in_=v(u % SETS), compare_op=ALU.is_ge, fill=0.0, base=-1,
                                             pattern=[[0, BPC], [-1, P]], channel_multiplier=1).then_inc(L.mask_done, 1)

                pool.wait_ge(L.pv_done, (g + 1) * L.n_unit)

            for kind, steps in PROGRAM:
                if steps is None:
                    L = att[kind]
                    pool.wait_ge(a_free, A_COUNT[kind])
                    with pool.Fori(0, NG) as g:
                        stage(L, g)
                    continue
                for k, c, d0, a0 in steps:
                    if (k, c) == ("p1", 0):
                        pool.wait_ge(w1_in, 32)
                        half = D // 2
                        for n, w in enumerate(("q", "k")):
                            for i in range(2):
                                dst = W1A[w].rearrange("p k (h i d) -> p k h i d", i=2, d=DH // 2)[:, :, :, i, :]
                                o = (2 * i + n) * half
                                src = WAT[:, :, o:o + half].rearrange("p k (h d) -> p k h d", d=DH // 2)
                                for kk in range(KD):
                                    g_.tensor_copy(dst[:, kk], src[:, kk]).then_inc(perm_done, 1)
                    if k in PROJ:
                        for w, e in PARTS_ORDER:
                            split(P)
                        if PROJ[k][0].rope:
                            for w in "qk":
                                split(ROPE)

        @block.tensor
        def _(pe):
            mm = nc.tensor.matmul
            nd, na = Count(), Count()

            def d_bank():
                n = nd.next() - 1
                if n >= 4:
                    pe.wait_ge(d_free, n - 3)
                return n % 4

            def a_bank():
                n = na.next() - 1
                if n >= 4:
                    pe.wait_ge(a_free, n - 3)
                return 4 + n % 4

            def over_k(dst, left, right, n=KD):
                for k in range(n):
                    ins = mm(dst, left(k), right(k), start=k == 0, stop=k == n - 1)
                return ins

            def weight_transposes():
                pe.wait_ge(w_nat_in, 16 * 7)
                for w in ("gate", "up"):
                    for k in range(KD):
                        for m0 in range(0, HID // P, 4):
                            b = a_bank()
                            for i in range(4):
                                ins = nc.tensor.transpose(bank(b, P, i * P), NAT[w][:, m0 + i, k * P:(k + 1) * P], IDF[:])
                            ins.then_inc(a_ready, 1)
                for m in range(0, HID // P, 2):
                    b = a_bank()
                    for i in range(4):
                        ins = nc.tensor.transpose(bank(b, P, i * P), NAT["down"][:, i % 2, (m + i // 2) * P:(m + i // 2 + 1) * P], IDF[:])
                    ins.then_inc(a_ready, 1)
                for w in ("q", "k", "v", "o"):
                    b = a_bank()
                    for i in range(4):
                        ins = nc.tensor.transpose(bank(b, P, i * P), NATL[w][:, i % 2, (i // 2) * P:(i // 2 + 1) * P], IDF[:])
                    ins.then_inc(a_ready, 1)

            def norm_transposes(n):
                pe.wait_ge(norm_ready, n + 1)
                for k in range(KD):
                    b = a_bank()
                    for i in range(BPC):
                        ins = nc.tensor.transpose(bank(b, P, i * P), LNH[:, n % 2, i, k * P:(k + 1) * P], IDF[:])
                    ins.then_inc(a_ready, 1)

            def token_major(left, right, n_k, ring, ready, wide=2):
                for h in range(BPC // 2):
                    b = ring()
                    for i in range(2):
                        ins = over_k(bank(b, D, i * D), lambda k: left(k, 2 * h + i), right, n_k)
                    ins.then_inc(ready, 1)

            def main(k, c, d0, a0):
                ht = lambda kk: HT[:, c, kk, :]
                blk = lambda i: slice(i * P, (i + 1) * P)
                if k not in ("o0", "o1", "o2"):
                    pe.wait_ge(a_free, HT_AT[NC * (norms.k // NC - 1) + c])
                if k in ("p0", "p1"):
                    L, W, _ = PROJ[k]
                    if (k, c) == ("p0", 0):
                        pe.wait_ge(w0_in, 16 * 4)
                    if (k, c) == ("p1", 0):
                        pe.wait_ge(perm_done, 4 * KD)
                    for w, e in PARTS_ORDER:
                        b = d_bank()
                        over_k(bank(b), lambda kk: W[w][:, kk, e * P:(e + 1) * P], ht).then_inc(d_ready, 1)
                    token_major(lambda kk, i: HT[:, c, kk, blk(i)], lambda kk: W["v"][:, kk, :], KD, a_bank, a_ready)
                if k == "p2":
                    L, W, _ = PROJ[k]
                    b = a_bank()
                    over_k(bank(b)[0:LATENT], lambda kk: WKV[:, kk, :], ht).then_inc(a_ready, 1)
                    latent_done = na.k
                    for e in range(KD):
                        b = d_bank()
                        over_k(bank(b), lambda kk: W["q"][:, kk, e * P:(e + 1) * P], ht).then_inc(d_ready, 1)
                    pe.wait_ge(a_free, latent_done)
                    for e in range(KD):
                        b = d_bank()
                        mm(bank(b), WKUP[:, e * P:(e + 1) * P], CKV[:, c % 2, :], start=True, stop=True).then_inc(d_ready, 1)
                    for i in range(2):
                        b = d_bank()
                        over_k(bank(b)[0:ROPE], lambda kk: WQR[i][:, kk, :], ht).then_inc(d_ready, 1)
                    for i in range(2):
                        b = d_bank()
                        mm(bank(b)[0:ROPE], WKR[i], CKV[:, c % 2, :], start=True, stop=True).then_inc(d_ready, 1)
                    token_major(lambda kk, i: CKV[:, c % 2, blk(i)], lambda kk: WVUP, 1, a_bank, a_ready)
                if k in ("o0", "o1", "o2"):
                    for kk in range(KD):
                        b = a_bank()
                        for i in range(BPC):
                            ins = nc.tensor.transpose(bank(b, P, i * P), ON[:, BPC * c + i, kk * P:(kk + 1) * P], IDF[:])
                        ins.then_inc(a_ready, 1)
                    pe.wait_ge(a_free, na.k)
                    token_major(lambda kk, i: OT[:, c % 2, kk, blk(i)], lambda kk: OUTW[k][:, kk, :], KD, d_bank, d_ready)
                if k == "ffn":
                    for m in range(HID // P):
                        for W in (WGT, WUT):
                            b = d_bank()
                            over_k(bank(b), lambda kk: W[:, kk, m * P:(m + 1) * P], ht).then_inc(d_ready, 1)
                    for h in range(BPC // 2):
                        b = d_bank()
                        for i in range(2):
                            for m in range(HID // P):
                                if h == 0 and i == 0:
                                    pe.wait_ge(d_free, d0 + 2 * m + 2)
                                ins = mm(bank(b, D, i * D), GT[:, m, blk(2 * h + i)], WDT[:, m, :], start=m == 0, stop=m == HID // P - 1)
                        ins.then_inc(d_ready, 1)
                if k == "lin":
                    for e in range(KD):
                        for w in ("v", "k", "q"):
                            b, ready = (a_bank(), a_ready) if w == "v" else (d_bank(), d_ready)
                            over_k(bank(b), lambda kk: WL[w][:, kk, e * P:(e + 1) * P], ht).then_inc(ready, 1)
                    pe.wait_ge(d_free, d0 + 2 * KD)
                    token_major(lambda kk, i: VH[:, kk, blk(i)], lambda kk: OUTW[k][:, kk, :], KD, d_bank, d_ready)
                if k in ("hyp", "hypout"):
                    token_major(lambda kk, i: HT[:, c, kk, blk(i)], lambda kk: WN[:, kk, :], KD, d_bank, d_ready)

            def max_job(L, n, ring, off):
                j, tb, i, s0, w, diag = L.jobs[n]
                slot = (ring.k - 1) % 2 * 2
                for x in range(0, w, CH):
                    width = min(CH, w - x)
                    q = QS[0:SROWS, bass.ds(off + (j * T + tb * P), P)]
                    k = KS[0:SROWS, bass.ds(off + (j * T + s0 + x), width)]
                    ins = mm(bank(slot + x // CH, width), q, k, start=True, stop=not L.rope)
                    if L.rope:
                        for r in range(3):
                            ins = mm(bank(slot + x // CH, width), RS[:, ROPE_Q[r], tb * P:(tb + 1) * P],
                                     RS[:, ROPE_K[r], s0 + x:s0 + x + width], start=False, stop=r == 2)
                return ins

            def attention_steps(L, steps, group, ring, off1, off2, group1):
                job = 0
                for step in steps:
                    if step[0] in ("max", "mtr", "otr"):
                        n = ring.next()
                        if not (type(n) is int and n <= 2):
                            pe.wait_ge(L.slot_free, n - 2)
                        slot = (ring.k - 1) % 2 * 2
                    if step[0] == "max":
                        if L.jobs[step[1]][1:3] == (0, 0):
                            pe.wait_ge(L.stack_in[L.jobs[step[1]][0]], (group1 + 1) * STACK_DMAS)
                        max_job(L, step[1], ring, off1).then_inc(L.slot_ready, 1)
                    if step[0] == "mtr":
                        pe.wait_ge(L.neg_ready, group1 + 1)
                        dst = bank(slot).bitcast(BF16)
                        src = NM[:, 2 * step[1]:2 * step[1] + 2, :].rearrange("p i n -> p (i n)")
                        nc.tensor.transpose(dst[:, 0:P], src, IDB[:]).then_inc(L.slot_ready, 1)
                    if step[0] == "otr":
                        pe.wait_ge(L.out_saved, group * NC + (step[1] + 1))
                        for i in range(BPC):
                            ins = nc.tensor.transpose(bank(slot, P, i * P), OS[:, i * P:(i + 1) * P], IDF[:])
                        ins.then_inc(L.slot_ready, 1)
                    if step[0] == "score":
                        u = step[1]
                        kind, c, sb_, off = L.units[u]
                        if u == 0:
                            pe.wait_ge(L.max_rows_in, (group + 1) * 16 * PARTS)
                        for j in range(HG):
                            n = L.exp_no[u] + j
                            if n >= RING2:
                                pe.wait_ge(L.exp_done, group * L.n_exp + (n - RING2 + 1))
                            q = QS[0:KROWS, bass.ds(off2 + (j * T + c * CH + off), CH - off)]
                            dst = bank(4 + n % RING2, CH - off)
                            if kind == "e":
                                ins = mm(dst, ONESEL[0:KROWS, :], q, start=True, stop=True)
                            else:
                                k = KS[0:KROWS, bass.ds(off2 + (j * T + sb_ * P), P)]
                                ins = mm(dst, k, q, start=True, stop=not L.rope)
                                if L.rope:
                                    for r in range(3):
                                        ins = mm(dst, RS[:, ROPE_K[r], sb_ * P:(sb_ + 1) * P],
                                                 RS[:, ROPE_Q[r], c * CH + off:(c + 1) * CH], start=False, stop=r == 2)
                            ins.then_inc(L.score_ready, 1)
                    if step[0] == "pv":
                        u = step[1]
                        kind, c, sb_, off = L.units[u]
                        first, last = u == 0 or u - 1 in L.chunk_last, u in L.chunk_last
                        if first and c == 0:
                            pe.wait_ge(L.v_ready, group * 4 + 1)
                        if kind == "s" and sb_ % 4 == 0 and c == (sb_ // 4 if L.causal else 0):
                            pe.wait_ge(L.v_ready, group * 4 + (sb_ // 4 + 1))
                        if kind == "e" and c == 0:
                            pe.wait_ge(L.suffix_ready, (group + 1) * (NB - 1))
                        if first and c > 0:
                            pe.wait_ge(L.out_saved, group * NC + c)
                        if kind == "m" or L.diagonal(u):
                            pe.wait_ge(L.mask_done, group * L.n_mask + (L.mask_no[u] + HG))
                        else:
                            pe.wait_ge(L.exp_done, group * L.n_exp + (L.exp_no[u] + HG))
                        pieces = [(off, CH)] if kind == "s" else [(i * P, (i + 1) * P) for i in range(BPC)]
                        for i, (t0, t1) in enumerate(pieces):
                            for j in range(HG):
                                V = VG[:, sb_, j, :] if kind == "s" else (FG if kind == "e" else VG)[:, BPC * c + i, j, :]
                                ins = mm(PS[32 * j:32 * j + 2 * DH, 7 * CH + t0:7 * CH + t1], V, PT[:, u % SETS, j, t0:t1],
                                         start=first, stop=last, tile_position=(0, 32 * j), skip_group_check=True)
                        ins.then_inc(L.pv_done, 1)

            def attention(L):
                pe.wait_ge(d_free, D_COUNT[L_KEY[L.name]])
                pe.wait_ge(a_free, A_COUNT[L_KEY[L.name]])
                pe.wait_ge(const_ready, N_CONST)
                if L.rope:
                    pe.wait_ge(L.rope_in, 16 * 10)
                attention_steps(L, L.first, None, Count(0), 0, None, 0)
                for g in range(NG - 1):
                    off2 = (g & 1) * HG * T
                    attention_steps(L, L.stage, g, Count(g * L.r_stage + L.r_first), HG * T - off2, off2, g + 1)
                g = NG - 1
                attention_steps(L, L.last, g, Count(g * L.r_stage + L.r_first), None, (g & 1) * HG * T, None)
                pe.wait_ge(L.slot_free, g * L.r_stage + L.r_first + NC)
                pe.wait_ge(L.out_saved, NG * NC)

            pe.wait_ge(const_ready, 1)
            weight_transposes()
            norms = Count()
            for kind, steps in PROGRAM:
                if steps is None:
                    attention(att[kind])
                    continue
                pending = None
                if kind == "" and steps[0][0] == "o1":
                    pe.wait_ge(w2_in, 16 * 15)
                for k, c, d0, a0 in steps:
                    if k != "in":
                        main(k, c, d0, a0)
                    if pending is not None:
                        norm_transposes(pending)
                    pending = norms.next() - 1 if k in HAS_NORM else None
                assert pending is None
            assert (nd.k, na.k) == (d_total, a_total)

        @block.scalar
        def _(act):
            sc = nc.scalar
            na, nd = Count(), Count()
            c_tanh, c_v, c_n2 = Count(), Count(), Count()

            def take(dst, src_of, scale=1.0, rows=P):
                n = na.next() - 1
                act.wait_ge(a_ready, n + 1)
                src = src_of(4 + n % 4)
                if scale == 1.0:
                    return sc.copy(dst, src)
                return sc.mul(dst, src, scale)

            def weight_copies():
                for w in (WGT, WUT):
                    for k in range(KD):
                        for m in range(2):
                            take(w[:, k, m * CH:(m + 1) * CH], bank).then_inc(a_free, 1)
                for m in range(4):
                    take(WDT[:, 2 * m:2 * m + 2, :], lambda b: bank(b).rearrange("p (m d) -> p m d", d=D)).then_inc(a_free, 1)
                for w in ("q", "k", "v", "o"):
                    take(WL[w], lambda b: bank(b).rearrange("p (k e) -> p k e", k=KD)).then_inc(a_free, 1)

            def main(k, c, d0, a0):
                if k == "lin":
                    for e in range(KD):
                        n = c_v.next()
                        if n > 2:
                            act.wait_ge(v_used, n - 2)
                        take(VS[:, n % 2, :], bank).then_inc(a_free, 1)
                if k in ("o0", "o1", "o2"):
                    for kk in range(KD):
                        take(OT[:, c % 2, kk, :], bank, 1.0 - LAMBDA_INIT if k == "o1" else 1.0).then_inc(a_free, 1)
                if k == "p2":
                    take(CKV[:, c % 2, :], lambda b: bank(b)[0:LATENT]).then_inc(a_free, 1)
                if k in ("p0", "p1", "p2"):
                    for h in range(2):
                        b0 = BPC * c + 2 * h
                        take(VALL[:, b0:b0 + 2, :], lambda b: bank(b).rearrange("p (b d) -> p b d", d=D)).then_inc(a_free, 1)
                if k == "ffn":
                    for m in range(HID // P):
                        n = c_tanh.next()
                        act.wait_ge(d_ready, d0 + 2 * m + 1)
                        if n > 2:
                            act.wait_ge(d_free, gates[n - 3])
                        gates.append(d0 + 2 * m + 1)
                        sc.activation(TH[:, n % 2, :], bank((d0 + 2 * m) % 4), ACT.Tanh, scale=0.5).then_inc(tanh_ready, 1)
                if k in ("hyp", "hypout"):
                    act.wait_ge(n2_ready, c_n2.next())
                    sc.activation(NW[:, 5, :], NW[:, 4, :], ACT.Tanh).then_inc(n2_tanh, 1)

            def norm_copies(c):
                for k in range(KD):
                    take(HT[:, c, k, :], bank).then_inc(a_free, 1)

            gates = []
            weight_copies()
            act.wait_ge(lam_dots, 1)
            sc.activation(LAM[:, 2:4], LAM[:, 4:6], ACT.Exp).then_inc(lam_exp, 1)
            for kind, steps in PROGRAM:
                if steps is None:
                    L = att[kind]
                    with act.Fori(0, NG) as g:
                        for u in L.exps:
                            for j in range(HG):
                                n = L.exp_no[u] + j
                                off = L.units[u][3]
                                act.wait_ge(L.score_ready, g * L.n_exp + (n + 1))
                                if j == 0 and u >= SETS:
                                    act.wait_ge(L.pv_done, g * L.n_unit + (u - SETS + 1))
                                if j == 0 and u >= SETS and L.units[u - SETS][0] == "e":
                                    act.wait_ge(L.mask_done, g * L.n_mask + (L.mask_no[u - SETS + 1] + HG))
                                sc.activation(PT[:, u % SETS, j, off:CH], bank(4 + n % RING2, CH - off), ACT.Exp).then_inc(L.exp_done, 1)
                    continue
                pending = None
                for k, c, d0, a0 in steps:
                    main(k, c, d0, a0)
                    if pending is not None:
                        norm_copies(pending)
                    pending = c if k in HAS_NORM else None

        @block.vector
        def _(dve):
            v = nc.vector
            order = Count()
            nd = Count()
            c_tanh, c_parts, c_n2 = Count(), Count(), Count()

            def link(*ins):
                for i in ins:
                    i.then_inc(vc, 1)
                    order.k += 1
                dve.wait_ge(vc, order.k)

            def bank_in():
                n = nd.next() - 1
                dve.wait_ge(d_ready, n + 1)
                return n % 4

            def rsqrt(dst, src, tmp):
                link(v.tensor_scalar(dst.bitcast(I32), src.bitcast(I32), 1, None, ALU.logical_shift_right))
                link(v.tensor_scalar(dst.bitcast(I32), dst.bitcast(I32), -1.0, float(0x5F3759DF), ALU.mult, ALU.add))
                for _ in range(4):
                    link(v.scalar_tensor_tensor(out=tmp, in0=dst, scalar=-0.5, in1=src, op0=ALU.mult, op1=ALU.mult))
                    link(v.tensor_tensor(tmp, tmp, dst, ALU.mult))
                    link(v.scalar_tensor_tensor(out=dst, in0=tmp, scalar=1.5, in1=dst, op0=ALU.add, op1=ALU.mult))

            norms = Count()

            def norm(c):
                n = norms.next() - 1
                link(*[v.bn_stats(ST[:, i, :], X[:, BPC * c + i, :]) for i in range(BPC)])
                link(*[v.bn_aggr(MV[:, i, :], ST[:, i, :]) for i in range(BPC)])
                link(v.tensor_scalar(NW[:, 0, :], MV[:, :, 1], LN_EPS, None, ALU.add))
                rsqrt(NW[:, 1, :], NW[:, 0, :], NW[:, 2, :])
                if n >= 2:
                    dve.wait_ge(a_free, HT_AT[n - 2])
                for i in range(BPC):
                    ins = v.tensor_scalar(LNH[:, n % 2, i, :], X[:, BPC * c + i, :], MV[:, i, 0:1], NW[:, 1, i:i + 1],
                                          ALU.subtract, ALU.mult)
                ins.then_inc(norm_ready, 1)

            def residual(c):
                for h in range(2):
                    b = bank_in()
                    x = X[:, BPC * c + 2 * h:BPC * c + 2 * h + 2, :]
                    ins = v.tensor_tensor(x, bank(b).rearrange("p (b d) -> p b d", d=D), x, ALU.add)
                    ins.then_inc(d_free, 1)
                    order_x(ins)

            def order_x(ins):
                dve.wait_ge(d_free, nd.k)

            def parts(rows, n):
                if n >= 2:
                    dve.wait_ge(parts_out[n % 2], 16 * (n // 2))
                link(v.tensor_copy(STG[0:rows, n % 2, 0, :], TH[0:rows, n % 2, :]))
                v.tensor_tensor(TA[0:rows, n % 2, :], TH[0:rows, n % 2, :], STG[0:rows, n % 2, 0, :], ALU.subtract)\
                    .then_inc(split_ready, 1)

            def main(k, c, d0, a0):
                if k in PROJ:
                    L, W, scale = PROJ[k]
                    for w, e in PARTS_ORDER:
                        b = bank_in()
                        n = c_parts.next() - 1
                        if w == "q" and scale is None:
                            if (c, e) == (0, 0):
                                dve.wait_ge(lam_done, 1)
                            ins = v.tensor_scalar(TH[:, n % 2, :], bank(b), QSC[:], None, ALU.mult)
                        elif w == "q":
                            ins = v.tensor_scalar(TH[:, n % 2, :], bank(b), float(scale), None, ALU.mult)
                        else:
                            ins = v.tensor_copy(TH[:, n % 2, :], bank(b))
                        ins.then_inc(d_free, 1)
                        dve.wait_ge(d_free, nd.k)
                        parts(P, n)
                    if L.rope:
                        if c == 0:
                            dve.wait_ge(rope_tab_in, 32)
                        t = slice(c * CH, (c + 1) * CH)
                        for w in "qk":
                            s = float(scale) if w == "q" else 1.0
                            n = c_parts.next() - 1
                            for i, tab in enumerate((COS, SIN)):
                                b = bank_in()
                                v.scalar_tensor_tensor(out=RA[:, i, :], in0=bank(b)[0:ROPE], scalar=s, in1=tab[:, t],
                                                       op0=ALU.mult, op1=ALU.mult).then_inc(d_free, 1)
                            dve.wait_ge(d_free, nd.k)
                            link(v.tensor_tensor(TH[0:ROPE, n % 2, :], RA[:, 0, :], RA[:, 1, :], ALU.add))
                            parts(ROPE, n)
                if k in ("o0", "o1", "o2"):
                    residual(c)
                if k == "ffn":
                    for m in range(HID // P):
                        n = c_tanh.next()
                        bg = bank_in()
                        dve.wait_ge(tanh_ready, n)
                        v.scalar_tensor_tensor(out=TA[:, n % 2, :], in0=TH[:, n % 2, :], scalar=1.0, in1=bank(bg),
                                               op0=ALU.add, op1=ALU.mult).then_inc(d_free, 1)
                        dve.wait_ge(d_free, nd.k)
                        bu = bank_in()
                        v.scalar_tensor_tensor(out=GT[:, m, :], in0=TA[:, n % 2, :], scalar=0.5, in1=bank(bu),
                                               op0=ALU.mult, op1=ALU.mult).then_inc(d_free, 1)
                    residual(c)
                if k == "lin":
                    for e in range(KD):
                        b = bank_in()
                        n = KD * c + e + 1
                        dve.wait_ge(a_free, a0 + e + 1)
                        v.tensor_tensor(TA[:, n % 2, :], bank(b), VS[:, n % 2, :], ALU.mult).then_inc(d_free, 1)
                        dve.wait_ge(d_free, nd.k)
                        init = 0.0 if c == 0 else CUM[:, (c + 1) % 2, e, CH - 1:CH]
                        ins = v.tensor_tensor_scan(CUM[:, c % 2, e, :], ONE[:].to_broadcast([P, CH]), TA[:, n % 2, :], init,
                                                   ALU.mult, ALU.add)
                        ins.then_inc(v_used, 1)
                        dve.wait_ge(v_used, n)
                        b = bank_in()
                        ins = v.scalar_tensor_tensor(out=VH[:, e, :], in0=bank(b), scalar=float(D) ** 0.5 / T, in1=CUM[:, c % 2, e, :],
                                                     op0=ALU.mult, op1=ALU.mult)
                        ins.then_inc(d_free, 1)
                    residual(c)
                    if c == NC - 1:
                        v.tensor_copy(NW[:, 6, 0:1], ONE[:]).then_inc(l1w_free, 1)
                if k in ("hyp", "hypout"):
                    if (k, c) == ("hyp", 0):
                        dve.wait_ge(w2_in, 16 * 15)
                    for h in range(2):
                        b = bank_in()
                        v.tensor_tensor(Y2[:, 2 * h:2 * h + 2, :], bank(b).rearrange("p (b d) -> p b d", d=D),
                                        SCALE.unsqueeze(1).to_broadcast([P, 2, D]), ALU.mult).then_inc(d_free, 1)
                    dve.wait_ge(d_free, nd.k)
                    link(*[v.tensor_tensor_reduce(out=JUNK[:, i * D:(i + 1) * D], in0=Y2[:, i, :], in1=Y2[:, i, :], scale=1.0, scalar=0.0,
                                                  op0=ALU.mult, op1=ALU.add, accum_out=NW[:, 0, i:i + 1]) for i in range(BPC)])
                    rsqrt(NW[:, 1, :], NW[:, 0, :], NW[:, 2, :])
                    link(v.tensor_tensor(NW[:, 3, :], NW[:, 0, :], NW[:, 1, :], ALU.mult))
                    v.tensor_scalar(NW[:, 4, :], NW[:, 3, :], EPS, None, ALU.max).then_inc(n2_ready, 1)
                    dve.wait_ge(n2_ready, c_n2.next())
                    link(v.tensor_scalar(NW[:, 6, :], NW[:, 4, :], EPS, None, ALU.add))
                    link(v.reciprocal(NW[:, 6, :], NW[:, 6, :]))
                    dve.wait_ge(n2_tanh, c_n2.k)
                    link(v.tensor_tensor(NW[:, 6, :], NW[:, 5, :], NW[:, 6, :], ALU.mult))
                    link(v.tensor_tensor(NW[:, 7, :], NW[:, 3, :], NW[:, 6, :], ALU.mult))
                    link(v.tensor_scalar(NW[:, 7, :], NW[:, 7, :], EPS, None, ALU.max))
                    link(v.reciprocal(NW[:, 7, :], NW[:, 7, :]))
                    link(v.tensor_scalar(NW[:, 7, :], NW[:, 7, :], MAX_NORM, 1.0, ALU.mult, ALU.min))
                    link(v.tensor_tensor(NW[:, 7, :], NW[:, 7, :], NW[:, 6, :], ALU.mult))
                    done = []
                    for i in range(BPC):
                        x = X[:, BPC * c + i, :]
                        done.append(v.scalar_tensor_tensor(out=x, in0=Y2[:, i, :], scalar=NW[:, 7, i:i + 1], in1=x,
                                                           op0=ALU.mult, op1=ALU.add))
                    if k == "hypout":
                        done[-1].then_inc(x_done, 1)
                        dve.wait_ge(x_done, c + 1)
                    else:
                        link(*done)

            def attention_steps(L, steps, group, ring, group1, chain):
                def clink(ins):
                    ins.then_inc(L.chain, 1)
                    dve.wait_ge(L.chain, chain.next())

                for step in steps:
                    if step[0] in ("max", "mtr", "otr"):
                        n = ring.next()
                        dve.wait_ge(L.slot_ready, n)
                        slot = (ring.k - 1) % 2 * 2
                    if step[0] == "max":
                        j, tb, i, s0, w, diag = L.jobs[step[1]]
                        src = PS[:, slot * CH:slot * CH + w]
                        dst = MP[:, i, j * NB + tb:j * NB + tb + 1]
                        if diag:
                            if not (type(n) is int and n == 1):
                                dve.wait_ge(L.slot_free, n - 1)
                            settled("dve", dve)
                            low = 0.0 if L.zeros and tb < NB - 1 else LOWEST
                            ins = v.tensor_tensor_reduce(out=JUNK[:, 0:w], in0=src, in1=MASKS[:, 0 if L.zeros else 1, W1 - w:W1],
                                                         scale=1.0, scalar=low, op0=ALU.mult if L.zeros else ALU.add, op1=ALU.max,
                                                         accum_out=dst)
                        else:
                            ins = v.reduce_max(dst, src, AX.X)
                        ins.then_inc(L.slot_free, 1)
                    if step[0] == "neg":
                        dve.wait_ge(L.slot_free, ring.base + ring.k)
                        clink(v.tensor_tensor(MX[:, 0, :], MP[:, 0, :], MP[:, 1, :], ALU.max))
                        clink(v.tensor_scalar(NM[:, 0, :], MX[:, 0, :], -1.0, None, ALU.mult))
                        clink(v.scalar_tensor_tensor(out=MX[:, 1, :], in0=MX[:, 0, :], scalar=-1.0, in1=NM[:, 0, :],
                                                     op0=ALU.mult, op1=ALU.subtract))
                        clink(v.tensor_copy(NM[:, 1, :], MX[:, 1, :]))
                        v.tensor_tensor(NM[:, 2, :], MX[:, 1, :], NM[:, 1, :], ALU.subtract).then_inc(L.neg_ready, 1)
                    if step[0] == "mtr":
                        if step[1] == 0 and not (type(group1) is int and group1 == 0):
                            dve.wait_ge(L.max_rows_in, group1 * (16 * PARTS))
                        v.tensor_copy(MR[:, step[1], :], bank(slot).bitcast(BF16)[:, 0:P]).then_inc(L.slot_free, 1)
                    if step[0] == "save":
                        dve.wait_ge(L.pv_done, group * L.n_unit + (L.chunk_last[step[1]] + 1))
                        v.tensor_copy(OS[:], bank(7)).then_inc(L.out_saved, 1)
                    if step[0] == "otr":
                        src = bank(slot).rearrange("p (b j d) -> p b j d", b=BPC, j=HG)
                        clink(v.reciprocal(RZ[:].unsqueeze(3), src[:, :, :, DH:DH + 1]))
                        b0 = BPC * step[1]
                        dst = ON[:, b0:b0 + BPC, bass.ds(group * (HG * DH), HG * DH)].rearrange("p b (j d) -> p b j d", d=DH)
                        v.tensor_tensor(dst, src[:, :, :, 0:DH], RZ[:].unsqueeze(3).to_broadcast([P, BPC, HG, DH]), ALU.mult)\
                            .then_inc(L.slot_free, 1)

            def lambdas():
                dve.wait_ge(lam_in, 16 * 5)
                link(*[v.tensor_tensor_reduce(out=JUNK[:, i * D:(i + 1) * D], in0=LV[:, 2 * i, :], in1=LV[:, 2 * i + 1, :], scale=1.0, scalar=0.0,
                                              op0=ALU.mult, op1=ALU.add, accum_out=LAM[:, i:i + 1]) for i in range(2)])
                v.tensor_copy(LAM[:, 4:6], LAM[:, 0:2]).then_inc(lam_dots, 1)
                dve.wait_ge(lam_exp, 1)
                link(v.tensor_tensor(LAM[:, 6:7], LAM[:, 2:3], LAM[:, 3:4], ALU.subtract))
                link(v.tensor_scalar(LAM[:, 6:7], LAM[:, 6:7], LAMBDA_INIT, -DIFF_SCALE, ALU.add, ALU.mult))
                link(v.tensor_scalar(LAM[:, 7:8], SEL[:, 0:1], DIFF_SCALE, None, ALU.mult))
                v.scalar_tensor_tensor(out=QSC[:], in0=SEL[:, 1:2], scalar=LAM[:, 6:7], in1=LAM[:, 7:8], op0=ALU.mult,
                                       op1=ALU.add).then_inc(lam_done, 1)

            def attention(L):
                link(v.memset(MP[:], LOWEST))
                attention_steps(L, L.first, None, Count(0), 0, Count(0))
                with dve.Fori(0, NG - 1) as g:
                    attention_steps(L, L.stage, g, Count(g * L.r_stage + L.r_first), g + 1, Count(g * L.chain_stage + L.chain_first))
                g = NG - 1
                attention_steps(L, L.last, g, Count(g * L.r_stage + L.r_first), None, Count(g * L.chain_stage + L.chain_first))

            dve.wait_ge(const_ready, N_CONST)
            lambdas()
            for kind, steps in PROGRAM:
                if steps is None:
                    attention(att[kind])
                    continue
                for k, c, d0, a0 in steps:
                    if k == "in":
                        dve.wait_ge(x_ins[c], 16)
                    else:
                        main(k, c, d0, a0)
                    if k in HAS_NORM:
                        norm(c)
    return nc


_NAMES = {"x": "L0_attn_a_x", "L0a_q": "L0_attn_a_Wq", "L0a_k": "L0_attn_a_Wk", "L0a_v": "L0_attn_a_Wv", "L0a_o": "L0_attn_a_Wo",
          "L0b_q": "L0_attn_b_Wq", "L0b_k": "L0_attn_b_Wk", "L0b_v": "L0_attn_b_Wv", "L0b_o": "L0_attn_b_Wo",
          "gate": "L0_ffn_w_gate", "up": "L0_ffn_w_up", "down": "L0_ffn_w_down", "attn": "L1_attn_a_W_attn",
          "proj": "L1_attn_a_W_proj", "lq1": "L1_attn_a_lambda_q1", "lk1": "L1_attn_a_lambda_k1",
          "lq2": "L1_attn_a_lambda_q2", "lk2": "L1_attn_a_lambda_k2", "kv": "L1_attn_b_Wkv", "kup": "L1_attn_b_Wkup",
          "vup": "L1_attn_b_Wvup", "L1b_q": "L1_attn_b_Wq", "qr": "L1_attn_b_Wqr", "kr": "L1_attn_b_Wkr",
          "L1b_o": "L1_attn_b_Wo", "hyp_w": "L1_ffn_weight", "hyp_scale": "L1_ffn_scale"}


def _shape_constants():
    inv = (1.0 / np.power(np.float32(10000.0), np.arange(0, ROPE, 2, dtype=np.float32) / np.float32(ROPE))).astype(np.float32)
    angle = np.outer(inv, np.arange(T, dtype=np.float32)).astype(np.float32)
    cos, sin = np.cos(angle).astype(np.float32), np.sin(angle).astype(np.float32)
    first = (np.arange(P) % DH < DH // 2).astype(np.float32)
    return {"cos": np.concatenate([cos, cos]), "sin": np.concatenate([-sin, sin]), "rows": np.stack([first, 1 - first], 1)}


def kernel(**inputs):
    import concourse.bacc as bacc
    from concourse.bass_utils import run_bass_kernel_spmd

    nc = bacc.Bacc("TRN2", target_bir_lowering=False, num_devices=1)
    given = {k: np.ascontiguousarray(inputs[n]) for k, n in _NAMES.items()}
    given.update(_shape_constants())
    arrays = {f"in_{k}": np.ascontiguousarray(x) for k, x in given.items()}
    aps = {k: nc.dram_tensor(f"in_{k}", x.shape, mybir.dt.from_np(x.dtype), kind="ExternalInput").ap() for k, x in given.items()}
    out = nc.dram_tensor("out_0", (1, T, D), F32, kind="ExternalOutput").ap()
    build(nc, aps, out)
    return run_bass_kernel_spmd(nc, [arrays], core_ids=[0]).results[0]["out_0"]
```

```python
from contextlib import ExitStack

import numpy as np

import concourse.bass as bass
from concourse import mybir

F32 = mybir.dt.float32
BF16 = mybir.dt.bfloat16
I32 = mybir.dt.int32
ALU = mybir.AluOpType
ACT = mybir.ActivationFunctionType
AX = mybir.AxisListType

P = 128
T, D, HID = 2048, 256, 1024
H, DH = 16, 16
NB = T // P
CH = 512
NC = T // CH
BPC = CH // P
KD = D // P
HG = 4
NG = H // HG
W1 = 1024
PARTS = 3
SROWS = 6 * DH
MROW = SROWS
KROWS = SROWS + PARTS
ROPE = 64
LATENT = 64
LN_EPS = 1e-5
EPS = 1e-7
LOWEST = -3.0e38
LAMBDA_INIT = 0.2
DIFF_SCALE = (D // H // 2) ** -0.5
MAX_NORM = 0.99
LAG = 2
SETS = 3
RING2 = 3


class Count:

    def __init__(self, base=0):
        self.base, self.k = base, 0

    def next(self):
        self.k += 1
        return self.base + self.k


class Layer:

    def __init__(self, name, causal, zeros, rope, sem):
        self.name, self.causal, self.zeros, self.rope = name, causal, zeros, rope
        self.units = []
        self.chunk_last = []
        for c in range(NC):
            for sb in range(BPC * (c + 1) if causal else NB):
                self.units.append(("s", c, sb, max(0, sb - BPC * c) * P if causal else 0))
            if zeros:
                self.units += [("e", c, None, 0), ("m", c, None, 0)]
            self.chunk_last.append(len(self.units) - 1)
        self.jobs = []
        for tb in range(NB):
            end = (tb + 1) * P if causal else T
            for i, s0 in enumerate(range(0, end, W1)):
                w = min(W1, end - s0)
                self.jobs += [(j, tb, i, s0, w, causal and s0 + w == end) for j in range(HG)]
        self.tiles = [(tb, i, s0, w) for j, tb, i, s0, w, _ in self.jobs if j == 0] if rope else []
        full = [u for u, x in enumerate(self.units) if x[0] == "s" and x[3] == 0 and x[2] < BPC * x[1]]
        self.added = {full[len(full) * (2 * n + 1) // (2 * KEPT)]: n for n in range(KEPT)} if rope else {}
        self.exps = [u for u, x in enumerate(self.units) if x[0] != "m"]
        self.exp_no = {u: HG * n for n, u in enumerate(self.exps)}
        self.n_exp = HG * len(self.exps)
        self.masked = [u for u, x in enumerate(self.units) if x[0] == "m" or (x[0] == "s" and self.diagonal(u))]
        self.mask_no = {u: HG * n for n, u in enumerate(self.masked)}
        self.n_mask = HG * len(self.masked)
        self.n_unit = len(self.units)
        self.chunk_first = [0] + [u + 1 for u in self.chunk_last[:-1]]
        self.plan()
        ring = lambda steps: sum(s[0] in ("mtr", "otr") or (s[0] == "max" and s[2] == 0) for s in steps)
        self.r_first, self.r_stage = ring(self.first), ring(self.stage)
        assert self.r_first % 2 == 0 and self.r_stage % 2 == 0
        n_first = sum(s[0] == "neg" for s in self.first)
        self.chain_first = n_first * CHAIN_NEG
        self.chain_stage = NC * (CHAIN_NEG + CHAIN_OUT)
        s = lambda x: sem(f"{name}_{x}")
        self.stack_in = s("stack_in")
        self.max_rows_in = s("max_rows_in")
        self.rope_in = s("rope_in")
        self.slot_ready = s("slot_ready")
        self.slot_free = s("slot_free")
        self.neg_ready = s("neg_ready")
        self.score_ready = s("score_ready")
        self.rope_added = s("rope_added")
        self.exp_done = s("exp_done")
        self.mask_done = s("mask_done")
        self.pv_done = s("pv_done")
        self.out_saved = s("out_saved")
        self.v_ready = s("v_ready")
        self.suffix_ready = s("suffix_ready")
        self.chain = s("chain")

    def diagonal(self, u):
        kind, c, sb, off = self.units[u]
        return self.causal and kind == "s" and sb >= BPC * c

    def plan(self):
        width = lambda u: (CH - self.units[u][3]) / CH
        ones, chunk_end = [], {}
        for n, (j, tb, i, s0, w, diag) in enumerate(self.jobs):
            for x in range(0, w, CH):
                ones.append((min(CH, w - x) / CH + (0.2 if x + CH >= w else 0), ("max", n, x // CH)))
            if n + 1 == len(self.jobs) or self.jobs[n + 1][1] // BPC > tb // BPC:
                c = tb // BPC
                ones += [(0.5, ("neg", c)), (2.0, ("mtr", c))]
                chunk_end[c] = sum(x[0] for x in ones)
        total = sum(x[0] for x in ones)
        twos = []
        for u in range(self.n_unit + LAG):
            if u < self.n_unit and self.units[u][0] != "m":
                r = 4 if self.rope else 1
                if u in self.added:
                    r = 0.2
                twos += [(r * width(u), ("score", u, j)) for j in range(HG)]
            if u >= LAG:
                k = u - LAG
                twos.append((4.3 * width(k) if self.units[k][0] == "s" else 6.0, ("pv", k)))
        whole = sum(x[0] for x in twos)
        start, run = {}, 0.0
        for cost, step in twos:
            if step[0] == "score" and step[1] in self.chunk_first and step[2] == 0:
                start[self.chunk_first.index(step[1])] = run / whole
            run += cost
        lead = max(chunk_end[c] - start[c] * total for c in range(NC)) + MARGIN * total
        n_lead, run = 0, 0.0
        while run < lead:
            run += ones[n_lead][0]
            n_lead += 1
        slots = lambda k: sum(s[0] == "mtr" or (s[0] == "max" and s[2] == 0) for _, s in ones[:k])
        while slots(n_lead) % 2 or (ones[n_lead][1][0] == "max" and ones[n_lead][1][2] > 0) or ones[n_lead][1][0] == "mtr":
            n_lead += 1
        self.first = [s + (0,) for _, s in ones[:n_lead]]

        def merge(ahead):
            steps, late, run, given, at = [], [], 0.0, 0.0, 0
            for cost, step in twos:
                while at < len(ahead) and (given < (run + cost / 2) / whole * total or late):
                    if late and not (ahead[at][1][0] == "max" and ahead[at][1][2] > 0):
                        break
                    given += ahead[at][0]
                    steps.append(ahead[at][1])
                    at += 1
                if late and late[0][0] <= run:
                    steps.append(late.pop(0)[1])
                steps.append(step)
                run += cost
                if step[0] == "pv" and step[1] in self.chunk_last:
                    c = self.chunk_last.index(step[1])
                    steps.append(("save", c))
                    late.append((run + 6.0, ("otr", c)))
            steps += [s for _, s in ahead[at:]]
            return steps + [s for _, s in late]
        rest = [(x, s + (0,)) for x, s in ones[n_lead:]]
        self.stage = merge(rest + [(x, s + (1,)) for x, s in ones[:n_lead]])
        self.last = merge(rest)


KEPT = 8
AR_RING = 3
AR_OUT = 4
MARGIN = 0.04
CHAIN_NEG = 4
CHAIN_OUT = 1


def build(nc, a, out):
    nc.disable_value_cache = True
    ctx = ExitStack()
    with ctx:
        def sb(name, shape, dt=F32):
            return ctx.enter_context(nc.sbuf_tensor(name, shape, dt))

        def sem(name):
            return ctx.enter_context(nc.semaphore(name))

        X = sb("X", [P, NB, D])
        HT = sb("HT", [P, NC, KD, CH])
        ON = HT[:].rearrange("p c k t -> p (c k t)").rearrange("p (b d) -> p b d", d=D)
        VALL = sb("VALL", [P, NB, D])
        VG = sb("VG", [P, NB, HG, 2 * DH])
        QF = sb("QF", [P, 2 * HG * T // 2])
        KF = sb("KF", [P, 2 * HG * T // 2])
        QS = QF[:].bitcast(BF16)
        KS = KF[:].bitcast(BF16)
        PF = sb("PF", [P, SETS * HG * CH])
        PT = PF[:].rearrange("p (u j t) -> p u j t", u=SETS, j=HG)
        WA = sb("WA", [P, 6144])
        WB = sb("WB", [P, 4096])
        WC = sb("WC", [P, 3072])
        MASKS = sb("MASKS", [P, 2, W1], BF16)
        JUNK = sb("JUNK", [P, W1], BF16)
        OS = sb("OS", [P, CH])
        IDF = sb("IDF", [P, P])
        IDB = sb("IDB", [P, P], BF16)
        ONE = sb("ONE", [P, 1])
        ONESEL = sb("ONESEL", [P, P], BF16)
        MP = sb("MP", [P, 2, NC, HG, BPC])
        MX = sb("MX", [P, 2, HG, BPC])
        NM = sb("NM", [P, HG, PARTS, BPC], BF16)
        MR = sb("MR", [P, P], BF16)
        RZ = sb("RZ", [P, BPC, HG])
        ST = sb("ST", [P, BPC, 6])
        MV = sb("MV", [P, BPC, 2])
        NW = sb("NW", [P, 8, BPC])
        LAM = sb("LAM", [P, 8])
        QSC = sb("QSC", [P, 1])
        SEL = sb("SEL", [P, 2])
        PS = ctx.enter_context(nc.psum_tensor("PS", [P, 8 * CH], F32))
        bank = lambda b, n=CH, o=0: PS[:, b * CH + o:b * CH + o + n]

        GT = QF[:, 0:4096].rearrange("p (m t) -> p m t", t=CH)
        LNH = QF[:, 4096:6144].rearrange("p (x b d) -> p x b d", x=2, d=D)
        OT = QF[:, 6144:8192].rearrange("p (x k t) -> p x k t", x=2, k=KD)
        TH = PF[:, 0:1024].rearrange("p (x t) -> p x t", x=2)
        TA = PF[:, 1024:2048].rearrange("p (x t) -> p x t", x=2)
        Y2 = PF[:, 2048:3072].rearrange("p (b d) -> p b d", d=D)
        CUM = PF[:, 2048:4096].rearrange("p (x k t) -> p x k t", x=2, k=KD)
        CKV = PF[0:LATENT, 3072:4096].rearrange("p (x t) -> p x t", x=2)
        VH = PF[:, 4096:5120].rearrange("p (k t) -> p k t", k=KD)
        VS = PF[:, 5120:6144].rearrange("p (x t) -> p x t", x=2)
        STG = PF[:, 4096:5632].bitcast(BF16).rearrange("p (x i t) -> p x i t", x=2, i=PARTS)
        RA = QF[0:ROPE, 0:1024].rearrange("p (x t) -> p x t", x=2)
        COS = KF[0:ROPE, 0:T]
        SIN = KF[0:ROPE, T:2 * T]

        WGT = WA[:, 0:2048].rearrange("p (k m) -> p k m", k=KD)
        WUT = WA[:, 2048:4096].rearrange("p (k m) -> p k m", k=KD)
        WDT = WA[:, 4096:6144].rearrange("p (m d) -> p m d", d=D)
        sq = lambda w, o: w[:, o:o + KD * D].rearrange("p (k n) -> p k n", k=KD)
        W0 = {x: sq(WB, 512 * i) for i, x in enumerate(("q", "k", "v", "o"))}
        WL = {x: sq(WB, 2048 + 512 * i) for i, x in enumerate(("q", "k", "v", "o"))}
        WAT = WB[:, 0:1536].rearrange("p (k n) -> p k n", k=KD)
        W1A = {"q": sq(WB, 1536), "k": sq(WB, 2048), "v": WAT[:, :, 2 * D:3 * D], "o": sq(WB, 2560)}
        FG = WC[:, 0:2048].rearrange("p (b j d) -> p b j d", b=NB, j=HG)
        W2 = {"q": sq(WC, 0), "o": sq(WC, 512)}
        WN = sq(WC, 1024)
        SCALE = WC[:, 1536:1792]
        WKV = WC[:, 1792:1920].rearrange("p (k n) -> p k n", k=KD)
        WQR = [WC[:, 1920 + 128 * i:2048 + 128 * i].rearrange("p (k n) -> p k n", k=KD) for i in range(2)]
        WKR = [WC[0:LATENT, 2176 + 64 * i:2240 + 64 * i] for i in range(2)]
        WKUP = WC[0:LATENT, 2304:2560]
        WVUP = WC[0:LATENT, 2560:2816]
        RS = WA[:, 0:5120].bitcast(BF16).rearrange("p (i t) -> p i t", t=T)
        AR = [WA[:, 5120:6144], WC[:, 1792:2816], MASKS[:].rearrange("p i s -> p (i s)").bitcast(F32)]
        ARK = WB[:, 0:KEPT * CH].rearrange("p (n t) -> p n t", n=KEPT)
        ARS = PF[:, 0:AR_OUT * W1].rearrange("p (n s) -> p n s", n=AR_OUT)
        ROPE_Q, ROPE_K = (0, 1, 2), (3, 3, 4)

        NAT = {"gate": QF[:, 0:2048].rearrange("p (m d) -> p m d", d=D),
               "up": QF[:, 2048:4096].rearrange("p (m d) -> p m d", d=D),
               "down": QF[:, 6144:8192].rearrange("p (r m) -> p r m", r=KD)}
        NATL = {x: PF[:, 512 * i:512 * (i + 1)].rearrange("p (e d) -> p e d", e=KD) for i, x in enumerate(("q", "k", "v", "o"))}

        LV = PF[:, 3072:4096].rearrange("p (i d) -> p i d", d=D)

        L0 = Layer("a", True, True, False, sem)
        L1 = Layer("b", False, False, False, sem)
        L2 = Layer("c", True, False, True, sem)
        scr = {(L.name, w): nc.dram_tensor(f"parts_{L.name}_{w}", (PARTS, D, T), BF16, kind="Internal").ap()
               for L in (L0, L1, L2) for w in "qk"}
        scr_ar = nc.dram_tensor("rope_scores", (NB, P, T), F32, kind="Internal").ap()
        scr_r = {w: nc.dram_tensor(f"rope_parts_{w}", (PARTS, ROPE, T), BF16, kind="Internal").ap() for w in "qk"}

        x_in = sem("x_in")
        x_ins = [x_in] + [sem(f"x_in{c}") for c in range(1, NC)]
        w_nat_in = sem("w_nat_in")
        w0_in = sem("w0_in")
        w1_in = sem("w1_in")
        w2_in = sem("w2_in")
        lam_in = sem("lam_in")
        rope_tab_in = sem("rope_tab_in")
        const_ready = sem("const_ready")
        gp = sem("gp")
        d_ready, d_free = sem("d_ready"), sem("d_free")
        a_ready, a_free = sem("a_ready"), sem("a_free")
        tanh_ready = sem("tanh_ready")
        v_used = sem("v_used")
        norm_ready = sem("norm_ready")
        split_ready = sem("split_ready")
        parts_ready = sem("parts_ready")
        parts_out = [sem("parts_out0"), sem("parts_out1")]
        n2_ready, n2_tanh = sem("n2_ready"), sem("n2_tanh")
        lam_dots, lam_exp, lam_done = sem("lam_dots"), sem("lam_exp"), sem("lam_done")
        perm_done = sem("perm_done")
        l1w_free = sem("l1w_free")
        out_dma = sem("out_dma")
        vc = sem("vc")
        x_done = sem("x_done")
        ar_out = [sem(f"ar_out{i}") for i in range(AR_OUT)]
        ar_in = [sem(f"ar_in{i}") for i in range(AR_RING)]

        att = {"A": L0, "B": L1, "C": L2}
        def each(*kinds):
            return [(k, c) for k in kinds for c in range(NC)]
        PROGRAM = [("in", each("in", "p0")), ("A", None), ("", each("o0", "ffn", "lin", "ffn", "p1")), ("B", None),
                   ("", each("o1", "hyp", "p2", "ar")), ("C", None), ("", each("o2", "hypout"))]
        HAS_NORM = {"in", "o0", "ffn", "lin", "o1", "hyp", "o2"}
        OUTW = {"o0": W0["o"], "o1": W1A["o"], "o2": W2["o"], "lin": WL["o"]}
        PROJ = {"p0": (L0, W0, T ** -0.5), "p1": (L1, W1A, None), "p2": (L2, W2, (DH + ROPE) ** -0.5)}
        N_TRANSPOSED = 16

        BANKS = {"in": (0, 0), "p0": (4, 2), "p1": (4, 2), "p2": (8, 3), "o0": (2, 2), "o1": (2, 2), "o2": (2, 2),
                 "ffn": (18, 0), "lin": (6, 2), "hyp": (2, 0), "hypout": (2, 0)}
        ar_banks = lambda c: (BPC * (c + 1), sum(L2.units[u][1] == c for u in L2.added))
        D_COUNT, A_COUNT, HT_AT = {}, {}, []
        d_total, a_total = 0, N_TRANSPOSED
        for kind, steps in PROGRAM:
            if steps is None:
                D_COUNT[kind], A_COUNT[kind] = d_total, a_total
                continue
            pending = False
            for i, (k, c) in enumerate(steps):
                steps[i] = (k, c, d_total, a_total)
                d_banks, a_banks = ar_banks(c) if k == "ar" else BANKS[k]
                d_total += d_banks
                a_total += a_banks
                if pending:
                    a_total += KD
                    HT_AT.append(a_total)
                pending = k in HAS_NORM
        L_KEY = {"a": "A", "b": "B", "c": "C"}

        block = ctx.enter_context(nc.Block())

        STACK_DMAS = 16 * 12
        ROW_DMAS = 16 * HG
        PARTS_ORDER = [("q", 0), ("q", 1), ("k", 0), ("k", 1)]
        N_CONST = 8

        passed = {n: sem(f"passed_{n}") for n in ("sp", "pool", "dve")}

        def settled(name, engine):
            engine.sem_inc(passed[name], 1)

        @block.sync
        def _(sp):
            xv = a["x"].rearrange("o (b p) d -> p (o b) d", p=P)
            for c in range(NC):
                sp.dma_start(X[:, BPC * c:BPC * (c + 1), :], xv[:, BPC * c:BPC * (c + 1), :]).then_inc(x_ins[c], 16)
            km = lambda w: w.rearrange("(k p) n -> p k n", p=P)
            for x in ("q", "k", "v", "o"):
                sp.dma_start(W0[x], km(a["L0a_" + x])).then_inc(w0_in, 16)
            sp.dma_start(NAT["gate"], km(a["gate"])).then_inc(w_nat_in, 16)
            sp.dma_start(NAT["up"], km(a["up"])).then_inc(w_nat_in, 16)
            sp.dma_start(NAT["down"], km(a["down"])).then_inc(w_nat_in, 16)
            for x in ("q", "k", "v", "o"):
                sp.dma_start(NATL[x], km(a["L0b_" + x])).then_inc(w_nat_in, 16)
            for i, x in enumerate(("lq1", "lk1", "lq2", "lk2")):
                sp.dma_start(LV[:, i, :], a[x].partition_broadcast(P)).then_inc(lam_in, 16)
            sp.dma_start(SEL[:], a["rows"]).then_inc(lam_in, 16)
            parts = Count()

            def parts_to_dram(dst, rows):
                n = parts.next() - 1
                sp.wait_ge(parts_ready, n + 1)
                sp.dma_start(dst, STG[0:rows, n % 2, :, :]).then_inc(parts_out[n % 2], 16)

            def project(kind, c):
                L = PROJ[kind][0]
                t = slice(c * CH, (c + 1) * CH)
                for w, e in PARTS_ORDER:
                    parts_to_dram(scr[L.name, w][:, e * P:(e + 1) * P, t].rearrange("i f t -> f i t"), P)
                if L.rope:
                    for w in "qk":
                        parts_to_dram(scr_r[w][:, :, t].rearrange("i f t -> f i t"), ROPE)

            def load_stacks(L, group, parity):
                def rows(w, i):
                    x = scr[L.name, w][i, bass.ds(group * (HG * DH), HG * DH), :]
                    return x.rearrange("(j d) t -> d j t", d=DH)
                for dst, w, order in ((QS, "q", (0, 0, 0, 1, 1, 2)), (KS, "k", (0, 1, 2, 0, 1, 0))):
                    for n, i in enumerate(order):
                        x = dst[n * DH:(n + 1) * DH, bass.ds(parity * (HG * T), HG * T)]
                        sp.dma_start(x.rearrange("d (j t) -> d j t", j=HG), rows(w, i)).then_inc(L.stack_in, 16)

            def max_rows(L, parity, c, ring):
                sp.wait_ge(L.slot_free, ring)
                settled("sp", sp)
                n = PARTS * BPC
                for j in range(HG):
                    dst = QS[MROW:KROWS, bass.ds(parity * (HG * T) + (j * T + c * CH), CH)]
                    sp.dma_start(dst.rearrange("i (n t) -> i n t", t=P), MR[j * n:(j + 1) * n, :]).then_inc(L.max_rows_in, 16)

            def ar_load(L, n):
                tb, i, s0, w = L.tiles[n]
                sp.dma_start(AR[n % AR_RING][:, 0:w], scr_ar[tb, :, s0:s0 + w]).then_inc(ar_in[n % AR_RING], 16)

            def rows_of(L, steps, group, base, more=True):
                ring = 0
                for step in steps:
                    if step[0] in ("mtr", "otr") or (step[0] == "max" and step[2] == 0):
                        ring += 1
                    if step[0] == "mtr":
                        max_rows(L, (group + step[2]) & 1, step[1], base + ring)
                    if L.rope and step[0] == "max" and L.jobs[step[1]][0] == HG - 1 and (step[2] + 1) * CH >= L.jobs[step[1]][4]:
                        n = step[1] // HG + AR_RING
                        if more or n < len(L.tiles):
                            sp.wait_ge(L.slot_free, base + ring)
                            settled("sp", sp)
                            ar_load(L, n % len(L.tiles))

            def parts_in_dram():
                for i in range(2):
                    sp.wait_ge(parts_out[i], 16 * ((parts.k + 1 - i) // 2))

            def rope_tiles(L, c, d0):
                if c == 0:
                    parts_in_dram()
                    rq, rk = scr_r["q"], scr_r["k"]
                    for i, (top, bottom) in enumerate(((rq[0], rq[0]), (rq[1], rq[1]), (rq[0], rq[2]), (rk[0], rk[1]), (rk[2], rk[0]))):
                        sp.dma_start(RS[0:ROPE, i, :], top).then_inc(L.rope_in, 16)
                        sp.dma_start(RS[ROPE:P, i, :], bottom).then_inc(L.rope_in, 16)
                    load_stacks(L, 0, 0)
                for n, (tb, i, s0, w) in enumerate(L.tiles):
                    if tb // BPC == c:
                        d0 += (w + CH - 1) // CH
                        sp.wait_ge(d_free, d0)
                        sp.dma_start(scr_ar[tb, :, s0:s0 + w], ARS[:, n % AR_OUT, 0:w]).then_inc(ar_out[n % AR_OUT], 16)

            def attention(L):
                if not L.rope:
                    parts_in_dram()
                    load_stacks(L, 0, 0)
                sp.wait_ge(L.stack_in, STACK_DMAS)
                load_stacks(L, 1, 1)
                if L.rope:
                    for i in range(AR_OUT):
                        sp.wait_ge(ar_out[i], 16 * len(L.tiles[i::AR_OUT]))
                    for n in range(AR_RING):
                        ar_load(L, n)
                rows_of(L, L.first, 0, 0)
                with sp.Fori(0, NG - 2) as g:
                    rows_of(L, L.stage, g, g * L.r_stage + L.r_first)
                    sp.wait_ge(L.pv_done, (g + 1) * L.n_unit)
                    sp.wait_ge(L.stack_in, (g + 2) * STACK_DMAS)
                    settled("sp", sp)
                    load_stacks(L, g + 2, g & 1)
                g = NG - 2
                rows_of(L, L.stage, g, g * L.r_stage + L.r_first)
                rows_of(L, L.last, g + 1, (g + 1) * L.r_stage + L.r_first, more=False)

            for kind, steps in PROGRAM:
                if steps is None:
                    attention(att[kind])
                    if kind == "A":
                        sp.wait_ge(L0.pv_done, NG * L0.n_unit)
                        for dst, src in ((W2["q"], km(a["L1b_q"])), (W2["o"], km(a["L1b_o"])), (WN, km(a["hyp_w"])),
                                         (SCALE, a["hyp_scale"].partition_broadcast(P)),
                                         (WKV, km(a["kv"])), (WKUP, a["kup"]), (WVUP, a["vup"])):
                            sp.dma_start(dst, src).then_inc(w2_in, 16)
                        half = ROPE // 2
                        for i in range(2):
                            for h in range(2):
                                o = half * (h if i == 0 else 1 - h)
                                dst = slice(o, o + half)
                                src = slice(half * h, half * (h + 1))
                                sp.dma_start(WQR[i][:, :, dst], km(a["qr"])[:, :, src]).then_inc(w2_in, 16)
                                sp.dma_start(WKR[i][:, dst], a["kr"][:, src]).then_inc(w2_in, 16)
                    continue
                for k, c, d0, a0 in steps:
                    if (k, c) == ("p1", 0):
                        sp.wait_ge(l1w_free, 1)
                        sp.dma_start(WAT, km(a["attn"])).then_inc(w1_in, 16)
                        sp.dma_start(W1A["o"], km(a["proj"])).then_inc(w1_in, 16)
                    if (k, c) == ("p2", 0):
                        sp.wait_ge(L1.pv_done, NG * L1.n_unit)
                        sp.dma_start(COS, a["cos"]).then_inc(rope_tab_in, 16)
                        sp.dma_start(SIN, a["sin"]).then_inc(rope_tab_in, 16)
                    if k in PROJ:
                        project(k, c)
                    if k == "ar":
                        rope_tiles(L2, c, d0)
                    if k == "hypout":
                        sp.wait_ge(x_done, c + 1)
                        ov = out.rearrange("o (b p) d -> p (o b) d", p=P)
                        sp.dma_start(ov[:, BPC * c:BPC * (c + 1), :], X[:, BPC * c:BPC * (c + 1), :]).then_inc(out_dma, 16)
            sp.wait_ge(out_dma, 16 * NC)

        @block.gpsimd
        def _(pool):
            g_ = nc.gpsimd
            order = Count()

            def link(ins):
                ins.then_inc(gp, 1)
                pool.wait_ge(gp, order.next())

            consts = Count()

            def constant(ins):
                ins.then_inc(const_ready, 1)
                pool.wait_ge(const_ready, consts.next())

            link(g_.memset(IDF[:], 0.0))
            link(g_.affine_select(out=IDF[:], in_=IDF[:], compare_op=ALU.not_equal, fill=1.0, base=0,
                                  pattern=[[-1, P]], channel_multiplier=1))
            constant(g_.tensor_copy(IDB[:], IDF[:]))
            link(g_.memset(MASKS[:, 0, :], 1.0))
            constant(g_.affine_select(out=MASKS[:, 0, W1 - P:W1], in_=MASKS[:, 0, W1 - P:W1], compare_op=ALU.is_ge, fill=0.0,
                                      base=0, pattern=[[-1, P]], channel_multiplier=1))
            constant(g_.tensor_scalar(MASKS[:, 1, :], MASKS[:, 0, :], -1.0, -LOWEST, ALU.add, ALU.mult))
            link(g_.memset(ONESEL[:], 0.0))
            constant(g_.memset(ONESEL[MROW:KROWS, :], 1.0))
            constant(g_.memset(ONE[:], 1.0))
            constant(g_.memset(VG[:, :, :, DH:2 * DH], 1.0))
            constant(g_.memset(FG[:, NB - 1, :, :], 0.0))
            constant(g_.memset(KS[MROW:KROWS, :], 1.0))
            parts = Count()

            def split(rows):
                n = parts.next() - 1
                pool.wait_ge(split_ready, n + 1)
                link(g_.tensor_copy(STG[0:rows, n % 2, 1, :], TA[0:rows, n % 2, :]))
                g_.tensor_tensor(STG[0:rows, n % 2, 2, :], TA[0:rows, n % 2, :], STG[0:rows, n % 2, 1, :], ALU.subtract)\
                    .then_inc(parts_ready, 1)

            def stage(L, g):
                chain = Count(g * (NB - 1))
                quarter = NB // 4
                for i in range(4):
                    b = slice(quarter * i, quarter * (i + 1))
                    src = VALL[:, b, bass.ds(g * (HG * DH), HG * DH)].rearrange("p b (j d) -> p b j d", d=DH)
                    g_.tensor_copy(VG[:, b, :, 0:DH], src).then_inc(L.v_ready, 1)
                for step in L.stage:
                    if step[0] != "score":
                        continue
                    _, u, j = step
                    kind, c, sb_, off = L.units[u]
                    if L.diagonal(u):
                        tile = PT[:, u % SETS, j, off:off + P]
                        pool.wait_ge(L.exp_done, g * L.n_exp + (L.exp_no[u] + j + 1))
                        settled("pool", pool)
                        g_.affine_select(out=tile, in_=tile, compare_op=ALU.is_ge, fill=0.0, base=0,
                                         pattern=[[1, P]], channel_multiplier=-1).then_inc(L.mask_done, 1)
                    if kind == "e":
                        if c == 0 and j == 0:
                            pool.wait_ge(L.v_ready, g * 4 + 4)
                            for b in range(NB - 2, -1, -1):
                                g_.tensor_tensor(FG[:, b], FG[:, b + 1], VG[:, b + 1], ALU.add).then_inc(L.suffix_ready, 1)
                                pool.wait_ge(L.suffix_ready, chain.next())
                        m = u + 1
                        if m >= SETS and j == 0:
                            pool.wait_ge(L.pv_done, g * L.n_unit + (m - SETS + 1))
                        pool.wait_ge(L.exp_done, g * L.n_exp + (L.exp_no[u] + j + 1))
                        settled("pool", pool)
                        v = lambda s: PT[:, s, j, :].rearrange("p (b t) -> p b t", t=P)
                        g_.affine_select(out=v(m % SETS), in_=v(u % SETS), compare_op=ALU.is_ge, fill=0.0, base=-1,
                                         pattern=[[0, BPC], [-1, P]], channel_multiplier=1).then_inc(L.mask_done, 1)
                pool.wait_ge(L.pv_done, (g + 1) * L.n_unit)

            for kind, steps in PROGRAM:
                if steps is None:
                    L = att[kind]
                    pool.wait_ge(a_free, A_COUNT[kind])
                    with pool.Fori(0, NG) as g:
                        stage(L, g)
                    continue
                for k, c, d0, a0 in steps:
                    if (k, c) == ("p1", 0):
                        pool.wait_ge(w1_in, 32)
                        half = D // 2
                        for n, w in enumerate(("q", "k")):
                            for i in range(2):
                                dst = W1A[w].rearrange("p k (h i d) -> p k h i d", i=2, d=DH // 2)[:, :, :, i, :]
                                o = (2 * i + n) * half
                                src = WAT[:, :, o:o + half].rearrange("p k (h d) -> p k h d", d=DH // 2)
                                for kk in range(KD):
                                    g_.tensor_copy(dst[:, kk], src[:, kk]).then_inc(perm_done, 1)
                    if k in PROJ:
                        for w, e in PARTS_ORDER:
                            split(P)
                        if PROJ[k][0].rope:
                            for w in "qk":
                                split(ROPE)

        @block.tensor
        def _(pe):
            mm = nc.tensor.matmul
            nd, na = Count(), Count()

            def d_bank():
                n = nd.next() - 1
                if n >= 4:
                    pe.wait_ge(d_free, n - 3)
                return n % 4

            def a_bank():
                n = na.next() - 1
                if n >= 4:
                    pe.wait_ge(a_free, n - 3)
                return 4 + n % 4

            def over_k(dst, left, right, n=KD):
                for k in range(n):
                    ins = mm(dst, left(k), right(k), start=k == 0, stop=k == n - 1)
                return ins

            def rope_product(dst, left, l0, m, right, r0, n, start=True):
                for r in range(3):
                    ins = mm(dst, RS[:, left[r], l0:l0 + m], RS[:, right[r], r0:r0 + n], start=start and r == 0, stop=r == 2)
                return ins

            def weight_transposes():
                pe.wait_ge(w_nat_in, 16 * 7)
                for w in ("gate", "up"):
                    for k in range(KD):
                        for m0 in range(0, HID // P, 4):
                            b = a_bank()
                            for i in range(4):
                                ins = nc.tensor.transpose(bank(b, P, i * P), NAT[w][:, m0 + i, k * P:(k + 1) * P], IDF[:])
                            ins.then_inc(a_ready, 1)
                for m in range(0, HID // P, 2):
                    b = a_bank()
                    for i in range(4):
                        ins = nc.tensor.transpose(bank(b, P, i * P), NAT["down"][:, i % 2, (m + i // 2) * P:(m + i // 2 + 1) * P], IDF[:])
                    ins.then_inc(a_ready, 1)
                for w in ("q", "k", "v", "o"):
                    b = a_bank()
                    for i in range(4):
                        ins = nc.tensor.transpose(bank(b, P, i * P), NATL[w][:, i % 2, (i // 2) * P:(i // 2 + 1) * P], IDF[:])
                    ins.then_inc(a_ready, 1)

            def norm_transposes(n):
                pe.wait_ge(norm_ready, n + 1)
                for k in range(KD):
                    b = a_bank()
                    for i in range(BPC):
                        ins = nc.tensor.transpose(bank(b, P, i * P), LNH[:, n % 2, i, k * P:(k + 1) * P], IDF[:])
                    ins.then_inc(a_ready, 1)

            def token_major(left, right, n_k, ring, ready, wide=2):
                for h in range(BPC // 2):
                    b = ring()
                    for i in range(2):
                        ins = over_k(bank(b, D, i * D), lambda k: left(k, 2 * h + i), right, n_k)
                    ins.then_inc(ready, 1)

            def main(k, c, d0, a0):
                ht = lambda kk: HT[:, c, kk, :]
                blk = lambda i: slice(i * P, (i + 1) * P)
                if k not in ("o0", "o1", "o2"):
                    pe.wait_ge(a_free, HT_AT[NC * (norms.k // NC - 1) + c])
                if k in ("p0", "p1"):
                    L, W, _ = PROJ[k]
                    if (k, c) == ("p0", 0):
                        pe.wait_ge(w0_in, 16 * 4)
                    if (k, c) == ("p1", 0):
                        pe.wait_ge(perm_done, 4 * KD)
                    for w, e in PARTS_ORDER:
                        b = d_bank()
                        over_k(bank(b), lambda kk: W[w][:, kk, e * P:(e + 1) * P], ht).then_inc(d_ready, 1)
                    token_major(lambda kk, i: HT[:, c, kk, blk(i)], lambda kk: W["v"][:, kk, :], KD, a_bank, a_ready)
                if k == "p2":
                    L, W, _ = PROJ[k]
                    b = a_bank()
                    over_k(bank(b)[0:LATENT], lambda kk: WKV[:, kk, :], ht).then_inc(a_ready, 1)
                    latent_done = na.k
                    for e in range(KD):
                        b = d_bank()
                        over_k(bank(b), lambda kk: W["q"][:, kk, e * P:(e + 1) * P], ht).then_inc(d_ready, 1)
                    pe.wait_ge(a_free, latent_done)
                    for e in range(KD):
                        b = d_bank()
                        mm(bank(b), WKUP[:, e * P:(e + 1) * P], CKV[:, c % 2, :], start=True, stop=True).then_inc(d_ready, 1)
                    for i in range(2):
                        b = d_bank()
                        over_k(bank(b)[0:ROPE], lambda kk: WQR[i][:, kk, :], ht).then_inc(d_ready, 1)
                    for i in range(2):
                        b = d_bank()
                        mm(bank(b)[0:ROPE], WKR[i], CKV[:, c % 2, :], start=True, stop=True).then_inc(d_ready, 1)
                    token_major(lambda kk, i: CKV[:, c % 2, blk(i)], lambda kk: WVUP, 1, a_bank, a_ready)
                if k in ("o0", "o1", "o2"):
                    for kk in range(KD):
                        b = a_bank()
                        for i in range(BPC):
                            ins = nc.tensor.transpose(bank(b, P, i * P), ON[:, BPC * c + i, kk * P:(kk + 1) * P], IDF[:])
                        ins.then_inc(a_ready, 1)
                    pe.wait_ge(a_free, na.k)
                    token_major(lambda kk, i: OT[:, c % 2, kk, blk(i)], lambda kk: OUTW[k][:, kk, :], KD, d_bank, d_ready)
                if k == "ffn":
                    for m in range(HID // P):
                        for W in (WGT, WUT):
                            b = d_bank()
                            over_k(bank(b), lambda kk: W[:, kk, m * P:(m + 1) * P], ht).then_inc(d_ready, 1)
                    for h in range(BPC // 2):
                        b = d_bank()
                        for i in range(2):
                            for m in range(HID // P):
                                if h == 0 and i == 0:
                                    pe.wait_ge(d_free, d0 + 2 * m + 2)
                                ins = mm(bank(b, D, i * D), GT[:, m, blk(2 * h + i)], WDT[:, m, :], start=m == 0, stop=m == HID // P - 1)
                        ins.then_inc(d_ready, 1)
                if k == "lin":
                    for e in range(KD):
                        for w in ("v", "k", "q"):
                            b, ready = (a_bank(), a_ready) if w == "v" else (d_bank(), d_ready)
                            over_k(bank(b), lambda kk: WL[w][:, kk, e * P:(e + 1) * P], ht).then_inc(ready, 1)
                    pe.wait_ge(d_free, d0 + 2 * KD)
                    token_major(lambda kk, i: VH[:, kk, blk(i)], lambda kk: OUTW[k][:, kk, :], KD, d_bank, d_ready)
                if k == "ar":
                    if c == 0:
                        pe.wait_ge(L2.rope_in, 16 * 10)
                    for tb, i, s0, w in L2.tiles:
                        if tb // BPC != c:
                            continue
                        for x in range(s0, s0 + w, CH):
                            b, width = d_bank(), min(CH, s0 + w - x)
                            rope_product(bank(b, width), ROPE_Q, tb * P, P, ROPE_K, x, width).then_inc(d_ready, 1)
                    for u in L2.added:
                        if L2.units[u][1] == c:
                            rope_product(bank(a_bank()), ROPE_K, L2.units[u][2] * P, P, ROPE_Q, c * CH, CH).then_inc(a_ready, 1)
                if k in ("hyp", "hypout"):
                    token_major(lambda kk, i: HT[:, c, kk, blk(i)], lambda kk: WN[:, kk, :], KD, d_bank, d_ready)

            def max_piece(L, n, x, slot, off):
                j, tb, i, s0, w, diag = L.jobs[n]
                s0, width = s0 + x * CH, min(CH, w - x * CH)
                ins = mm(bank(slot + x, width), QS[0:SROWS, off + j * T + tb * P:off + j * T + (tb + 1) * P],
                         KS[0:SROWS, off + j * T + s0:off + j * T + s0 + width], start=True, stop=True)
                if (x + 1) * CH >= w:
                    ins.then_inc(L.slot_ready, 1)

            def attention_steps(L, steps, group, base):
                ring = Count(base)
                for step in steps:
                    if step[0] in ("mtr", "otr") or (step[0] == "max" and step[2] == 0):
                        n = ring.next()
                        if n > 2:
                            pe.wait_ge(L.slot_free, n - 2)
                        slot = (n - 1) % 2 * 2
                    if step[0] == "max":
                        _, job, x, nxt = step
                        if job == 0 and x == 0:
                            pe.wait_ge(L.stack_in, (group + nxt + 1) * STACK_DMAS)
                        max_piece(L, job, x, slot, (group + nxt) % 2 * HG * T)
                    if step[0] == "mtr":
                        pe.wait_ge(L.neg_ready, (group + step[2]) * NC + step[1] + 1)
                        dst = bank(slot).bitcast(BF16)[0:PARTS * HG * BPC, 0:P]
                        nc.tensor.transpose(dst, NM[:].rearrange("p j i n -> p (j i n)"), IDB[:]).then_inc(L.slot_ready, 1)
                    if step[0] == "otr":
                        pe.wait_ge(L.out_saved, group * NC + (step[1] + 1))
                        for i in range(BPC):
                            ins = nc.tensor.transpose(bank(slot, P, i * P), OS[:, i * P:(i + 1) * P], IDF[:])
                        ins.then_inc(L.slot_ready, 1)
                    if step[0] == "score":
                        _, u, j = step
                        kind, c, sb_, off = L.units[u]
                        off2 = group % 2 * HG * T + j * T
                        if u in L.chunk_first and j == 0:
                            pe.wait_ge(L.max_rows_in, (group * NC + c + 1) * ROW_DMAS)
                        n = L.exp_no[u] + j
                        if n >= RING2:
                            pe.wait_ge(L.exp_done, group * L.n_exp + (n - RING2 + 1))
                        q = QS[0:KROWS, off2 + c * CH + off:off2 + (c + 1) * CH]
                        dst = bank(4 + n % RING2, CH - off)
                        if kind == "e":
                            ins = mm(dst, ONESEL[0:KROWS, :], q, start=True, stop=True)
                        else:
                            k = KS[0:KROWS, off2 + sb_ * P:off2 + (sb_ + 1) * P]
                            rope = L.rope and u not in L.added
                            ins = mm(dst, k, q, start=True, stop=not rope)
                            if rope:
                                ins = rope_product(dst, ROPE_K, sb_ * P, P, ROPE_Q, c * CH + off, CH - off, start=False)
                        ins.then_inc(L.score_ready, 1)
                    if step[0] == "pv":
                        u = step[1]
                        kind, c, sb_, off = L.units[u]
                        first, last = u == 0 or u - 1 in L.chunk_last, u in L.chunk_last
                        if first and c == 0:
                            pe.wait_ge(L.v_ready, group * 4 + 1)
                        if kind == "s" and sb_ % 4 == 0 and c == (sb_ // 4 if L.causal else 0):
                            pe.wait_ge(L.v_ready, group * 4 + (sb_ // 4 + 1))
                        if kind == "e" and c == 0:
                            pe.wait_ge(L.suffix_ready, (group + 1) * (NB - 1))
                        if first and c > 0:
                            pe.wait_ge(L.out_saved, group * NC + c)
                        if kind == "m" or L.diagonal(u):
                            pe.wait_ge(L.mask_done, group * L.n_mask + (L.mask_no[u] + HG))
                        else:
                            pe.wait_ge(L.exp_done, group * L.n_exp + (L.exp_no[u] + HG))
                        pieces = [(off, CH)] if kind == "s" else [(i * P, (i + 1) * P) for i in range(BPC)]
                        for i, (t0, t1) in enumerate(pieces):
                            for j in range(HG):
                                V = VG[:, sb_, j, :] if kind == "s" else (FG if kind == "e" else VG)[:, BPC * c + i, j, :]
                                ins = mm(PS[32 * j:32 * j + 2 * DH, 7 * CH + t0:7 * CH + t1], V, PT[:, u % SETS, j, t0:t1],
                                         start=first, stop=last, tile_position=(0, 32 * j), skip_group_check=True)
                        ins.then_inc(L.pv_done, 1)

            def attention(L):
                pe.wait_ge(d_free, D_COUNT[L_KEY[L.name]])
                pe.wait_ge(a_free, A_COUNT[L_KEY[L.name]])
                pe.wait_ge(const_ready, N_CONST)
                attention_steps(L, L.first, 0, 0)
                for g in range(NG - 1):
                    attention_steps(L, L.stage, g, g * L.r_stage + L.r_first)
                g = NG - 1
                attention_steps(L, L.last, g, g * L.r_stage + L.r_first)
                pe.wait_ge(L.slot_free, NG * L.r_stage)
                pe.wait_ge(L.out_saved, NG * NC)

            pe.wait_ge(const_ready, 1)
            weight_transposes()
            norms = Count()
            for kind, steps in PROGRAM:
                if steps is None:
                    attention(att[kind])
                    continue
                pending = None
                if kind == "" and steps[0][0] == "o1":
                    pe.wait_ge(w2_in, 16 * 15)
                for k, c, d0, a0 in steps:
                    if k != "in":
                        main(k, c, d0, a0)
                    if pending is not None:
                        norm_transposes(pending)
                    pending = norms.next() - 1 if k in HAS_NORM else None
                assert pending is None
            assert (nd.k, na.k) == (d_total, a_total)

        @block.scalar
        def _(act):
            sc = nc.scalar
            na, nd = Count(), Count()
            c_tanh, c_v, c_n2 = Count(), Count(), Count()

            def take(dst, src_of, scale=1.0, rows=P):
                n = na.next() - 1
                act.wait_ge(a_ready, n + 1)
                src = src_of(4 + n % 4)
                if scale == 1.0:
                    return sc.copy(dst, src)
                return sc.mul(dst, src, scale)

            def weight_copies():
                for w in (WGT, WUT):
                    for k in range(KD):
                        for m in range(2):
                            take(w[:, k, m * CH:(m + 1) * CH], bank).then_inc(a_free, 1)
                for m in range(4):
                    take(WDT[:, 2 * m:2 * m + 2, :], lambda b: bank(b).rearrange("p (m d) -> p m d", d=D)).then_inc(a_free, 1)
                for w in ("q", "k", "v", "o"):
                    take(WL[w], lambda b: bank(b).rearrange("p (k e) -> p k e", k=KD)).then_inc(a_free, 1)

            def main(k, c, d0, a0):
                if k == "lin":
                    for e in range(KD):
                        n = c_v.next()
                        if n > 2:
                            act.wait_ge(v_used, n - 2)
                        take(VS[:, n % 2, :], bank).then_inc(a_free, 1)
                if k in ("o0", "o1", "o2"):
                    for kk in range(KD):
                        take(OT[:, c % 2, kk, :], bank, 1.0 - LAMBDA_INIT if k == "o1" else 1.0).then_inc(a_free, 1)
                if k == "p2":
                    take(CKV[:, c % 2, :], lambda b: bank(b)[0:LATENT]).then_inc(a_free, 1)
                if k in ("p0", "p1", "p2"):
                    for h in range(2):
                        b0 = BPC * c + 2 * h
                        take(VALL[:, b0:b0 + 2, :], lambda b: bank(b).rearrange("p (b d) -> p b d", d=D)).then_inc(a_free, 1)
                if k == "ffn":
                    for m in range(HID // P):
                        n = c_tanh.next()
                        act.wait_ge(d_ready, d0 + 2 * m + 1)
                        if n > 2:
                            act.wait_ge(d_free, gates[n - 3])
                        gates.append(d0 + 2 * m + 1)
                        sc.activation(TH[:, n % 2, :], bank((d0 + 2 * m) % 4), ACT.Tanh, scale=0.5).then_inc(tanh_ready, 1)
                if k == "ar":
                    for u, n in L2.added.items():
                        if L2.units[u][1] == c:
                            take(ARK[:, n, :], bank).then_inc(a_free, 1)
                if k in ("hyp", "hypout"):
                    act.wait_ge(n2_ready, c_n2.next())
                    sc.activation(NW[:, 5, :], NW[:, 4, :], ACT.Tanh).then_inc(n2_tanh, 1)

            def norm_copies(c):
                for k in range(KD):
                    take(HT[:, c, k, :], bank).then_inc(a_free, 1)

            gates = []
            weight_copies()
            act.wait_ge(lam_dots, 1)
            sc.activation(LAM[:, 2:4], LAM[:, 4:6], ACT.Exp).then_inc(lam_exp, 1)
            for kind, steps in PROGRAM:
                if steps is None:
                    L = att[kind]
                    if L.rope:
                        for i in range(AR_OUT):
                            act.wait_ge(ar_out[i], 16 * len(L.tiles[i::AR_OUT]))
                    with act.Fori(0, NG) as g:
                        for u in L.exps:
                            for j in range(HG):
                                n = L.exp_no[u] + j
                                off = L.units[u][3]
                                if u in L.added:
                                    act.wait_ge(L.rope_added, g * (HG * len(L.added)) + (HG * L.added[u] + j + 1))
                                else:
                                    act.wait_ge(L.score_ready, g * L.n_exp + (n + 1))
                                if j == 0 and u >= SETS:
                                    act.wait_ge(L.pv_done, g * L.n_unit + (u - SETS + 1))
                                if j == 0 and u >= SETS and L.units[u - SETS][0] == "e":
                                    act.wait_ge(L.mask_done, g * L.n_mask + (L.mask_no[u - SETS + 1] + HG))
                                sc.activation(PT[:, u % SETS, j, off:CH], bank(4 + n % RING2, CH - off), ACT.Exp).then_inc(L.exp_done, 1)
                    continue
                pending = None
                for k, c, d0, a0 in steps:
                    main(k, c, d0, a0)
                    if pending is not None:
                        norm_copies(pending)
                    pending = c if k in HAS_NORM else None

        @block.vector
        def _(dve):
            v = nc.vector
            order = Count()
            nd = Count()
            c_tanh, c_parts, c_n2 = Count(), Count(), Count()

            def link(*ins):
                for i in ins:
                    i.then_inc(vc, 1)
                    order.k += 1
                dve.wait_ge(vc, order.k)

            def bank_in():
                n = nd.next() - 1
                dve.wait_ge(d_ready, n + 1)
                return n % 4

            def rsqrt(dst, src, tmp):
                link(v.tensor_scalar(dst.bitcast(I32), src.bitcast(I32), 1, None, ALU.logical_shift_right))
                link(v.tensor_scalar(dst.bitcast(I32), dst.bitcast(I32), -1.0, float(0x5F3759DF), ALU.mult, ALU.add))
                for _ in range(4):
                    link(v.scalar_tensor_tensor(out=tmp, in0=dst, scalar=-0.5, in1=src, op0=ALU.mult, op1=ALU.mult))
                    link(v.tensor_tensor(tmp, tmp, dst, ALU.mult))
                    link(v.scalar_tensor_tensor(out=dst, in0=tmp, scalar=1.5, in1=dst, op0=ALU.add, op1=ALU.mult))

            norms = Count()

            def norm(c):
                n = norms.next() - 1
                link(*[v.bn_stats(ST[:, i, :], X[:, BPC * c + i, :]) for i in range(BPC)])
                link(*[v.bn_aggr(MV[:, i, :], ST[:, i, :]) for i in range(BPC)])
                link(v.tensor_scalar(NW[:, 0, :], MV[:, :, 1], LN_EPS, None, ALU.add))
                rsqrt(NW[:, 1, :], NW[:, 0, :], NW[:, 2, :])
                if n >= 2:
                    dve.wait_ge(a_free, HT_AT[n - 2])
                for i in range(BPC):
                    ins = v.tensor_scalar(LNH[:, n % 2, i, :], X[:, BPC * c + i, :], MV[:, i, 0:1], NW[:, 1, i:i + 1],
                                          ALU.subtract, ALU.mult)
                ins.then_inc(norm_ready, 1)

            def residual(c):
                for h in range(2):
                    b = bank_in()
                    x = X[:, BPC * c + 2 * h:BPC * c + 2 * h + 2, :]
                    ins = v.tensor_tensor(x, bank(b).rearrange("p (b d) -> p b d", d=D), x, ALU.add)
                    ins.then_inc(d_free, 1)
                    order_x(ins)

            def order_x(ins):
                dve.wait_ge(d_free, nd.k)

            def parts(rows, n):
                if n >= 2:
                    dve.wait_ge(parts_out[n % 2], 16 * (n // 2))
                link(v.tensor_copy(STG[0:rows, n % 2, 0, :], TH[0:rows, n % 2, :]))
                v.tensor_tensor(TA[0:rows, n % 2, :], TH[0:rows, n % 2, :], STG[0:rows, n % 2, 0, :], ALU.subtract)\
                    .then_inc(split_ready, 1)

            def main(k, c, d0, a0):
                if k in PROJ:
                    L, W, scale = PROJ[k]
                    for w, e in PARTS_ORDER:
                        b = bank_in()
                        n = c_parts.next() - 1
                        if w == "q" and scale is None:
                            if (c, e) == (0, 0):
                                dve.wait_ge(lam_done, 1)
                            ins = v.tensor_scalar(TH[:, n % 2, :], bank(b), QSC[:], None, ALU.mult)
                        elif w == "q":
                            ins = v.tensor_scalar(TH[:, n % 2, :], bank(b), float(scale), None, ALU.mult)
                        else:
                            ins = v.tensor_copy(TH[:, n % 2, :], bank(b))
                        ins.then_inc(d_free, 1)
                        dve.wait_ge(d_free, nd.k)
                        parts(P, n)
                    if L.rope:
                        if c == 0:
                            dve.wait_ge(rope_tab_in, 32)
                        t = slice(c * CH, (c + 1) * CH)
                        for w in "qk":
                            s = float(scale) if w == "q" else 1.0
                            n = c_parts.next() - 1
                            for i, tab in enumerate((COS, SIN)):
                                b = bank_in()
                                v.scalar_tensor_tensor(out=RA[:, i, :], in0=bank(b)[0:ROPE], scalar=s, in1=tab[:, t],
                                                       op0=ALU.mult, op1=ALU.mult).then_inc(d_free, 1)
                            dve.wait_ge(d_free, nd.k)
                            link(v.tensor_tensor(TH[0:ROPE, n % 2, :], RA[:, 0, :], RA[:, 1, :], ALU.add))
                            parts(ROPE, n)
                if k in ("o0", "o1", "o2"):
                    residual(c)
                if k == "ffn":
                    for m in range(HID // P):
                        n = c_tanh.next()
                        bg = bank_in()
                        dve.wait_ge(tanh_ready, n)
                        v.scalar_tensor_tensor(out=TA[:, n % 2, :], in0=TH[:, n % 2, :], scalar=1.0, in1=bank(bg),
                                               op0=ALU.add, op1=ALU.mult).then_inc(d_free, 1)
                        dve.wait_ge(d_free, nd.k)
                        bu = bank_in()
                        v.scalar_tensor_tensor(out=GT[:, m, :], in0=TA[:, n % 2, :], scalar=0.5, in1=bank(bu),
                                               op0=ALU.mult, op1=ALU.mult).then_inc(d_free, 1)
                    residual(c)
                if k == "lin":
                    for e in range(KD):
                        b = bank_in()
                        n = KD * c + e + 1
                        dve.wait_ge(a_free, a0 + e + 1)
                        v.tensor_tensor(TA[:, n % 2, :], bank(b), VS[:, n % 2, :], ALU.mult).then_inc(d_free, 1)
                        dve.wait_ge(d_free, nd.k)
                        init = 0.0 if c == 0 else CUM[:, (c + 1) % 2, e, CH - 1:CH]
                        ins = v.tensor_tensor_scan(CUM[:, c % 2, e, :], ONE[:].to_broadcast([P, CH]), TA[:, n % 2, :], init,
                                                   ALU.mult, ALU.add)
                        ins.then_inc(v_used, 1)
                        dve.wait_ge(v_used, n)
                        b = bank_in()
                        ins = v.scalar_tensor_tensor(out=VH[:, e, :], in0=bank(b), scalar=float(D) ** 0.5 / T, in1=CUM[:, c % 2, e, :],
                                                     op0=ALU.mult, op1=ALU.mult)
                        ins.then_inc(d_free, 1)
                    residual(c)
                    if c == NC - 1:
                        v.tensor_copy(NW[:, 6, 0:1], ONE[:]).then_inc(l1w_free, 1)
                if k == "ar":
                    for n, (tb, i, s0, w) in enumerate(L2.tiles):
                        if tb // BPC != c:
                            continue
                        if n >= AR_OUT:
                            dve.wait_ge(ar_out[n % AR_OUT], 16 * (n // AR_OUT))
                        for x in range(0, w, CH):
                            b, width = bank_in(), min(CH, w - x)
                            dst, src = ARS[:, n % AR_OUT, x:x + width], bank(b, width)
                            if s0 + x + width == (tb + 1) * P:
                                ins = v.tensor_tensor(dst, src, MASKS[:, 1, W1 - width:W1], ALU.add)
                            else:
                                ins = v.tensor_copy(dst, src)
                            ins.then_inc(d_free, 1)
                if k in ("hyp", "hypout"):
                    if (k, c) == ("hyp", 0):
                        dve.wait_ge(w2_in, 16 * 15)
                    for h in range(2):
                        b = bank_in()
                        v.tensor_tensor(Y2[:, 2 * h:2 * h + 2, :], bank(b).rearrange("p (b d) -> p b d", d=D),
                                        SCALE.unsqueeze(1).to_broadcast([P, 2, D]), ALU.mult).then_inc(d_free, 1)
                    dve.wait_ge(d_free, nd.k)
                    link(*[v.tensor_tensor_reduce(out=JUNK[:, i * D:(i + 1) * D], in0=Y2[:, i, :], in1=Y2[:, i, :], scale=1.0, scalar=0.0,
                                                  op0=ALU.mult, op1=ALU.add, accum_out=NW[:, 0, i:i + 1]) for i in range(BPC)])
                    rsqrt(NW[:, 1, :], NW[:, 0, :], NW[:, 2, :])
                    link(v.tensor_tensor(NW[:, 3, :], NW[:, 0, :], NW[:, 1, :], ALU.mult))
                    v.tensor_scalar(NW[:, 4, :], NW[:, 3, :], EPS, None, ALU.max).then_inc(n2_ready, 1)
                    dve.wait_ge(n2_ready, c_n2.next())
                    link(v.tensor_scalar(NW[:, 6, :], NW[:, 4, :], EPS, None, ALU.add))
                    link(v.reciprocal(NW[:, 6, :], NW[:, 6, :]))
                    dve.wait_ge(n2_tanh, c_n2.k)
                    link(v.tensor_tensor(NW[:, 6, :], NW[:, 5, :], NW[:, 6, :], ALU.mult))
                    link(v.tensor_tensor(NW[:, 7, :], NW[:, 3, :], NW[:, 6, :], ALU.mult))
                    link(v.tensor_scalar(NW[:, 7, :], NW[:, 7, :], EPS, None, ALU.max))
                    link(v.reciprocal(NW[:, 7, :], NW[:, 7, :]))
                    link(v.tensor_scalar(NW[:, 7, :], NW[:, 7, :], MAX_NORM, 1.0, ALU.mult, ALU.min))
                    link(v.tensor_tensor(NW[:, 7, :], NW[:, 7, :], NW[:, 6, :], ALU.mult))
                    done = []
                    for i in range(BPC):
                        x = X[:, BPC * c + i, :]
                        done.append(v.scalar_tensor_tensor(out=x, in0=Y2[:, i, :], scalar=NW[:, 7, i:i + 1], in1=x,
                                                           op0=ALU.mult, op1=ALU.add))
                    if k == "hypout":
                        done[-1].then_inc(x_done, 1)
                        dve.wait_ge(x_done, c + 1)
                    else:
                        link(*done)

            def attention_steps(L, steps, group, base, chain_base):
                ring, chain = Count(base), Count(chain_base)

                def clink(ins):
                    ins.then_inc(L.chain, 1)
                    dve.wait_ge(L.chain, chain.next())

                for step in steps:
                    if step[0] in ("mtr", "otr") or (step[0] == "max" and step[2] == 0):
                        n = ring.next()
                        slot = (n - 1) % 2 * 2
                        if step[0] != "max":
                            dve.wait_ge(L.slot_ready, n)
                    if step[0] == "max" and (step[2] + 1) * CH >= L.jobs[step[1]][4]:
                        j, tb, i, s0, w, diag = L.jobs[step[1]]
                        dve.wait_ge(L.slot_ready, n)
                        src = PS[:, slot * CH:slot * CH + w]
                        dst = MP[:, i, tb // BPC, j, tb % BPC:tb % BPC + 1]
                        if L.rope:
                            if n > 1:
                                dve.wait_ge(L.slot_free, n - 1)
                            a = step[1] // HG
                            if j == 0:
                                dve.wait_ge(ar_in[a % AR_RING], 16 * ((group + step[3]) * (len(L.tiles) // AR_RING) + a // AR_RING + 1))
                            ins = v.tensor_tensor_reduce(out=JUNK[:, 0:w], in0=src, in1=AR[a % AR_RING][:, 0:w], scale=1.0,
                                                         scalar=LOWEST, op0=ALU.add, op1=ALU.max, accum_out=dst)
                        elif diag:
                            if n > 1:
                                dve.wait_ge(L.slot_free, n - 1)
                            low = 0.0 if L.zeros and tb < NB - 1 else LOWEST
                            ins = v.tensor_tensor_reduce(out=JUNK[:, 0:w], in0=src, in1=MASKS[:, 0 if L.zeros else 1, W1 - w:W1],
                                                         scale=1.0, scalar=low, op0=ALU.mult if L.zeros else ALU.add, op1=ALU.max,
                                                         accum_out=dst)
                        else:
                            ins = v.reduce_max(dst, src, AX.X)
                        ins.then_inc(L.slot_free, 1)
                    if step[0] == "score" and step[1] in L.added:
                        _, u, j = step
                        e = L.exp_no[u] + j
                        dve.wait_ge(L.score_ready, group * L.n_exp + e + 1)
                        b = bank(4 + e % RING2)
                        v.tensor_tensor(b, b, ARK[:, L.added[u], :], ALU.add).then_inc(L.rope_added, 1)
                    if step[0] == "neg":
                        c = step[1]
                        dve.wait_ge(L.slot_free, base + ring.k)
                        clink(v.tensor_tensor(MX[:, 0], MP[:, 0, c], MP[:, 1, c], ALU.max))
                        clink(v.tensor_scalar(NM[:, :, 0], MX[:, 0], -1.0, None, ALU.mult))
                        clink(v.scalar_tensor_tensor(out=MX[:, 1], in0=MX[:, 0], scalar=-1.0, in1=NM[:, :, 0],
                                                     op0=ALU.mult, op1=ALU.subtract))
                        clink(v.tensor_copy(NM[:, :, 1], MX[:, 1]))
                        v.tensor_tensor(NM[:, :, 2], MX[:, 1], NM[:, :, 1], ALU.subtract).then_inc(L.neg_ready, 1)
                    if step[0] == "mtr":
                        count = (group + step[2]) * NC + step[1]
                        if count > 0:
                            dve.wait_ge(L.max_rows_in, count * ROW_DMAS)
                        rows = PARTS * HG * BPC
                        v.tensor_copy(MR[0:rows, :], bank(slot).bitcast(BF16)[0:rows, 0:P]).then_inc(L.slot_free, 1)
                    if step[0] == "save":
                        dve.wait_ge(L.pv_done, group * L.n_unit + (L.chunk_last[step[1]] + 1))
                        v.tensor_copy(OS[:], bank(7)).then_inc(L.out_saved, 1)
                    if step[0] == "otr":
                        src = bank(slot).rearrange("p (b j d) -> p b j d", b=BPC, j=HG)
                        clink(v.reciprocal(RZ[:].unsqueeze(3), src[:, :, :, DH:DH + 1]))
                        b0 = BPC * step[1]
                        f = group * HG * DH
                        dst = ON[:, b0:b0 + BPC, f:f + HG * DH].rearrange("p b (j d) -> p b j d", d=DH)
                        v.tensor_tensor(dst, src[:, :, :, 0:DH], RZ[:].unsqueeze(3).to_broadcast([P, BPC, HG, DH]), ALU.mult)\
                            .then_inc(L.slot_free, 1)

            def lambdas():
                dve.wait_ge(lam_in, 16 * 5)
                link(*[v.tensor_tensor_reduce(out=JUNK[:, i * D:(i + 1) * D], in0=LV[:, 2 * i, :], in1=LV[:, 2 * i + 1, :], scale=1.0, scalar=0.0,
                                              op0=ALU.mult, op1=ALU.add, accum_out=LAM[:, i:i + 1]) for i in range(2)])
                v.tensor_copy(LAM[:, 4:6], LAM[:, 0:2]).then_inc(lam_dots, 1)
                dve.wait_ge(lam_exp, 1)
                link(v.tensor_tensor(LAM[:, 6:7], LAM[:, 2:3], LAM[:, 3:4], ALU.subtract))
                link(v.tensor_scalar(LAM[:, 6:7], LAM[:, 6:7], LAMBDA_INIT, -DIFF_SCALE, ALU.add, ALU.mult))
                link(v.tensor_scalar(LAM[:, 7:8], SEL[:, 0:1], DIFF_SCALE, None, ALU.mult))
                v.scalar_tensor_tensor(out=QSC[:], in0=SEL[:, 1:2], scalar=LAM[:, 6:7], in1=LAM[:, 7:8], op0=ALU.mult,
                                       op1=ALU.add).then_inc(lam_done, 1)

            def attention(L):
                link(v.memset(MP[:], LOWEST))
                if L.rope:
                    dve.wait_ge(a_free, A_COUNT[L_KEY[L.name]])
                attention_steps(L, L.first, 0, 0, 0)
                for g in range(NG - 1):
                    attention_steps(L, L.stage, g, g * L.r_stage + L.r_first, g * L.chain_stage + L.chain_first)
                g = NG - 1
                attention_steps(L, L.last, g, g * L.r_stage + L.r_first, g * L.chain_stage + L.chain_first)

            dve.wait_ge(const_ready, N_CONST)
            lambdas()
            for kind, steps in PROGRAM:
                if steps is None:
                    attention(att[kind])
                    continue
                for k, c, d0, a0 in steps:
                    if k == "in":
                        dve.wait_ge(x_ins[c], 16)
                    else:
                        main(k, c, d0, a0)
                    if k in HAS_NORM:
                        norm(c)
    return nc


_NAMES = {"x": "L0_attn_a_x", "L0a_q": "L0_attn_a_Wq", "L0a_k": "L0_attn_a_Wk", "L0a_v": "L0_attn_a_Wv", "L0a_o": "L0_attn_a_Wo",
          "L0b_q": "L0_attn_b_Wq", "L0b_k": "L0_attn_b_Wk", "L0b_v": "L0_attn_b_Wv", "L0b_o": "L0_attn_b_Wo",
          "gate": "L0_ffn_w_gate", "up": "L0_ffn_w_up", "down": "L0_ffn_w_down", "attn": "L1_attn_a_W_attn",
          "proj": "L1_attn_a_W_proj", "lq1": "L1_attn_a_lambda_q1", "lk1": "L1_attn_a_lambda_k1",
          "lq2": "L1_attn_a_lambda_q2", "lk2": "L1_attn_a_lambda_k2", "kv": "L1_attn_b_Wkv", "kup": "L1_attn_b_Wkup",
          "vup": "L1_attn_b_Wvup", "L1b_q": "L1_attn_b_Wq", "qr": "L1_attn_b_Wqr", "kr": "L1_attn_b_Wkr",
          "L1b_o": "L1_attn_b_Wo", "hyp_w": "L1_ffn_weight", "hyp_scale": "L1_ffn_scale"}


def _shape_constants():
    inv = (1.0 / np.power(np.float32(10000.0), np.arange(0, ROPE, 2, dtype=np.float32) / np.float32(ROPE))).astype(np.float32)
    angle = np.outer(inv, np.arange(T, dtype=np.float32)).astype(np.float32)
    cos, sin = np.cos(angle).astype(np.float32), np.sin(angle).astype(np.float32)
    first = (np.arange(P) % DH < DH // 2).astype(np.float32)
    return {"cos": np.concatenate([cos, cos]), "sin": np.concatenate([-sin, sin]), "rows": np.stack([first, 1 - first], 1)}


def kernel(**inputs):
    import concourse.bacc as bacc
    from concourse.bass_utils import run_bass_kernel_spmd

    nc = bacc.Bacc("TRN2", target_bir_lowering=False, num_devices=1)
    given = {k: np.ascontiguousarray(inputs[n]) for k, n in _NAMES.items()}
    given.update(_shape_constants())
    arrays = {f"in_{k}": np.ascontiguousarray(x) for k, x in given.items()}
    aps = {k: nc.dram_tensor(f"in_{k}", x.shape, mybir.dt.from_np(x.dtype), kind="ExternalInput").ap() for k, x in given.items()}
    out = nc.dram_tensor("out_0", (1, T, D), F32, kind="ExternalOutput").ap()
    build(nc, aps, out)
    return run_bass_kernel_spmd(nc, [arrays], core_ids=[0]).results[0]["out_0"]
```

```python
from contextlib import ExitStack

import numpy as np

import concourse.bass as bass
from concourse import mybir

F32 = mybir.dt.float32
BF16 = mybir.dt.bfloat16
I32 = mybir.dt.int32
ALU = mybir.AluOpType
ACT = mybir.ActivationFunctionType
AX = mybir.AxisListType

P = 128
T, D, HID = 2048, 256, 1024
H, DH = 16, 16
NB = T // P
CH = 512
NC = T // CH
BPC = CH // P
KD = D // P
HG = 4
NG = H // HG
MW = 1024
PARTS = 3
SROWS = 6 * DH
MROW = SROWS
KROWS = SROWS + PARTS
ROPE = 64
LATENT = 64
LN_EPS = 1e-5
EPS = 1e-7
LOWEST = -3.0e38
LAMBDA_INIT = 0.2
DIFF_SCALE = (D // H // 2) ** -0.5
MAX_NORM = 0.99
LAG = 2
SETS = 3
RING2 = 3


class Count:

    def __init__(self, base=0):
        self.base, self.k = base, 0

    def next(self):
        self.k += 1
        return self.base + self.k


class Layer:

    def __init__(self, name, causal, zeros, rope, w1, sem):
        self.name, self.causal, self.zeros, self.rope = name, causal, zeros, rope
        self.w1, self.slots = w1, 4 * CH // w1
        self.units = []
        self.chunk_last = []
        for c in range(NC):
            for sb in range(BPC * (c + 1) if causal else NB):
                self.units.append(("s", c, sb, max(0, sb - BPC * c) * P if causal else 0))
            if zeros:
                self.units += [("e", c, None, 0), ("m", c, None, 0)]
            self.chunk_last.append(len(self.units) - 1)
        self.jobs = []
        for tb in range(NB):
            end = (tb + 1) * P if causal else T
            for i, s0 in enumerate(range(0, end, w1)):
                w = min(w1, end - s0)
                self.jobs += [(j, tb, i, s0, w, causal and s0 + w == end) for j in range(HG)]
        self.tiles = [(tb, i, s0, w) for j, tb, i, s0, w, _ in self.jobs if j == 0] if rope else []
        full = [u for u, x in enumerate(self.units) if x[0] == "s" and x[3] == 0 and x[2] < BPC * x[1]]
        self.added = {full[len(full) * (2 * n + 1) // (2 * KEPT)]: n for n in range(KEPT)} if rope else {}
        self.exps = [u for u, x in enumerate(self.units) if x[0] != "m"]
        self.exp_no = {u: HG * n for n, u in enumerate(self.exps)}
        self.n_exp = HG * len(self.exps)
        self.masked = [u for u, x in enumerate(self.units) if x[0] == "m" or (x[0] == "s" and self.diagonal(u))]
        self.mask_no = {u: HG * n for n, u in enumerate(self.masked)}
        self.n_mask = HG * len(self.masked)
        self.n_unit = len(self.units)
        self.chunk_first = [0] + [u + 1 for u in self.chunk_last[:-1]]
        self.plan()
        ring = lambda steps: sum(s[0] in ("mtr", "otr") or (s[0] == "max" and s[2] == 0) for s in steps)
        self.r_first, self.r_stage = ring(self.first), ring(self.stage)
        n_first = sum(s[0] == "neg" for s in self.first)
        self.chain_first = n_first * CHAIN_NEG
        self.chain_stage = NC * (CHAIN_NEG + CHAIN_OUT)
        s = lambda x: sem(f"{name}_{x}")
        self.stack_in = s("stack_in")
        self.max_rows_in = s("max_rows_in")
        self.rope_in = s("rope_in")
        self.slot_ready = s("slot_ready")
        self.slot_free = s("slot_free")
        self.neg_ready = s("neg_ready")
        self.score_ready = s("score_ready")
        self.rope_added = s("rope_added")
        self.exp_done = s("exp_done")
        self.mask_done = s("mask_done")
        self.pv_done = s("pv_done")
        self.out_saved = s("out_saved")
        self.v_ready = s("v_ready")
        self.suffix_ready = s("suffix_ready")
        self.chain = s("chain")

    def diagonal(self, u):
        kind, c, sb, off = self.units[u]
        return self.causal and kind == "s" and sb >= BPC * c

    def plan(self):
        width = lambda u: (CH - self.units[u][3]) / CH
        ones, chunk_end = [], {}
        for n, (j, tb, i, s0, w, diag) in enumerate(self.jobs):
            for x in range(0, w, CH):
                ones.append((min(CH, w - x) / CH + (0.2 if x + CH >= w else 0), ("max", n, x // CH)))
            if n + 1 == len(self.jobs) or self.jobs[n + 1][1] // BPC > tb // BPC:
                c = tb // BPC
                ones += [(0.5, ("neg", c)), (2.0, ("mtr", c))]
                chunk_end[c] = sum(x[0] for x in ones)
        total = sum(x[0] for x in ones)
        twos = []
        for u in range(self.n_unit + LAG):
            if u < self.n_unit and self.units[u][0] != "m":
                r = 4 if self.rope else 1
                if u in self.added:
                    r = 0.2
                twos += [(r * width(u), ("score", u, j)) for j in range(HG)]
            if u >= LAG:
                k = u - LAG
                at = len(twos) - 2 if twos[-1][1][:2] == ("score", u) else len(twos)
                twos.insert(at, (4.3 * width(k) if self.units[k][0] == "s" else 6.0, ("pv", k)))
        whole = sum(x[0] for x in twos)
        start, run = {}, 0.0
        for cost, step in twos:
            if step[0] == "score" and step[1] in self.chunk_first and step[2] == 0:
                start[self.chunk_first.index(step[1])] = run / whole
            run += cost
        lead = max(chunk_end[c] - start[c] * total for c in range(NC)) + MARGIN * total
        n_lead, run = 0, 0.0
        while run < lead:
            run += ones[n_lead][0]
            n_lead += 1
        while (ones[n_lead][1][0] == "max" and ones[n_lead][1][2] > 0) or ones[n_lead][1][0] == "mtr":
            n_lead += 1
        self.first = [s + (0,) for _, s in ones[:n_lead]]

        def merge(ahead):
            steps, late, run, given, at = [], [], 0.0, 0.0, 0
            work = total + NC * (SAVE_WORK + OTR_WORK)
            for cost, step in twos:
                while at < len(ahead) and given < (run + cost / 2) / whole * work:
                    given += ahead[at][0]
                    steps.append(ahead[at][1])
                    at += 1
                if step[0] == "score" and step[1] in self.chunk_first and step[2] == 0:
                    need = ("mtr", self.chunk_first.index(step[1]), 0)
                    while need in [s for _, s in ahead[at:]]:
                        given += ahead[at][0]
                        steps.append(ahead[at][1])
                        at += 1
                if late and late[0][0] <= run:
                    while at < len(ahead) and ahead[at][1][0] == "max" and ahead[at][1][2] > 0:
                        given += ahead[at][0]
                        steps.append(ahead[at][1])
                        at += 1
                    steps.append(late.pop(0)[1])
                    given += OTR_WORK
                steps.append(step)
                run += cost
                if step[0] == "pv" and step[1] in self.chunk_last:
                    c = self.chunk_last.index(step[1])
                    steps.append(("save", c))
                    given += SAVE_WORK
                    late.append((run + 6.0, ("otr", c)))
            steps += [s for _, s in ahead[at:]]
            return steps + [s for _, s in late]
        rest = [(x, s + (0,)) for x, s in ones[n_lead:]]
        self.stage = merge(rest + [(x, s + (1,)) for x, s in ones[:n_lead]])
        self.last = merge(rest)


KEPT = 16
AR_RING = 5
SAVE_WORK, OTR_WORK = 1.0, 0.8
MARGIN = 0.04
CHAIN_NEG = 4
CHAIN_OUT = 1


def build(nc, a, out):
    nc.disable_value_cache = True
    ctx = ExitStack()
    with ctx:
        def sb(name, shape, dt=F32):
            return ctx.enter_context(nc.sbuf_tensor(name, shape, dt))

        def sem(name):
            return ctx.enter_context(nc.semaphore(name))

        X = sb("X", [P, NB, D])
        HT = sb("HT", [P, NC, KD, CH])
        ON = HT[:].rearrange("p c k t -> p (c k t)").rearrange("p (b d) -> p b d", d=D)
        VALL = sb("VALL", [P, NB, D])
        VG = sb("VG", [P, NB, HG, 2 * DH])
        QF = sb("QF", [P, 2 * HG * T // 2])
        KF = sb("KF", [P, 2 * HG * T // 2])
        QS = QF[:].bitcast(BF16)
        KS = KF[:].bitcast(BF16)
        PF = sb("PF", [P, SETS * HG * CH])
        PT = PF[:].rearrange("p (u j t) -> p u j t", u=SETS, j=HG)
        WA = sb("WA", [P, 6144])
        WB = sb("WB", [P, 4096])
        WC = sb("WC", [P, 3072])
        MASKS = sb("MASKS", [P, 2, MW], BF16)
        JUNK = sb("JUNK", [P, MW], BF16)
        OS = sb("OS", [P, CH])
        IDF = sb("IDF", [P, P])
        IDB = sb("IDB", [P, P], BF16)
        ONE = sb("ONE", [P, 1])
        ONESEL = sb("ONESEL", [P, P], BF16)
        MP = sb("MP", [P, NC, NC, HG, BPC])
        MX = sb("MX", [P, 2, HG, BPC])
        NM = sb("NM", [P, HG, PARTS, BPC], BF16)
        MR = sb("MR", [P, P], BF16)
        RZ = sb("RZ", [P, BPC, HG])
        ST = sb("ST", [P, BPC, 6])
        MV = sb("MV", [P, BPC, 2])
        NW = sb("NW", [P, 8, BPC])
        LAM = sb("LAM", [P, 8])
        QSC = sb("QSC", [P, 1])
        SEL = sb("SEL", [P, 2])
        PS = ctx.enter_context(nc.psum_tensor("PS", [P, 8 * CH], F32))
        bank = lambda b, n=CH, o=0: PS[:, b * CH + o:b * CH + o + n]

        GT = QF[:, 0:4096].rearrange("p (m t) -> p m t", t=CH)
        LNH = QF[:, 4096:6144].rearrange("p (x b d) -> p x b d", x=2, d=D)
        OT = QF[:, 6144:8192].rearrange("p (x k t) -> p x k t", x=2, k=KD)
        TH = PF[:, 0:1024].rearrange("p (x t) -> p x t", x=2)
        TA = PF[:, 1024:2048].rearrange("p (x t) -> p x t", x=2)
        Y2 = PF[:, 2048:3072].rearrange("p (b d) -> p b d", d=D)
        CUM = PF[:, 2048:4096].rearrange("p (x k t) -> p x k t", x=2, k=KD)
        CKV = PF[0:LATENT, 3072:4096].rearrange("p (x t) -> p x t", x=2)
        VH = PF[:, 4096:5120].rearrange("p (k t) -> p k t", k=KD)
        VS = PF[:, 5120:6144].rearrange("p (x t) -> p x t", x=2)
        STG = PF[:, 4096:5632].bitcast(BF16).rearrange("p (x i t) -> p x i t", x=2, i=PARTS)
        COS = KF[0:ROPE, 4096:4096 + T]
        SIN = KF[0:ROPE, 4096 + T:4096 + 2 * T]
        RA = WA[0:ROPE, 5120:6144].rearrange("p (x t) -> p x t", x=2)

        WGT = WA[:, 0:2048].rearrange("p (k m) -> p k m", k=KD)
        WUT = WA[:, 2048:4096].rearrange("p (k m) -> p k m", k=KD)
        WDT = WA[:, 4096:6144].rearrange("p (m d) -> p m d", d=D)
        sq = lambda w, o: w[:, o:o + KD * D].rearrange("p (k n) -> p k n", k=KD)
        W0 = {x: sq(WB, 512 * i) for i, x in enumerate(("q", "k", "v", "o"))}
        WL = {x: sq(WB, 2048 + 512 * i) for i, x in enumerate(("q", "k", "v", "o"))}
        WAT = WB[:, 0:1536].rearrange("p (k n) -> p k n", k=KD)
        W1A = {"q": sq(WB, 1536), "k": sq(WB, 2048), "v": WAT[:, :, 2 * D:3 * D], "o": sq(WB, 2560)}
        FG = WC[:, 0:2048].rearrange("p (b j d) -> p b j d", b=NB, j=HG)
        W2 = {"q": sq(WC, 0), "o": sq(WC, 512)}
        WN = sq(WC, 1024)
        SCALE = WC[:, 1536:1792]
        WKV = WC[:, 1792:1920].rearrange("p (k n) -> p k n", k=KD)
        WQR = [WC[:, 1920 + 128 * i:2048 + 128 * i].rearrange("p (k n) -> p k n", k=KD) for i in range(2)]
        WKR = [WC[0:LATENT, 2176 + 64 * i:2240 + 64 * i] for i in range(2)]
        WKUP = WC[0:LATENT, 2304:2560]
        WVUP = WC[0:LATENT, 2560:2816]
        RS = WA[:, 0:5120].bitcast(BF16).rearrange("p (i t) -> p i t", t=T)
        AR = [WA[:, 5120:5632], WA[:, 5632:6144], WC[:, 1792:2304], WC[:, 2304:2816],
              MASKS[:].rearrange("p i s -> p (i s)").bitcast(F32)[:, 0:CH]]
        XT = X[:].rearrange("p b d -> p (b d)")
        ARK = [w[:, n * CH:(n + 1) * CH] for w in (WB, XT) for n in range(KEPT // 2)]
        ARS = [HT[:, c].rearrange("p k t -> p (k t)") for c in range(NC)]
        ROPE_Q, ROPE_K = (0, 1, 2), (3, 3, 4)

        NAT = {"gate": QF[:, 0:2048].rearrange("p (m d) -> p m d", d=D),
               "up": QF[:, 2048:4096].rearrange("p (m d) -> p m d", d=D),
               "down": QF[:, 6144:8192].rearrange("p (r m) -> p r m", r=KD)}
        NATL = {x: PF[:, 2048 + 512 * i:2048 + 512 * (i + 1)].rearrange("p (e d) -> p e d", e=KD) for i, x in enumerate(("q", "k", "v", "o"))}

        LV = WC[:, 2048:3072].rearrange("p (i d) -> p i d", d=D)

        L0 = Layer("a", True, True, False, CH, sem)
        L1 = Layer("b", False, False, False, CH, sem)
        L2 = Layer("c", True, False, True, CH, sem)
        scr = {(L.name, w): nc.dram_tensor(f"parts_{L.name}_{w}", (PARTS, D, T), BF16, kind="Internal").ap()
               for L in (L0, L1, L2) for w in "qk"}
        scr_x = nc.dram_tensor("residual", (P, NB, D), F32, kind="Internal").ap()
        scr_ar = nc.dram_tensor("rope_scores", (NB, P, T), F32, kind="Internal").ap()
        scr_r = {w: nc.dram_tensor(f"rope_parts_{w}", (PARTS, ROPE, T), BF16, kind="Internal").ap() for w in "qk"}

        x_in = sem("x_in")
        x_ins = [x_in] + [sem(f"x_in{c}") for c in range(1, NC)]
        w_nat_in = sem("w_nat_in")
        w0_in = sem("w0_in")
        w1_in = sem("w1_in")
        w2_in = sem("w2_in")
        lam_in = sem("lam_in")
        rope_tab_in = sem("rope_tab_in")
        const_ready = sem("const_ready")
        gp = sem("gp")
        d_ready, d_free = sem("d_ready"), sem("d_free")
        a_ready, a_free = sem("a_ready"), sem("a_free")
        tanh_ready = sem("tanh_ready")
        v_used = sem("v_used")
        norm_ready = sem("norm_ready")
        split_ready = sem("split_ready")
        middle_ready = sem("middle_ready")
        parts_ready = sem("parts_ready")
        parts_out = [sem("parts_out0"), sem("parts_out1")]
        n2_ready, n2_tanh = sem("n2_ready"), sem("n2_tanh")
        lam_dots, lam_exp, lam_done = sem("lam_dots"), sem("lam_exp"), sem("lam_done")
        perm_done = sem("perm_done")
        l1w_free = sem("l1w_free")
        out_dma = sem("out_dma")
        vc = sem("vc")
        x_done = sem("x_done")
        x_out, x_back = sem("x_out"), sem("x_back")
        ar_out = [sem(f"ar_out{i}") for i in range(NC)]
        ar_in = [sem(f"ar_in{i}") for i in range(AR_RING)]

        att = {"A": L0, "B": L1, "C": L2}
        def each(*kinds):
            return [(k, c) for k in kinds for c in range(NC)]

        def wave(*kinds):
            return [(kinds[i], c) for t in range(2 * len(kinds) + NC) for i in range(len(kinds)) for c in [t - 2 * i] if 0 <= c < NC]

        start = wave("in", "p0")
        start.insert(start.index(("p0", 0)) + 1, ("wt", 0))
        PROGRAM = [("in", start), ("A", None), ("", wave("o0", "ffn", "lin", "ffn") + each("p1")), ("B", None),
                   ("", wave("o1", "hyp", "p2") + each("ar")), ("C", None), ("", wave("o2", "hypout"))]
        HAS_NORM = {"in", "o0", "ffn", "lin", "o1", "hyp", "o2"}
        OUTW = {"o0": W0["o"], "o1": W1A["o"], "o2": W2["o"], "lin": WL["o"]}
        PROJ = {"p0": (L0, W0, T ** -0.5), "p1": (L1, W1A, None), "p2": (L2, W2, (DH + ROPE) ** -0.5)}
        N_TRANSPOSED = 16

        BANKS = {"in": (0, 0), "wt": (0, N_TRANSPOSED), "p0": (4, 2), "p1": (4, 2), "p2": (8, 3), "o0": (2, 2), "o1": (2, 2), "o2": (2, 2),
                 "ffn": (18, 0), "lin": (6, 2), "hyp": (2, 0), "hypout": (2, 0)}
        ar_banks = lambda c: (BPC * (c + 1), sum(L2.units[u][1] == c for u in L2.added))
        D_COUNT, A_COUNT, HT_AT = {}, {}, []
        NORM_OF = {}
        d_total, a_total = 0, 0
        for kind, steps in PROGRAM:
            if steps is None:
                D_COUNT[kind], A_COUNT[kind] = d_total, a_total
                continue
            pending = False
            for i, (k, c) in enumerate(steps):
                steps[i] = (k, c, d_total, a_total)
                d_banks, a_banks = ar_banks(c) if k == "ar" else BANKS[k]
                d_total += d_banks
                a_total += a_banks
                if k == "wt":
                    wt_done = a_total
                if pending:
                    a_total += KD
                    HT_AT.append(a_total)
                pending = k in HAS_NORM
                if pending:
                    NORM_OF[k, c] = len(HT_AT)
        ar_place, ar_use = [], []
        for n, (tb, _, _, _) in enumerate(L2.tiles):
            ar_place.append(n % NC)
            ar_use.append(ar_place.count(ar_place[n]))
        L_KEY = {"a": "A", "b": "B", "c": "C"}

        block = ctx.enter_context(nc.Block())

        STACK_DMAS = 16 * 12
        ROW_DMAS = 16 * HG
        ROPE_DMAS = 16 * 10
        PARTS_ORDER = [("q", 0), ("q", 1), ("k", 0), ("k", 1)]
        N_CONST = 8

        passed = {n: sem(f"passed_{n}") for n in ("sp", "pool", "dve")}

        def settled(name, engine):
            engine.sem_inc(passed[name], 1)

        @block.sync
        def _(sp):
            xv = a["x"].rearrange("o (b p) d -> p (o b) d", p=P)
            for c in range(NC):
                sp.dma_start(X[:, BPC * c:BPC * (c + 1), :], xv[:, BPC * c:BPC * (c + 1), :]).then_inc(x_ins[c], 16)
            km = lambda w: w.rearrange("(k p) n -> p k n", p=P)
            for x in ("q", "k", "v", "o"):
                sp.dma_start(W0[x], km(a["L0a_" + x])).then_inc(w0_in, 16)
            sp.dma_start(NAT["gate"], km(a["gate"])).then_inc(w_nat_in, 16)
            sp.dma_start(NAT["up"], km(a["up"])).then_inc(w_nat_in, 16)
            sp.dma_start(NAT["down"], km(a["down"])).then_inc(w_nat_in, 16)
            for x in ("q", "k", "v", "o"):
                sp.dma_start(NATL[x], km(a["L0b_" + x])).then_inc(w_nat_in, 16)
            for i, x in enumerate(("lq1", "lk1", "lq2", "lk2")):
                sp.dma_start(LV[:, i, :], a[x].partition_broadcast(P)).then_inc(lam_in, 16)
            sp.dma_start(SEL[:], a["rows"]).then_inc(lam_in, 16)
            parts = Count()
            parts_at = {}

            def parts_to_dram(dst, rows):
                n = parts.next() - 1
                sp.wait_ge(parts_ready, n + 1)
                sp.dma_start(dst, STG[0:rows, n % 2, :, :]).then_inc(parts_out[n % 2], 16)

            def project(kind, c):
                L = PROJ[kind][0]
                t = slice(c * CH, (c + 1) * CH)
                tiles = [(scr[L.name, w][:, e * P:(e + 1) * P, t], P) for w, e in PARTS_ORDER]
                if L.rope:
                    tiles += [(scr_r[w][:, :, t], ROPE) for w in "qk"]
                for n, (dst, rows) in enumerate(tiles):
                    if n == 0 and c > 0:
                        parts_in_dram(L, c - 1)
                    parts_to_dram(dst.rearrange("i f t -> f i t"), rows)
                    if (kind, c, n) == ("p0", 1, 0):
                        sp.wait_ge(a_free, wt_done)
                    if c > 0:
                        load_chunk(L, c - 1, range(6 * n // len(tiles), 6 * (n + 1) // len(tiles)))
                        if L.rope and n < 5:
                            load_rope(L, c - 1, range(n, n + 1))
                parts_at[L.name, c] = parts.k

            def load_stacks(L, group, parity, t=slice(0, T), pieces=range(6)):
                def rows(w, i):
                    x = scr[L.name, w][i, bass.ds(group * (HG * DH), HG * DH), t]
                    return x.rearrange("(j d) t -> d j t", d=DH)
                for n in pieces:
                    for dst, w, i in ((QS, "q", (0, 0, 0, 1, 1, 2)[n]), (KS, "k", (0, 1, 2, 0, 1, 0)[n])):
                        x = dst[n * DH:(n + 1) * DH, bass.ds(parity * (HG * T), HG * T)]
                        sp.dma_start(x.rearrange("d (j t) -> d j t", j=HG)[:, :, t], rows(w, i)).then_inc(L.stack_in, 16)

            def parts_in_dram(L, c):
                for i in range(2):
                    sp.wait_ge(parts_out[i], 16 * ((parts_at[L.name, c] + 1 - i) // 2))

            def load_chunk(L, c, pieces=range(6)):
                if c > 0 and pieces[0] == 0:
                    sp.wait_ge(L.stack_in, c * STACK_DMAS)
                load_stacks(L, 0, 0, slice(c * CH, (c + 1) * CH), pieces)

            def max_rows(L, parity, c, ring):
                sp.wait_ge(L.slot_free, ring)
                settled("sp", sp)
                n = PARTS * BPC
                for j in range(HG):
                    dst = QS[MROW:KROWS, bass.ds(parity * (HG * T) + (j * T + c * CH), CH)]
                    sp.dma_start(dst.rearrange("i (n t) -> i n t", t=P), MR[j * n:(j + 1) * n, :]).then_inc(L.max_rows_in, 16)

            def ar_load(L, n):
                tb, i, s0, w = L.tiles[n]
                sp.dma_start(AR[n % AR_RING][:, 0:w], scr_ar[tb, :, s0:s0 + w]).then_inc(ar_in[n % AR_RING], 16)

            def rows_of(L, steps, group, base, more=True):
                ring = 0
                for step in steps:
                    if step[0] in ("mtr", "otr") or (step[0] == "max" and step[2] == 0):
                        ring += 1
                    if step[0] == "mtr":
                        max_rows(L, (group + step[2]) & 1, step[1], base + ring)
                    if L.rope and step[0] == "max" and L.jobs[step[1]][0] == HG - 1 and (step[2] + 1) * CH >= L.jobs[step[1]][4]:
                        n = step[1] // HG + AR_RING
                        if more or n < len(L.tiles):
                            sp.wait_ge(L.slot_free, base + ring)
                            settled("sp", sp)
                            ar_load(L, n % len(L.tiles))

            def load_rope(L, c, pieces=range(5)):
                if c > 0 and pieces[0] == 0:
                    sp.wait_ge(L.rope_in, c * ROPE_DMAS)
                rq, rk, t = scr_r["q"], scr_r["k"], slice(c * CH, (c + 1) * CH)
                for i in pieces:
                    top, bottom = ((rq[0], rq[0]), (rq[1], rq[1]), (rq[0], rq[2]), (rk[0], rk[1]), (rk[2], rk[0]))[i]
                    sp.dma_start(RS[0:ROPE, i, t], top[:, t]).then_inc(L.rope_in, 16)
                    sp.dma_start(RS[ROPE:P, i, t], bottom[:, t]).then_inc(L.rope_in, 16)

            def rope_tiles(L, c, d0):
                if c == 0:
                    parts_in_dram(L, NC - 1)
                    load_rope(L, NC - 1)
                for n, (tb, i, s0, w) in enumerate(L.tiles):
                    if tb // BPC == c:
                        d0 += (w + CH - 1) // CH
                        sp.wait_ge(d_free, d0)
                        sp.dma_start(scr_ar[tb, :, s0:s0 + w], ARS[ar_place[n]][:, 0:w]).then_inc(ar_out[ar_place[n]], 16)

            def attention(L):
                if not L.rope:
                    parts_in_dram(L, NC - 1)
                load_chunk(L, NC - 1)
                if L.rope:
                    for i in range(NC):
                        sp.wait_ge(ar_out[i], 16 * ar_place.count(i))
                    for n in range(AR_RING):
                        ar_load(L, n)
                sp.wait_ge(L.stack_in, NC * STACK_DMAS)
                load_stacks(L, 1, 1)
                rows_of(L, L.first, 0, 0)
                with sp.Fori(0, NG - 2) as g:
                    rows_of(L, L.stage, g, g * L.r_stage + L.r_first)
                    sp.wait_ge(L.pv_done, (g + 1) * L.n_unit)
                    sp.wait_ge(L.stack_in, (g + (NC + 1)) * STACK_DMAS)
                    settled("sp", sp)
                    load_stacks(L, g + 2, g & 1)
                g = NG - 2
                rows_of(L, L.stage, g, g * L.r_stage + L.r_first)
                rows_of(L, L.last, g + 1, (g + 1) * L.r_stage + L.r_first, more=False)
                if L.rope:
                    sp.wait_ge(L.rope_added, NG * HG * KEPT)
                    for c in range(NC):
                        b = slice(BPC * c, BPC * (c + 1))
                        sp.dma_start(X[:, b, :], scr_x[:, b, :]).then_inc(x_back, 16)

            for kind, steps in PROGRAM:
                if steps is None:
                    attention(att[kind])
                    if kind == "A":
                        sp.wait_ge(L0.pv_done, NG * L0.n_unit)
                        for dst, src in ((W2["q"], km(a["L1b_q"])), (W2["o"], km(a["L1b_o"])), (WN, km(a["hyp_w"])),
                                         (SCALE, a["hyp_scale"].partition_broadcast(P)),
                                         (WKV, km(a["kv"])), (WKUP, a["kup"]), (WVUP, a["vup"])):
                            sp.dma_start(dst, src).then_inc(w2_in, 16)
                        half = ROPE // 2
                        for i in range(2):
                            for h in range(2):
                                o = half * (h if i == 0 else 1 - h)
                                dst = slice(o, o + half)
                                src = slice(half * h, half * (h + 1))
                                sp.dma_start(WQR[i][:, :, dst], km(a["qr"])[:, :, src]).then_inc(w2_in, 16)
                                sp.dma_start(WKR[i][:, dst], a["kr"][:, src]).then_inc(w2_in, 16)
                    continue
                for k, c, d0, a0 in steps:
                    if (k, c) == ("p1", 0):
                        sp.wait_ge(l1w_free, 1)
                        sp.dma_start(WAT, km(a["attn"])).then_inc(w1_in, 16)
                        sp.dma_start(W1A["o"], km(a["proj"])).then_inc(w1_in, 16)
                    if (k, c) == ("p2", 0):
                        sp.wait_ge(L1.pv_done, NG * L1.n_unit)
                        sp.dma_start(COS, a["cos"]).then_inc(rope_tab_in, 16)
                        sp.dma_start(SIN, a["sin"]).then_inc(rope_tab_in, 16)
                    if k in PROJ:
                        project(k, c)
                    if k == "p2":
                        sp.wait_ge(norm_ready, NORM_OF["hyp", c] + 1)
                        b = slice(BPC * c, BPC * (c + 1))
                        sp.dma_start(scr_x[:, b, :], X[:, b, :]).then_inc(x_out, 16)
                    if k == "ar":
                        rope_tiles(L2, c, d0)
                    if k == "hypout":
                        sp.wait_ge(x_done, c + 1)
                        ov = out.rearrange("o (b p) d -> p (o b) d", p=P)
                        sp.dma_start(ov[:, BPC * c:BPC * (c + 1), :], X[:, BPC * c:BPC * (c + 1), :]).then_inc(out_dma, 16)
            sp.wait_ge(out_dma, 16 * NC)

        @block.gpsimd
        def _(pool):
            g_ = nc.gpsimd
            order = Count()

            def link(ins):
                ins.then_inc(gp, 1)
                pool.wait_ge(gp, order.next())

            consts = Count()

            def constant(ins):
                ins.then_inc(const_ready, 1)
                pool.wait_ge(const_ready, consts.next())

            link(g_.memset(IDF[:], 0.0))
            link(g_.affine_select(out=IDF[:], in_=IDF[:], compare_op=ALU.not_equal, fill=1.0, base=0,
                                  pattern=[[-1, P]], channel_multiplier=1))
            constant(g_.tensor_copy(IDB[:], IDF[:]))
            link(g_.memset(MASKS[:, 0, :], 1.0))
            constant(g_.affine_select(out=MASKS[:, 0, MW - P:MW], in_=MASKS[:, 0, MW - P:MW], compare_op=ALU.is_ge, fill=0.0,
                                      base=0, pattern=[[-1, P]], channel_multiplier=1))
            constant(g_.tensor_scalar(MASKS[:, 1, :], MASKS[:, 0, :], -1.0, -LOWEST, ALU.add, ALU.mult))
            link(g_.memset(ONESEL[:], 0.0))
            constant(g_.memset(ONESEL[MROW:KROWS, :], 1.0))
            constant(g_.memset(ONE[:], 1.0))
            constant(g_.memset(VG[:, :, :, DH:2 * DH], 1.0))
            constant(g_.memset(FG[:, NB - 1, :, :], 0.0))
            constant(g_.memset(KS[MROW:KROWS, :], 1.0))
            parts = Count()

            def split(rows):
                n = parts.next() - 1
                pool.wait_ge(middle_ready, n + 1)
                g_.tensor_tensor(STG[0:rows, n % 2, 2, :], TA[0:rows, n % 2, :], STG[0:rows, n % 2, 1, :], ALU.subtract)\
                    .then_inc(parts_ready, 1)

            def stage(L, g):
                chain = Count(g * (NB - 1))
                quarter = NB // 4
                for i in range(4):
                    b = slice(quarter * i, quarter * (i + 1))
                    src = VALL[:, b, bass.ds(g * (HG * DH), HG * DH)].rearrange("p b (j d) -> p b j d", d=DH)
                    g_.tensor_copy(VG[:, b, :, 0:DH], src).then_inc(L.v_ready, 1)
                for step in L.stage:
                    if step[0] != "score":
                        continue
                    _, u, j = step
                    kind, c, sb_, off = L.units[u]
                    if L.diagonal(u):
                        tile = PT[:, u % SETS, j, off:off + P]
                        pool.wait_ge(L.exp_done, g * L.n_exp + (L.exp_no[u] + j + 1))
                        settled("pool", pool)
                        g_.affine_select(out=tile, in_=tile, compare_op=ALU.is_ge, fill=0.0, base=0,
                                         pattern=[[1, P]], channel_multiplier=-1).then_inc(L.mask_done, 1)
                    if kind == "e":
                        if c == 0 and j == 0:
                            pool.wait_ge(L.v_ready, g * 4 + 4)
                            for b in range(NB - 2, -1, -1):
                                g_.tensor_tensor(FG[:, b], FG[:, b + 1], VG[:, b + 1], ALU.add).then_inc(L.suffix_ready, 1)
                                pool.wait_ge(L.suffix_ready, chain.next())
                        m = u + 1
                        if m >= SETS and j == 0:
                            pool.wait_ge(L.pv_done, g * L.n_unit + (m - SETS + 1))
                        pool.wait_ge(L.exp_done, g * L.n_exp + (L.exp_no[u] + j + 1))
                        settled("pool", pool)
                        v = lambda s: PT[:, s, j, :].rearrange("p (b t) -> p b t", t=P)
                        g_.affine_select(out=v(m % SETS), in_=v(u % SETS), compare_op=ALU.is_ge, fill=0.0, base=-1,
                                         pattern=[[0, BPC], [-1, P]], channel_multiplier=1).then_inc(L.mask_done, 1)
                pool.wait_ge(L.pv_done, (g + 1) * L.n_unit)

            for kind, steps in PROGRAM:
                if steps is None:
                    L = att[kind]
                    pool.wait_ge(a_free, A_COUNT[kind])
                    with pool.Fori(0, NG) as g:
                        stage(L, g)
                    continue
                for k, c, d0, a0 in steps:
                    if (k, c) == ("p1", 0):
                        pool.wait_ge(w1_in, 32)
                        half = D // 2
                        for n, w in enumerate(("q", "k")):
                            for i in range(2):
                                dst = W1A[w].rearrange("p k (h i d) -> p k h i d", i=2, d=DH // 2)[:, :, :, i, :]
                                o = (2 * i + n) * half
                                src = WAT[:, :, o:o + half].rearrange("p k (h d) -> p k h d", d=DH // 2)
                                for kk in range(KD):
                                    g_.tensor_copy(dst[:, kk], src[:, kk]).then_inc(perm_done, 1)
                    if k in PROJ:
                        for w, e in PARTS_ORDER:
                            split(P)
                        if PROJ[k][0].rope:
                            for w in "qk":
                                split(ROPE)

        @block.tensor
        def _(pe):
            mm = nc.tensor.matmul
            nd, na = Count(), Count()

            def d_bank():
                n = nd.next() - 1
                if n >= 4:
                    pe.wait_ge(d_free, n - 3)
                return n % 4

            def a_bank():
                n = na.next() - 1
                if n >= 4:
                    pe.wait_ge(a_free, n - 3)
                return 4 + n % 4

            def over_k(dst, left, right, n=KD):
                for k in range(n):
                    ins = mm(dst, left(k), right(k), start=k == 0, stop=k == n - 1)
                return ins

            def rope_product(dst, left, l0, m, right, r0, n, start=True):
                for r in range(3):
                    ins = mm(dst, RS[:, left[r], l0:l0 + m], RS[:, right[r], r0:r0 + n], start=start and r == 0, stop=r == 2)
                return ins

            def weight_transposes():
                pe.wait_ge(w_nat_in, 16 * 7)
                for w in ("gate", "up"):
                    for k in range(KD):
                        for m0 in range(0, HID // P, 4):
                            b = a_bank()
                            for i in range(4):
                                ins = nc.tensor.transpose(bank(b, P, i * P), NAT[w][:, m0 + i, k * P:(k + 1) * P], IDF[:])
                            ins.then_inc(a_ready, 1)
                for m in range(0, HID // P, 2):
                    b = a_bank()
                    for i in range(4):
                        ins = nc.tensor.transpose(bank(b, P, i * P), NAT["down"][:, i % 2, (m + i // 2) * P:(m + i // 2 + 1) * P], IDF[:])
                    ins.then_inc(a_ready, 1)
                for w in ("q", "k", "v", "o"):
                    b = a_bank()
                    for i in range(4):
                        ins = nc.tensor.transpose(bank(b, P, i * P), NATL[w][:, i % 2, (i // 2) * P:(i // 2 + 1) * P], IDF[:])
                    ins.then_inc(a_ready, 1)

            def norm_transposes(n):
                pe.wait_ge(norm_ready, n + 1)
                for k in range(KD):
                    b = a_bank()
                    for i in range(BPC):
                        ins = nc.tensor.transpose(bank(b, P, i * P), LNH[:, n % 2, i, k * P:(k + 1) * P], IDF[:])
                    ins.then_inc(a_ready, 1)

            def token_major(left, right, n_k, ring, ready, wide=2):
                for h in range(BPC // 2):
                    b = ring()
                    for i in range(2):
                        ins = over_k(bank(b, D, i * D), lambda k: left(k, 2 * h + i), right, n_k)
                    ins.then_inc(ready, 1)

            def main(k, c, d0, a0):
                if k == "wt":
                    weight_transposes()
                    return
                ht = lambda kk: HT[:, c, kk, :]
                blk = lambda i: slice(i * P, (i + 1) * P)
                if k not in ("o0", "o1", "o2"):
                    pe.wait_ge(a_free, HT_AT[norm_of[c]])
                if k in ("p0", "p1"):
                    L, W, _ = PROJ[k]
                    if (k, c) == ("p0", 0):
                        pe.wait_ge(w0_in, 16 * 4)
                    if (k, c) == ("p1", 0):
                        pe.wait_ge(perm_done, 4 * KD)
                    for w, e in PARTS_ORDER:
                        b = d_bank()
                        over_k(bank(b), lambda kk: W[w][:, kk, e * P:(e + 1) * P], ht).then_inc(d_ready, 1)
                    token_major(lambda kk, i: HT[:, c, kk, blk(i)], lambda kk: W["v"][:, kk, :], KD, a_bank, a_ready)
                if k == "p2":
                    L, W, _ = PROJ[k]
                    b = a_bank()
                    over_k(bank(b)[0:LATENT], lambda kk: WKV[:, kk, :], ht).then_inc(a_ready, 1)
                    latent_done = na.k
                    for e in range(KD):
                        b = d_bank()
                        over_k(bank(b), lambda kk: W["q"][:, kk, e * P:(e + 1) * P], ht).then_inc(d_ready, 1)
                    pe.wait_ge(a_free, latent_done)
                    for e in range(KD):
                        b = d_bank()
                        mm(bank(b), WKUP[:, e * P:(e + 1) * P], CKV[:, c % 2, :], start=True, stop=True).then_inc(d_ready, 1)
                    for i in range(2):
                        b = d_bank()
                        over_k(bank(b)[0:ROPE], lambda kk: WQR[i][:, kk, :], ht).then_inc(d_ready, 1)
                    for i in range(2):
                        b = d_bank()
                        mm(bank(b)[0:ROPE], WKR[i], CKV[:, c % 2, :], start=True, stop=True).then_inc(d_ready, 1)
                    token_major(lambda kk, i: CKV[:, c % 2, blk(i)], lambda kk: WVUP, 1, a_bank, a_ready)
                if k in ("o0", "o1", "o2"):
                    for kk in range(KD):
                        b = a_bank()
                        for i in range(BPC):
                            ins = nc.tensor.transpose(bank(b, P, i * P), ON[:, BPC * c + i, kk * P:(kk + 1) * P], IDF[:])
                        ins.then_inc(a_ready, 1)
                    pe.wait_ge(a_free, na.k)
                    token_major(lambda kk, i: OT[:, c % 2, kk, blk(i)], lambda kk: OUTW[k][:, kk, :], KD, d_bank, d_ready)
                if k == "ffn":
                    for m in range(HID // P):
                        for W in (WGT, WUT):
                            b = d_bank()
                            over_k(bank(b), lambda kk: W[:, kk, m * P:(m + 1) * P], ht).then_inc(d_ready, 1)
                    for h in range(BPC // 2):
                        b = d_bank()
                        for i in range(2):
                            for m in range(HID // P):
                                if h == 0 and i == 0:
                                    pe.wait_ge(d_free, d0 + 2 * m + 2)
                                ins = mm(bank(b, D, i * D), GT[:, m, blk(2 * h + i)], WDT[:, m, :], start=m == 0, stop=m == HID // P - 1)
                        ins.then_inc(d_ready, 1)
                if k == "lin":
                    for e in range(KD):
                        for w in ("v", "k", "q"):
                            b, ready = (a_bank(), a_ready) if w == "v" else (d_bank(), d_ready)
                            over_k(bank(b), lambda kk: WL[w][:, kk, e * P:(e + 1) * P], ht).then_inc(ready, 1)
                    pe.wait_ge(d_free, d0 + 2 * KD)
                    token_major(lambda kk, i: VH[:, kk, blk(i)], lambda kk: OUTW[k][:, kk, :], KD, d_bank, d_ready)
                if k == "ar":
                    pe.wait_ge(L2.rope_in, (c + 1) * ROPE_DMAS)
                    for tb, i, s0, w in L2.tiles:
                        if tb // BPC != c:
                            continue
                        for x in range(s0, s0 + w, CH):
                            b, width = d_bank(), min(CH, s0 + w - x)
                            rope_product(bank(b, width), ROPE_Q, tb * P, P, ROPE_K, x, width).then_inc(d_ready, 1)
                    for u in L2.added:
                        if L2.units[u][1] == c:
                            rope_product(bank(a_bank()), ROPE_K, L2.units[u][2] * P, P, ROPE_Q, c * CH, CH).then_inc(a_ready, 1)
                if k in ("hyp", "hypout"):
                    token_major(lambda kk, i: HT[:, c, kk, blk(i)], lambda kk: WN[:, kk, :], KD, d_bank, d_ready)

            def max_piece(L, n, x, slot, off):
                j, tb, i, s0, w, diag = L.jobs[n]
                s0, width = s0 + x * CH, min(CH, w - x * CH)
                ins = mm(bank(slot + x, width), QS[0:SROWS, off + j * T + tb * P:off + j * T + (tb + 1) * P],
                         KS[0:SROWS, off + j * T + s0:off + j * T + s0 + width], start=True, stop=True)
                if (x + 1) * CH >= w:
                    ins.then_inc(L.slot_ready, 1)

            def attention_steps(L, steps, group, base):
                ring = Count(base)
                for step in steps:
                    if step[0] in ("mtr", "otr") or (step[0] == "max" and step[2] == 0):
                        n = ring.next()
                        if n > L.slots:
                            pe.wait_ge(L.slot_free, n - L.slots)
                        slot = (n - 1) % L.slots * (L.w1 // CH)
                    if step[0] == "max":
                        _, job, x, nxt = step
                        tb = L.jobs[job][1]
                        if x == 0 and group + nxt > 0 and job == 0:
                            pe.wait_ge(L.stack_in, (NC + group + nxt) * STACK_DMAS)
                        if x == 0 and group + nxt == 0 and tb % BPC == 0 and L.jobs[job - 1][1] != tb:
                            pe.wait_ge(L.stack_in, (tb // BPC + 1 if L.causal else NC) * STACK_DMAS)
                        max_piece(L, job, x, slot, (group + nxt) % 2 * HG * T)
                    if step[0] == "mtr":
                        pe.wait_ge(L.neg_ready, (group + step[2]) * NC + step[1] + 1)
                        dst = bank(slot).bitcast(BF16)[0:PARTS * HG * BPC, 0:P]
                        nc.tensor.transpose(dst, NM[:].rearrange("p j i n -> p (j i n)"), IDB[:]).then_inc(L.slot_ready, 1)
                    if step[0] == "otr":
                        pe.wait_ge(L.out_saved, group * NC + (step[1] + 1))
                        for i in range(BPC):
                            ins = nc.tensor.transpose(bank(slot, P, i * P), OS[:, i * P:(i + 1) * P], IDF[:])
                        ins.then_inc(L.slot_ready, 1)
                    if step[0] == "score":
                        _, u, j = step
                        kind, c, sb_, off = L.units[u]
                        off2 = group % 2 * HG * T + j * T
                        if u in L.chunk_first and j == 0:
                            pe.wait_ge(L.max_rows_in, (group * NC + c + 1) * ROW_DMAS)
                        n = L.exp_no[u] + j
                        if n >= RING2:
                            pe.wait_ge(L.exp_done, group * L.n_exp + (n - RING2 + 1))
                        q = QS[0:KROWS, off2 + c * CH + off:off2 + (c + 1) * CH]
                        dst = bank(4 + n % RING2, CH - off)
                        if kind == "e":
                            ins = mm(dst, ONESEL[0:KROWS, :], q, start=True, stop=True)
                        else:
                            k = KS[0:KROWS, off2 + sb_ * P:off2 + (sb_ + 1) * P]
                            rope = L.rope and u not in L.added
                            ins = mm(dst, k, q, start=True, stop=not rope)
                            if rope:
                                ins = rope_product(dst, ROPE_K, sb_ * P, P, ROPE_Q, c * CH + off, CH - off, start=False)
                        ins.then_inc(L.score_ready, 1)
                    if step[0] == "pv":
                        u = step[1]
                        kind, c, sb_, off = L.units[u]
                        first, last = u == 0 or u - 1 in L.chunk_last, u in L.chunk_last
                        if first and c == 0:
                            pe.wait_ge(L.v_ready, group * 4 + 1)
                        if kind == "s" and sb_ % 4 == 0 and c == (sb_ // 4 if L.causal else 0):
                            pe.wait_ge(L.v_ready, group * 4 + (sb_ // 4 + 1))
                        if kind == "e" and c == 0:
                            pe.wait_ge(L.suffix_ready, (group + 1) * (NB - 1))
                        if first and c > 0:
                            pe.wait_ge(L.out_saved, group * NC + c)
                        if kind == "m" or L.diagonal(u):
                            pe.wait_ge(L.mask_done, group * L.n_mask + (L.mask_no[u] + HG))
                        else:
                            pe.wait_ge(L.exp_done, group * L.n_exp + (L.exp_no[u] + HG))
                        pieces = [(off, CH)] if kind == "s" else [(i * P, (i + 1) * P) for i in range(BPC)]
                        for i, (t0, t1) in enumerate(pieces):
                            for j in range(HG):
                                V = VG[:, sb_, j, :] if kind == "s" else (FG if kind == "e" else VG)[:, BPC * c + i, j, :]
                                ins = mm(PS[32 * j:32 * j + 2 * DH, 7 * CH + t0:7 * CH + t1], V, PT[:, u % SETS, j, t0:t1],
                                         start=first, stop=last, tile_position=(0, 32 * j), skip_group_check=True)
                        ins.then_inc(L.pv_done, 1)

            def attention(L):
                pe.wait_ge(d_free, D_COUNT[L_KEY[L.name]])
                pe.wait_ge(a_free, A_COUNT[L_KEY[L.name]])
                pe.wait_ge(const_ready, N_CONST)
                attention_steps(L, L.first, 0, 0)
                for g in range(NG - 1):
                    attention_steps(L, L.stage, g, g * L.r_stage + L.r_first)
                g = NG - 1
                attention_steps(L, L.last, g, g * L.r_stage + L.r_first)
                pe.wait_ge(L.slot_free, NG * L.r_stage)
                pe.wait_ge(L.out_saved, NG * NC)

            pe.wait_ge(const_ready, 1)
            norms = Count()
            norm_of = {}
            for kind, steps in PROGRAM:
                if steps is None:
                    attention(att[kind])
                    continue
                pending = None
                if kind == "" and steps[0][0] == "o1":
                    pe.wait_ge(w2_in, 16 * 15)
                for k, c, d0, a0 in steps:
                    if k != "in":
                        main(k, c, d0, a0)
                    if pending is not None:
                        norm_transposes(pending)
                    pending = norms.next() - 1 if k in HAS_NORM else None
                    if pending is not None:
                        norm_of[c] = pending
                assert pending is None
            assert (nd.k, na.k) == (d_total, a_total)

        @block.scalar
        def _(act):
            sc = nc.scalar
            na, nd = Count(), Count()
            c_tanh, c_v, c_n2 = Count(), Count(), Count()

            def take(dst, src_of, scale=1.0, rows=P):
                n = na.next() - 1
                act.wait_ge(a_ready, n + 1)
                src = src_of(4 + n % 4)
                if scale == 1.0:
                    return sc.copy(dst, src)
                return sc.mul(dst, src, scale)

            def weight_copies():
                for w in (WGT, WUT):
                    for k in range(KD):
                        for m in range(2):
                            take(w[:, k, m * CH:(m + 1) * CH], bank).then_inc(a_free, 1)
                for m in range(4):
                    take(WDT[:, 2 * m:2 * m + 2, :], lambda b: bank(b).rearrange("p (m d) -> p m d", d=D)).then_inc(a_free, 1)
                for w in ("q", "k", "v", "o"):
                    take(WL[w], lambda b: bank(b).rearrange("p (k e) -> p k e", k=KD)).then_inc(a_free, 1)

            def main(k, c, d0, a0):
                if k == "wt":
                    weight_copies()
                if k == "lin":
                    for e in range(KD):
                        n = c_v.next()
                        if n > 2:
                            act.wait_ge(v_used, n - 2)
                        take(VS[:, n % 2, :], bank).then_inc(a_free, 1)
                if k in ("o0", "o1", "o2"):
                    for kk in range(KD):
                        take(OT[:, c % 2, kk, :], bank, 1.0 - LAMBDA_INIT if k == "o1" else 1.0).then_inc(a_free, 1)
                if k == "p2":
                    take(CKV[:, c % 2, :], lambda b: bank(b)[0:LATENT]).then_inc(a_free, 1)
                if k in ("p0", "p1", "p2"):
                    for i in range(len(PARTS_ORDER)):
                        middle_part(P, d_free, d0 + i + 1)
                    if PROJ[k][0].rope:
                        for _ in "qk":
                            middle_part(ROPE, split_ready, rope_parts.next())
                    for h in range(2):
                        b0 = BPC * c + 2 * h
                        take(VALL[:, b0:b0 + 2, :], lambda b: bank(b).rearrange("p (b d) -> p b d", d=D)).then_inc(a_free, 1)
                if k == "ffn":
                    for m in range(HID // P):
                        n = c_tanh.next()
                        act.wait_ge(d_ready, d0 + 2 * m + 1)
                        if n > 2:
                            act.wait_ge(d_free, gates[n - 3])
                        gates.append(d0 + 2 * m + 1)
                        sc.activation(TH[:, n % 2, :], bank((d0 + 2 * m) % 4), ACT.Tanh, scale=0.5).then_inc(tanh_ready, 1)
                if k == "ar":
                    for u, n in L2.added.items():
                        if L2.units[u][1] == c:
                            if n == KEPT // 2:
                                act.wait_ge(x_out, 16 * NC)
                            take(ARK[n], bank).then_inc(a_free, 1)
                if k in ("hyp", "hypout"):
                    act.wait_ge(n2_ready, c_n2.next())
                    sc.activation(NW[:, 5, :], NW[:, 4, :], ACT.Tanh).then_inc(n2_tanh, 1)

            parts, rope_parts = Count(), Count()

            def middle_part(rows, ready, count):
                n = parts.next() - 1
                act.wait_ge(ready, count)
                sc.copy(STG[0:rows, n % 2, 1, :], TA[0:rows, n % 2, :]).then_inc(middle_ready, 1)

            def norm_copies(c):
                for k in range(KD):
                    take(HT[:, c, k, :], bank).then_inc(a_free, 1)

            gates = []
            for kind, steps in PROGRAM:
                if steps is None:
                    L = att[kind]
                    if kind == "A":
                        act.wait_ge(lam_dots, 1)
                        sc.activation(LAM[:, 2:4], LAM[:, 4:6], ACT.Exp).then_inc(lam_exp, 1)
                    with act.Fori(0, NG) as g:
                        for u in L.exps:
                            for j in range(HG):
                                n = L.exp_no[u] + j
                                off = L.units[u][3]
                                if u in L.added:
                                    act.wait_ge(L.rope_added, g * (HG * len(L.added)) + (HG * L.added[u] + j + 1))
                                else:
                                    act.wait_ge(L.score_ready, g * L.n_exp + (n + 1))
                                if j == 0 and u >= SETS:
                                    act.wait_ge(L.pv_done, g * L.n_unit + (u - SETS + 1))
                                if j == 0 and u >= SETS and L.units[u - SETS][0] == "e":
                                    act.wait_ge(L.mask_done, g * L.n_mask + (L.mask_no[u - SETS + 1] + HG))
                                sc.activation(PT[:, u % SETS, j, off:CH], bank(4 + n % RING2, CH - off), ACT.Exp).then_inc(L.exp_done, 1)
                    continue
                pending = None
                for k, c, d0, a0 in steps:
                    main(k, c, d0, a0)
                    if pending is not None:
                        norm_copies(pending)
                    pending = c if k in HAS_NORM else None

        @block.vector
        def _(dve):
            v = nc.vector
            order = Count()
            nd = Count()
            c_tanh, c_parts, c_n2 = Count(), Count(), Count()

            def link(*ins):
                for i in ins:
                    i.then_inc(vc, 1)
                    order.k += 1
                dve.wait_ge(vc, order.k)

            def bank_in():
                n = nd.next() - 1
                dve.wait_ge(d_ready, n + 1)
                return n % 4

            def rsqrt(dst, src, tmp):
                link(v.tensor_scalar(dst.bitcast(I32), src.bitcast(I32), 1, None, ALU.logical_shift_right))
                link(v.tensor_scalar(dst.bitcast(I32), dst.bitcast(I32), -1.0, float(0x5F3759DF), ALU.mult, ALU.add))
                for _ in range(3):
                    link(v.scalar_tensor_tensor(out=tmp, in0=dst, scalar=-0.5, in1=src, op0=ALU.mult, op1=ALU.mult))
                    link(v.tensor_tensor(tmp, tmp, dst, ALU.mult))
                    link(v.scalar_tensor_tensor(out=dst, in0=tmp, scalar=1.5, in1=dst, op0=ALU.add, op1=ALU.mult))

            norms = Count()

            def norm(c):
                n = norms.next() - 1
                link(*[v.bn_stats(ST[:, i, :], X[:, BPC * c + i, :]) for i in range(BPC)])
                link(*[v.bn_aggr(MV[:, i, :], ST[:, i, :]) for i in range(BPC)])
                link(v.tensor_scalar(NW[:, 0, :], MV[:, :, 1], LN_EPS, None, ALU.add))
                rsqrt(NW[:, 1, :], NW[:, 0, :], NW[:, 2, :])
                if n >= 2:
                    dve.wait_ge(a_free, HT_AT[n - 2])
                for i in range(BPC):
                    ins = v.tensor_scalar(LNH[:, n % 2, i, :], X[:, BPC * c + i, :], MV[:, i, 0:1], NW[:, 1, i:i + 1],
                                          ALU.subtract, ALU.mult)
                ins.then_inc(norm_ready, 1)

            def residual(c):
                for h in range(2):
                    b = bank_in()
                    x = X[:, BPC * c + 2 * h:BPC * c + 2 * h + 2, :]
                    ins = v.tensor_tensor(x, bank(b).rearrange("p (b d) -> p b d", d=D), x, ALU.add)
                    ins.then_inc(d_free, 1)
                    order_x(ins)

            def order_x(ins):
                dve.wait_ge(d_free, nd.k)

            def parts(rows, n):
                if n >= 2:
                    dve.wait_ge(parts_out[n % 2], 16 * (n // 2))
                link(v.tensor_copy(STG[0:rows, n % 2, 0, :], TH[0:rows, n % 2, :]))
                v.tensor_tensor(TA[0:rows, n % 2, :], TH[0:rows, n % 2, :], STG[0:rows, n % 2, 0, :], ALU.subtract)\
                    .then_inc(split_ready, 1)

            def main(k, c, d0, a0):
                if k in PROJ:
                    L, W, scale = PROJ[k]
                    for w, e in PARTS_ORDER:
                        b = bank_in()
                        n = c_parts.next() - 1
                        if (w, scale, c, e) == ("q", None, 0, 0):
                            dve.wait_ge(lam_done, 1)
                        factor = 1.0 if w == "k" else QSC[:] if scale is None else float(scale)
                        if n >= 2:
                            dve.wait_ge(parts_out[n % 2], 16 * (n // 2))
                        link(v.tensor_scalar(STG[:, n % 2, 0, :], bank(b), factor, None, ALU.mult))
                        v.scalar_tensor_tensor(out=TA[:, n % 2, :], in0=bank(b), scalar=factor, in1=STG[:, n % 2, 0, :],
                                               op0=ALU.mult, op1=ALU.subtract).then_inc(d_free, 1)
                    if L.rope:
                        if c == 0:
                            dve.wait_ge(rope_tab_in, 32)
                        t = slice(c * CH, (c + 1) * CH)
                        for w in "qk":
                            s = float(scale) if w == "q" else 1.0
                            n = c_parts.next() - 1
                            for i, tab in enumerate((COS, SIN)):
                                b = bank_in()
                                v.scalar_tensor_tensor(out=RA[:, i, :], in0=bank(b)[0:ROPE], scalar=s, in1=tab[:, t],
                                                       op0=ALU.mult, op1=ALU.mult).then_inc(d_free, 1)
                            dve.wait_ge(d_free, nd.k)
                            link(v.tensor_tensor(TH[0:ROPE, n % 2, :], RA[:, 0, :], RA[:, 1, :], ALU.add))
                            parts(ROPE, n)
                if k in ("o0", "o1", "o2"):
                    if (k, c) == ("o2", 0):
                        dve.wait_ge(x_back, 16 * NC)
                    residual(c)
                if k == "ffn":
                    for m in range(HID // P):
                        n = c_tanh.next()
                        bg = bank_in()
                        dve.wait_ge(tanh_ready, n)
                        v.scalar_tensor_tensor(out=TA[:, n % 2, :], in0=TH[:, n % 2, :], scalar=1.0, in1=bank(bg),
                                               op0=ALU.add, op1=ALU.mult).then_inc(d_free, 1)
                        dve.wait_ge(d_free, nd.k)
                        bu = bank_in()
                        v.scalar_tensor_tensor(out=GT[:, m, :], in0=TA[:, n % 2, :], scalar=0.5, in1=bank(bu),
                                               op0=ALU.mult, op1=ALU.mult).then_inc(d_free, 1)
                    residual(c)
                if k == "lin":
                    for e in range(KD):
                        b = bank_in()
                        n = KD * c + e + 1
                        dve.wait_ge(a_free, a0 + e + 1)
                        v.tensor_tensor(TA[:, n % 2, :], bank(b), VS[:, n % 2, :], ALU.mult).then_inc(d_free, 1)
                        dve.wait_ge(d_free, nd.k)
                        init = 0.0 if c == 0 else CUM[:, (c + 1) % 2, e, CH - 1:CH]
                        ins = v.tensor_tensor_scan(CUM[:, c % 2, e, :], ONE[:].to_broadcast([P, CH]), TA[:, n % 2, :], init,
                                                   ALU.mult, ALU.add)
                        ins.then_inc(v_used, 1)
                        dve.wait_ge(v_used, n)
                        b = bank_in()
                        ins = v.scalar_tensor_tensor(out=VH[:, e, :], in0=bank(b), scalar=float(D) ** 0.5 / T, in1=CUM[:, c % 2, e, :],
                                                     op0=ALU.mult, op1=ALU.mult)
                        ins.then_inc(d_free, 1)
                    residual(c)
                    if c == NC - 1:
                        v.tensor_copy(NW[:, 6, 0:1], ONE[:]).then_inc(l1w_free, 1)
                if k == "ar":
                    for n, (tb, i, s0, w) in enumerate(L2.tiles):
                        if tb // BPC != c:
                            continue
                        place, use = ar_place[n], ar_use[n]
                        if use > 1:
                            dve.wait_ge(ar_out[place], 16 * (use - 1))
                        for x in range(0, w, CH):
                            b, width = bank_in(), min(CH, w - x)
                            dst, src = ARS[place][:, x:x + width], bank(b, width)
                            if s0 + x + width == (tb + 1) * P:
                                ins = v.tensor_tensor(dst, src, MASKS[:, 1, MW - width:MW], ALU.add)
                            else:
                                ins = v.tensor_copy(dst, src)
                            ins.then_inc(d_free, 1)
                if k in ("hyp", "hypout"):
                    if (k, c) == ("hyp", 0):
                        dve.wait_ge(w2_in, 16 * 15)
                    for h in range(2):
                        b = bank_in()
                        v.tensor_tensor(Y2[:, 2 * h:2 * h + 2, :], bank(b).rearrange("p (b d) -> p b d", d=D),
                                        SCALE.unsqueeze(1).to_broadcast([P, 2, D]), ALU.mult).then_inc(d_free, 1)
                    dve.wait_ge(d_free, nd.k)
                    link(*[v.tensor_tensor_reduce(out=JUNK[:, i * D:(i + 1) * D], in0=Y2[:, i, :], in1=Y2[:, i, :], scale=1.0, scalar=0.0,
                                                  op0=ALU.mult, op1=ALU.add, accum_out=NW[:, 0, i:i + 1]) for i in range(BPC)])
                    rsqrt(NW[:, 1, :], NW[:, 0, :], NW[:, 2, :])
                    link(v.tensor_tensor(NW[:, 3, :], NW[:, 0, :], NW[:, 1, :], ALU.mult))
                    v.tensor_scalar(NW[:, 4, :], NW[:, 3, :], EPS, None, ALU.max).then_inc(n2_ready, 1)
                    dve.wait_ge(n2_ready, c_n2.next())
                    link(v.tensor_scalar(NW[:, 6, :], NW[:, 4, :], EPS, None, ALU.add))
                    link(v.reciprocal(NW[:, 6, :], NW[:, 6, :]))
                    dve.wait_ge(n2_tanh, c_n2.k)
                    link(v.tensor_tensor(NW[:, 6, :], NW[:, 5, :], NW[:, 6, :], ALU.mult))
                    link(v.tensor_tensor(NW[:, 7, :], NW[:, 3, :], NW[:, 6, :], ALU.mult))
                    link(v.tensor_scalar(NW[:, 7, :], NW[:, 7, :], EPS, None, ALU.max))
                    link(v.reciprocal(NW[:, 7, :], NW[:, 7, :]))
                    link(v.tensor_scalar(NW[:, 7, :], NW[:, 7, :], MAX_NORM, 1.0, ALU.mult, ALU.min))
                    link(v.tensor_tensor(NW[:, 7, :], NW[:, 7, :], NW[:, 6, :], ALU.mult))
                    done = []
                    for i in range(BPC):
                        x = X[:, BPC * c + i, :]
                        done.append(v.scalar_tensor_tensor(out=x, in0=Y2[:, i, :], scalar=NW[:, 7, i:i + 1], in1=x,
                                                           op0=ALU.mult, op1=ALU.add))
                    if k == "hypout":
                        done[-1].then_inc(x_done, 1)
                        dve.wait_ge(x_done, c + 1)
                    else:
                        link(*done)

            def attention_steps(L, steps, group, base, chain_base):
                ring, chain = Count(base), Count(chain_base)

                def clink(ins):
                    ins.then_inc(L.chain, 1)
                    dve.wait_ge(L.chain, chain.next())

                for step in steps:
                    if step[0] in ("mtr", "otr") or (step[0] == "max" and step[2] == 0):
                        n = ring.next()
                        slot = (n - 1) % L.slots * (L.w1 // CH)
                        if step[0] != "max":
                            dve.wait_ge(L.slot_ready, n)
                    if step[0] == "max" and (step[2] + 1) * CH >= L.jobs[step[1]][4]:
                        j, tb, i, s0, w, diag = L.jobs[step[1]]
                        dve.wait_ge(L.slot_ready, n)
                        src = PS[:, slot * CH:slot * CH + w]
                        dst = MP[:, i, tb // BPC, j, tb % BPC:tb % BPC + 1]
                        if L.rope:
                            if n > 1:
                                dve.wait_ge(L.slot_free, n - 1)
                            a = step[1] // HG
                            if j == 0:
                                dve.wait_ge(ar_in[a % AR_RING], 16 * ((group + step[3]) * (len(L.tiles) // AR_RING) + a // AR_RING + 1))
                            ins = v.tensor_tensor_reduce(out=JUNK[:, 0:w], in0=src, in1=AR[a % AR_RING][:, 0:w], scale=1.0,
                                                         scalar=LOWEST, op0=ALU.add, op1=ALU.max, accum_out=dst)
                        elif diag:
                            if n > 1:
                                dve.wait_ge(L.slot_free, n - 1)
                            low = 0.0 if L.zeros and tb < NB - 1 else LOWEST
                            ins = v.tensor_tensor_reduce(out=JUNK[:, 0:w], in0=src, in1=MASKS[:, 0 if L.zeros else 1, MW - w:MW],
                                                         scale=1.0, scalar=low, op0=ALU.mult if L.zeros else ALU.add, op1=ALU.max,
                                                         accum_out=dst)
                        else:
                            ins = v.reduce_max(dst, src, AX.X)
                        ins.then_inc(L.slot_free, 1)
                    if step[0] == "score" and step[1] in L.added:
                        _, u, j = step
                        e = L.exp_no[u] + j
                        dve.wait_ge(L.score_ready, group * L.n_exp + e + 1)
                        b = bank(4 + e % RING2)
                        v.tensor_tensor(b, b, ARK[L.added[u]], ALU.add).then_inc(L.rope_added, 1)
                    if step[0] == "neg":
                        c = step[1]
                        dve.wait_ge(L.slot_free, base + ring.k)
                        clink(v.reduce_max(MX[:, 0], MP[:, :, c].rearrange("p i j b -> p j b i"), AX.X))
                        clink(v.tensor_scalar(NM[:, :, 0], MX[:, 0], -1.0, None, ALU.mult))
                        clink(v.scalar_tensor_tensor(out=MX[:, 1], in0=MX[:, 0], scalar=-1.0, in1=NM[:, :, 0],
                                                     op0=ALU.mult, op1=ALU.subtract))
                        clink(v.tensor_copy(NM[:, :, 1], MX[:, 1]))
                        v.tensor_tensor(NM[:, :, 2], MX[:, 1], NM[:, :, 1], ALU.subtract).then_inc(L.neg_ready, 1)
                    if step[0] == "mtr":
                        count = (group + step[2]) * NC + step[1]
                        if count > 0:
                            dve.wait_ge(L.max_rows_in, count * ROW_DMAS)
                        rows = PARTS * HG * BPC
                        v.tensor_copy(MR[0:rows, :], bank(slot).bitcast(BF16)[0:rows, 0:P]).then_inc(L.slot_free, 1)
                    if step[0] == "save":
                        dve.wait_ge(L.pv_done, group * L.n_unit + (L.chunk_last[step[1]] + 1))
                        v.tensor_copy(OS[:], bank(7)).then_inc(L.out_saved, 1)
                    if step[0] == "otr":
                        src = bank(slot).rearrange("p (b j d) -> p b j d", b=BPC, j=HG)
                        clink(v.reciprocal(RZ[:].unsqueeze(3), src[:, :, :, DH:DH + 1]))
                        b0 = BPC * step[1]
                        f = group * HG * DH
                        dst = ON[:, b0:b0 + BPC, f:f + HG * DH].rearrange("p b (j d) -> p b j d", d=DH)
                        v.tensor_tensor(dst, src[:, :, :, 0:DH], RZ[:].unsqueeze(3).to_broadcast([P, BPC, HG, DH]), ALU.mult)\
                            .then_inc(L.slot_free, 1)

            def lambdas():
                dve.wait_ge(lam_in, 16 * 5)
                link(*[v.tensor_tensor_reduce(out=JUNK[:, i * D:(i + 1) * D], in0=LV[:, 2 * i, :], in1=LV[:, 2 * i + 1, :], scale=1.0, scalar=0.0,
                                              op0=ALU.mult, op1=ALU.add, accum_out=LAM[:, i:i + 1]) for i in range(2)])
                v.tensor_copy(LAM[:, 4:6], LAM[:, 0:2]).then_inc(lam_dots, 1)
                dve.wait_ge(lam_exp, 1)
                link(v.tensor_tensor(LAM[:, 6:7], LAM[:, 2:3], LAM[:, 3:4], ALU.subtract))
                link(v.tensor_scalar(LAM[:, 6:7], LAM[:, 6:7], LAMBDA_INIT, -DIFF_SCALE, ALU.add, ALU.mult))
                link(v.tensor_scalar(LAM[:, 7:8], SEL[:, 0:1], DIFF_SCALE, None, ALU.mult))
                v.scalar_tensor_tensor(out=QSC[:], in0=SEL[:, 1:2], scalar=LAM[:, 6:7], in1=LAM[:, 7:8], op0=ALU.mult,
                                       op1=ALU.add).then_inc(lam_done, 1)

            def attention(L):
                link(v.memset(MP[:], LOWEST))
                if L.rope:
                    dve.wait_ge(a_free, A_COUNT[L_KEY[L.name]])
                    for i in range(NC):
                        dve.wait_ge(ar_out[i], 16 * ar_place.count(i))
                attention_steps(L, L.first, 0, 0, 0)
                for g in range(NG - 1):
                    attention_steps(L, L.stage, g, g * L.r_stage + L.r_first, g * L.chain_stage + L.chain_first)
                g = NG - 1
                attention_steps(L, L.last, g, g * L.r_stage + L.r_first, g * L.chain_stage + L.chain_first)

            for kind, steps in PROGRAM:
                if steps is None:
                    if kind == "A":
                        dve.wait_ge(const_ready, N_CONST)
                        lambdas()
                    attention(att[kind])
                    continue
                for k, c, d0, a0 in steps:
                    if k == "in":
                        dve.wait_ge(x_ins[c], 16)
                    else:
                        main(k, c, d0, a0)
                    if k in HAS_NORM:
                        norm(c)
    return nc


_NAMES = {"x": "L0_attn_a_x", "L0a_q": "L0_attn_a_Wq", "L0a_k": "L0_attn_a_Wk", "L0a_v": "L0_attn_a_Wv", "L0a_o": "L0_attn_a_Wo",
          "L0b_q": "L0_attn_b_Wq", "L0b_k": "L0_attn_b_Wk", "L0b_v": "L0_attn_b_Wv", "L0b_o": "L0_attn_b_Wo",
          "gate": "L0_ffn_w_gate", "up": "L0_ffn_w_up", "down": "L0_ffn_w_down", "attn": "L1_attn_a_W_attn",
          "proj": "L1_attn_a_W_proj", "lq1": "L1_attn_a_lambda_q1", "lk1": "L1_attn_a_lambda_k1",
          "lq2": "L1_attn_a_lambda_q2", "lk2": "L1_attn_a_lambda_k2", "kv": "L1_attn_b_Wkv", "kup": "L1_attn_b_Wkup",
          "vup": "L1_attn_b_Wvup", "L1b_q": "L1_attn_b_Wq", "qr": "L1_attn_b_Wqr", "kr": "L1_attn_b_Wkr",
          "L1b_o": "L1_attn_b_Wo", "hyp_w": "L1_ffn_weight", "hyp_scale": "L1_ffn_scale"}


def _shape_constants():
    inv = (1.0 / np.power(np.float32(10000.0), np.arange(0, ROPE, 2, dtype=np.float32) / np.float32(ROPE))).astype(np.float32)
    angle = np.outer(inv, np.arange(T, dtype=np.float32)).astype(np.float32)
    cos, sin = np.cos(angle).astype(np.float32), np.sin(angle).astype(np.float32)
    first = (np.arange(P) % DH < DH // 2).astype(np.float32)
    return {"cos": np.concatenate([cos, cos]), "sin": np.concatenate([-sin, sin]), "rows": np.stack([first, 1 - first], 1)}


def kernel(**inputs):
    import concourse.bacc as bacc
    from concourse.bass_utils import run_bass_kernel_spmd

    nc = bacc.Bacc("TRN2", target_bir_lowering=False, num_devices=1)
    given = {k: np.ascontiguousarray(inputs[n]) for k, n in _NAMES.items()}
    given.update(_shape_constants())
    arrays = {f"in_{k}": np.ascontiguousarray(x) for k, x in given.items()}
    aps = {k: nc.dram_tensor(f"in_{k}", x.shape, mybir.dt.from_np(x.dtype), kind="ExternalInput").ap() for k, x in given.items()}
    out = nc.dram_tensor("out_0", (1, T, D), F32, kind="ExternalOutput").ap()
    build(nc, aps, out)
    return run_bass_kernel_spmd(nc, [arrays], core_ids=[0]).results[0]["out_0"]
```
